# Optimizing a Trainium2 kernel written in Bass

```python
import numpy as np
import jax
import jax.numpy as jnp

def _softmax(x, axis=-1):
    return jax.nn.softmax(x, axis=axis)

def _gelu(x):
    return jax.nn.gelu(x, approximate=True)

def _silu(x):
    return jax.nn.silu(x)

def _sigmoid(x):
    return jax.nn.sigmoid(x)

def _layernorm(x, axis=-1, eps=1e-05):
    m = jnp.mean(x, axis=axis, keepdims=True)
    v = jnp.var(x, axis=axis, keepdims=True)
    return (x - m) / jnp.sqrt(v + eps)

def _scatter_add(tgt, idx, src, axis=0):
    return tgt.at[idx].add(src)

def _segment_sum(src, seg, n):
    return jax.ops.segment_sum(src, seg, n)
kernel_name = 'mk_cond_resid_d4_seqx_r8_f57638'

def setup_inputs(seed: int=0):
    np.random.seed(seed)
    _w = jnp.asarray

    def _rec_inputs():
        import jax
        import jax.numpy as jnp
        _rk = jax.random.key(seed)
        x = -0.000125 + 0.9999 * jax.random.normal(jax.random.fold_in(_rk, 1), (32, 128, 128), jnp.float32)
        _lenS = 128 - jax.random.randint(jax.random.fold_in(_rk, 7), (32,), 0, max(1, 128 // 4) + 1, jnp.int32)
        _lenS2 = 128 - jax.random.randint(jax.random.fold_in(_rk, 8), (32,), 0, max(1, 128 // 4) + 1, jnp.int32)
        cond_1024 = 0.00782532 + 1.00527 * jax.random.normal(jax.random.fold_in(_rk, 11), (32, 128), jnp.float32)
        fside_Bx1x1024x16_0 = 0.00222621 + 0.99962 * jax.random.normal(jax.random.fold_in(_rk, 12), (32, 1, 128, 16), jnp.float32)
        return (x, cond_1024, fside_Bx1x1024x16_0)
    x, cond_1024, fside_Bx1x1024x16_0 = _rec_inputs()

    def _L0_cond_setup():
        import jax, jax.numpy as jnp
        import numpy as np
        key = jax.random.key(seed)
        k1, k2, k3 = jax.random.split(key, 3)
        B, R, C = (8, 512, 128)
        input_dim = 128
        weight_params = jax.random.normal(k1, (B, R, C), dtype=jnp.float32)
        logits = jax.random.normal(k2, (B, input_dim), dtype=jnp.float32)
        score_w = jax.random.normal(k3, (input_dim, 1), dtype=jnp.float32) * (1.0 / np.sqrt(input_dim))
        score_b = jnp.zeros((1,), dtype=jnp.float32)
        return {'weight_params': weight_params, 'logits': logits, 'score_w': score_w, 'score_b': score_b}
    _L0_cond_all = _L0_cond_setup()
    _L0_cond_in = {k: v for k, v in _L0_cond_all.items() if k in ('score_w', 'score_b')}
    del _L0_cond_all

    def _L1_cond_setup():
        import jax, jax.numpy as jnp
        import numpy as np
        B, F_, IN, OUT, R = (32, 64, 128, 128, 16)
        key = jax.random.key(seed)
        ks = jax.random.split(key, 6)
        x = jax.random.normal(ks[0], (B, F_, IN), dtype=jnp.float32)
        u = jax.random.normal(ks[1], (B, 1, OUT, R), dtype=jnp.float32)
        v = jax.random.normal(ks[2], (B, 1, IN, R), dtype=jnp.float32)
        b = jax.random.normal(ks[3], (B, 1, OUT), dtype=jnp.float32)
        lim = 1.0 / np.sqrt(IN)
        W = jax.random.uniform(ks[4], (OUT, IN), minval=-lim, maxval=lim, dtype=jnp.float32)
        fc_bias = jax.random.uniform(ks[5], (OUT,), minval=-lim, maxval=lim, dtype=jnp.float32)
        return {'x': x, 'u': u, 'v': v, 'b': b, 'W': W, 'fc_bias': fc_bias}
    _L1_cond_all = _L1_cond_setup()
    _L1_cond_in = {k: v for k, v in _L1_cond_all.items() if k in ('W', 'fc_bias')}
    del _L1_cond_all

    def _L2_cond_setup():
        import math
        import jax, jax.numpy as jnp
        import numpy as np
        EPS = 1e-07
        MAX_TANH_ARG = 1.0 - 1e-05

        def _norm(x):
            return jnp.sqrt(jnp.sum(x * x, axis=-1, keepdims=True)).clip(EPS)

        def logmap0(x):
            n = _norm(x)
            return jnp.arctanh(jnp.clip(n, EPS, MAX_TANH_ARG)) * x / n

        def expmap0(v):
            n = _norm(v)
            return jnp.tanh(n) * v / n

        def mobius_add(x, y):
            x2 = jnp.sum(x * x, -1, keepdims=True)
            y2 = jnp.sum(y * y, -1, keepdims=True)
            xy = jnp.sum(x * y, -1, keepdims=True)
            num = (1 + 2 * xy + y2) * x + (1 - x2) * y
            den = (1 + 2 * xy + x2 * y2).clip(EPS)
            return num / den

        def plin(x, w, b):
            return expmap0(logmap0(x) @ w + b)

        def layer_norm(x, eps=1e-06):
            m = x.mean(-1, keepdims=True)
            v = ((x - m) ** 2).mean(-1, keepdims=True)
            return (x - m) / jnp.sqrt(v + eps)

        def _beta(a, b):
            return math.exp(math.lgamma(a) + math.lgamma(b) - math.lgamma(a + b))
        D, H, FF = (128, 16, 512)
        HD = D // H
        BETA_N = _beta(D / 2, 0.5)
        BETA_H = _beta(HD / 2, 0.5)

        def _to_heads(p):
            B, S, _ = p.shape
            t = logmap0(p).reshape(B, S, H, HD) * (BETA_H / BETA_N)
            return expmap0(jnp.transpose(t, (0, 2, 1, 3)))

        def _from_heads(ph):
            B, _, S, _ = ph.shape
            t = logmap0(ph) * (BETA_N / BETA_H)
            t = jnp.transpose(t, (0, 2, 1, 3)).reshape(B, S, D)
            return expmap0(t)
        key = jax.random.key(seed)
        ks = jax.random.split(key, 20)
        B, S = (4, 128)
        x = expmap0(0.02 * jax.random.normal(ks[0], (B, S, D), jnp.float32))
        t_emb = jax.random.normal(ks[1], (B, 1, D), jnp.float32)
        g = lambda k, sh: 0.02 * jax.random.normal(k, sh, jnp.float32)
        return {'x': x, 't_emb': t_emb, 'w_q': g(ks[2], (D, D)), 'b_q': jnp.zeros((D,), jnp.float32), 'w_k': g(ks[3], (D, D)), 'b_k': jnp.zeros((D,), jnp.float32), 'w_v': g(ks[4], (D, D)), 'b_v': jnp.zeros((D,), jnp.float32), 'w_o': g(ks[5], (D, D)), 'b_o': jnp.zeros((D,), jnp.float32), 'w_f1': g(ks[6], (D, FF)), 'b_f1': jnp.zeros((FF,), jnp.float32), 'w_f2': g(ks[7], (FF, D)), 'b_f2': jnp.zeros((D,), jnp.float32), 'w_ada': g(ks[8], (D, 6 * D)), 'b_ada': jnp.zeros((6 * D,), jnp.float32)}
    _L2_cond_all = _L2_cond_setup()
    _L2_cond_in = {k: v for k, v in _L2_cond_all.items() if k in ('w_q', 'b_q', 'w_k', 'b_k', 'w_v', 'b_v', 'w_o', 'b_o', 'w_f1', 'b_f1', 'w_f2', 'b_f2', 'w_ada', 'b_ada')}
    del _L2_cond_all

    def _L3_cond_setup():
        import jax, jax.numpy as jnp
        import numpy as np
        D_MODEL = 128
        D_FF = 512
        N_EXPERTS = 8
        TOP_K = 2
        N_SHARED = 2
        B, T = (4, 256)
        key = jax.random.key(seed)
        ks = jax.random.split(key, 9)
        Hs = D_FF // 2
        Hr = D_FF // 4
        inp = {'x': jax.random.normal(ks[0], (B, T, D_MODEL), dtype=jnp.float32), 't_emb': jax.random.normal(ks[1], (B, D_MODEL), dtype=jnp.float32), 'W_router': 0.01 * jax.random.normal(ks[2], (N_EXPERTS, 2 * D_MODEL), dtype=jnp.float32), 'router_bias': jnp.zeros((N_EXPERTS,), dtype=jnp.float32), 's_w1': 0.02 * jax.random.normal(ks[3], (N_SHARED, Hs, D_MODEL), dtype=jnp.float32), 's_w3': 0.02 * jax.random.normal(ks[4], (N_SHARED, Hs, D_MODEL), dtype=jnp.float32), 's_w2': 0.02 * jax.random.normal(ks[5], (N_SHARED, D_MODEL, Hs), dtype=jnp.float32), 'r_w1': 0.02 * jax.random.normal(ks[6], (N_EXPERTS, Hr, D_MODEL), dtype=jnp.float32), 'r_w2': 0.02 * jax.random.normal(ks[7], (N_EXPERTS, D_MODEL, Hr), dtype=jnp.float32)}
        return inp
    _L3_cond_all = _L3_cond_setup()
    _L3_cond_in = {k: v for k, v in _L3_cond_all.items() if k in ('W_router', 'router_bias', 's_w1', 's_w3', 's_w2', 'r_w1', 'r_w2')}
    del _L3_cond_all
    return {'x': x, 'cond_1024': cond_1024, 'fside_Bx1x1024x16_0': fside_Bx1x1024x16_0, 'L0_cond_score_w': _L0_cond_in['score_w'], 'L0_cond_score_b': _L0_cond_in['score_b'], 'L1_cond_W': _L1_cond_in['W'], 'L1_cond_fc_bias': _L1_cond_in['fc_bias'], 'L2_cond_w_q': _L2_cond_in['w_q'], 'L2_cond_b_q': _L2_cond_in['b_q'], 'L2_cond_w_k': _L2_cond_in['w_k'], 'L2_cond_b_k': _L2_cond_in['b_k'], 'L2_cond_w_v': _L2_cond_in['w_v'], 'L2_cond_b_v': _L2_cond_in['b_v'], 'L2_cond_w_o': _L2_cond_in['w_o'], 'L2_cond_b_o': _L2_cond_in['b_o'], 'L2_cond_w_f1': _L2_cond_in['w_f1'], 'L2_cond_b_f1': _L2_cond_in['b_f1'], 'L2_cond_w_f2': _L2_cond_in['w_f2'], 'L2_cond_b_f2': _L2_cond_in['b_f2'], 'L2_cond_w_ada': _L2_cond_in['w_ada'], 'L2_cond_b_ada': _L2_cond_in['b_ada'], 'L3_cond_W_router': _L3_cond_in['W_router'], 'L3_cond_router_bias': _L3_cond_in['router_bias'], 'L3_cond_s_w1': _L3_cond_in['s_w1'], 'L3_cond_s_w3': _L3_cond_in['s_w3'], 'L3_cond_s_w2': _L3_cond_in['s_w2'], 'L3_cond_r_w1': _L3_cond_in['r_w1'], 'L3_cond_r_w2': _L3_cond_in['r_w2']}

def reference(x, cond_1024, fside_Bx1x1024x16_0, L0_cond_score_w, L0_cond_score_b, L1_cond_W, L1_cond_fc_bias, L2_cond_w_q, L2_cond_b_q, L2_cond_w_k, L2_cond_b_k, L2_cond_w_v, L2_cond_b_v, L2_cond_w_o, L2_cond_b_o, L2_cond_w_f1, L2_cond_b_f1, L2_cond_w_f2, L2_cond_b_f2, L2_cond_w_ada, L2_cond_b_ada, L3_cond_W_router, L3_cond_router_bias, L3_cond_s_w1, L3_cond_s_w3, L3_cond_s_w2, L3_cond_r_w1, L3_cond_r_w2):
    import jax
    import jax.numpy as jnp

    def _L0_cond_ref(weight_params, logits, score_w, score_b):
        import jax, jax.numpy as jnp
        import numpy as np
        keep_fraction = jax.nn.sigmoid(logits @ score_w + score_b)
        total_row_count = weight_params.shape[-2]
        rows_to_keep = jnp.clip((keep_fraction * total_row_count).astype(jnp.int32), 1, None).squeeze(-1)
        row_magnitudes = jnp.linalg.norm(weight_params, axis=-1)
        sorted_magnitudes = jnp.sort(row_magnitudes, axis=-1)[..., ::-1]
        thresholds = jnp.take_along_axis(sorted_magnitudes, (rows_to_keep - 1)[:, None], axis=-1)
        top_k_row_mask = (row_magnitudes >= thresholds).astype(weight_params.dtype)
        return weight_params * top_k_row_mask[..., None]

    def _L1_cond_ref(x, u, v, b, W, fc_bias):
        import jax, jax.numpy as jnp
        import numpy as np
        B, F_, IN, OUT, R = (32, 64, 128, 128, 16)
        inch = x.shape[-1]
        r = v.shape[-1]
        z1 = jnp.einsum('bfi,bir->bfr', x, v[:, 0]) / inch
        z = jnp.einsum('bfr,bor->bfo', z1, u[:, 0]) / r
        y = jnp.einsum('bfi,oi->bfo', x, W) + fc_bias + z + b
        return jax.nn.gelu(y, approximate=False)

    def _L2_cond_ref(x, t_emb, w_q, b_q, w_k, b_k, w_v, b_v, w_o, b_o, w_f1, b_f1, w_f2, b_f2, w_ada, b_ada):
        import math
        import jax, jax.numpy as jnp
        import numpy as np
        EPS = 1e-07
        MAX_TANH_ARG = 1.0 - 1e-05

        def _norm(x):
            return jnp.sqrt(jnp.sum(x * x, axis=-1, keepdims=True)).clip(EPS)

        def logmap0(x):
            n = _norm(x)
            return jnp.arctanh(jnp.clip(n, EPS, MAX_TANH_ARG)) * x / n

        def expmap0(v):
            n = _norm(v)
            return jnp.tanh(n) * v / n

        def mobius_add(x, y):
            x2 = jnp.sum(x * x, -1, keepdims=True)
            y2 = jnp.sum(y * y, -1, keepdims=True)
            xy = jnp.sum(x * y, -1, keepdims=True)
            num = (1 + 2 * xy + y2) * x + (1 - x2) * y
            den = (1 + 2 * xy + x2 * y2).clip(EPS)
            return num / den

        def plin(x, w, b):
            return expmap0(logmap0(x) @ w + b)

        def layer_norm(x, eps=1e-06):
            m = x.mean(-1, keepdims=True)
            v = ((x - m) ** 2).mean(-1, keepdims=True)
            return (x - m) / jnp.sqrt(v + eps)

        def _beta(a, b):
            return math.exp(math.lgamma(a) + math.lgamma(b) - math.lgamma(a + b))
        D, H, FF = (128, 16, 512)
        HD = D // H
        BETA_N = _beta(D / 2, 0.5)
        BETA_H = _beta(HD / 2, 0.5)

        def _to_heads(p):
            B, S, _ = p.shape
            t = logmap0(p).reshape(B, S, H, HD) * (BETA_H / BETA_N)
            return expmap0(jnp.transpose(t, (0, 2, 1, 3)))

        def _from_heads(ph):
            B, _, S, _ = ph.shape
            t = logmap0(ph) * (BETA_N / BETA_H)
            t = jnp.transpose(t, (0, 2, 1, 3)).reshape(B, S, D)
            return expmap0(t)
        ada = t_emb @ w_ada + b_ada
        sh_msa, sc_msa, g_msa, sh_mlp, sc_mlp, g_mlp = jnp.split(ada, 6, axis=-1)
        residual = x
        xn = layer_norm(logmap0(x))
        xm = expmap0(xn * (1 + sc_msa) + sh_msa)
        q = _to_heads(plin(xm, w_q, b_q))
        k = _to_heads(plin(xm, w_k, b_k))
        v = _to_heads(plin(xm, w_v, b_v))
        qt, kt, vt = (logmap0(q), logmap0(k), logmap0(v))
        scores = jnp.einsum('bhqd,bhkd->bhqk', qt, kt) / math.sqrt(HD)
        attn = jax.nn.softmax(scores, axis=-1)
        out_h = expmap0(jnp.einsum('bhqk,bhkd->bhqd', attn, vt))
        attn_out = plin(_from_heads(out_h), w_o, b_o)
        attn_t = g_msa * logmap0(attn_out)
        x = mobius_add(residual, expmap0(attn_t))
        residual = x
        xn = layer_norm(logmap0(x))
        xm = expmap0(xn * (1 + sc_mlp) + sh_mlp)
        ff = plin(plin(xm, w_f1, b_f1), w_f2, b_f2)
        ff_t = g_mlp * logmap0(ff)
        return mobius_add(residual, expmap0(ff_t))

    def _L3_cond_ref(x, t_emb, W_router, router_bias, s_w1, s_w3, s_w2, r_w1, r_w2):
        import jax, jax.numpy as jnp
        import numpy as np
        D_MODEL = 128
        D_FF = 512
        N_EXPERTS = 8
        TOP_K = 2
        N_SHARED = 2
        B, T = (4, 256)
        Bn, Tn, C = x.shape
        N = Bn * Tn
        x_flat = x.reshape(N, C)
        t_flat = jnp.broadcast_to(t_emb[:, None, :], (Bn, Tn, C)).reshape(N, C)
        shared_out = jnp.zeros_like(x_flat)
        for e in range(N_SHARED):
            h = jax.nn.silu(x_flat @ s_w1[e].T) * (x_flat @ s_w3[e].T)
            shared_out = shared_out + h @ s_w2[e].T
        shared_out = shared_out / N_SHARED
        router_in = jnp.concatenate([x_flat, t_flat], axis=-1)
        s = jax.nn.sigmoid((router_in @ W_router.T).astype(jnp.float32))
        sel_scores = s + router_bias
        _, topk_idx = jax.lax.top_k(sel_scores, TOP_K)
        s_sel = jnp.take_along_axis(s, topk_idx, axis=1)
        denom = jnp.sum(s_sel, axis=1, keepdims=True)
        gates = jnp.where(denom > 1e-09, s_sel / (denom + 1e-09), 1.0 / TOP_K).astype(x.dtype)
        gates_full = jnp.sum(jax.nn.one_hot(topk_idx, N_EXPERTS, dtype=x.dtype) * gates[..., None], axis=1)
        routed_out = jnp.zeros_like(x_flat)
        for e in range(N_EXPERTS):
            h = jax.nn.gelu(x_flat @ r_w1[e].T, approximate=False)
            routed_out = routed_out + h @ r_w2[e].T * gates_full[:, e:e + 1]
        out = (shared_out + routed_out) / (N_SHARED + TOP_K)
        return out.reshape(Bn, Tn, C)
    x = x + _L0_cond_ref(x, cond_1024, L0_cond_score_w, L0_cond_score_b)
    x = x + _L1_cond_ref(x, fside_Bx1x1024x16_0, fside_Bx1x1024x16_0, cond_1024[:, None, :], L1_cond_W, L1_cond_fc_bias)
    x = x + _L2_cond_ref(x, cond_1024[:, None, :], L2_cond_w_q, L2_cond_b_q, L2_cond_w_k, L2_cond_b_k, L2_cond_w_v, L2_cond_b_v, L2_cond_w_o, L2_cond_b_o, L2_cond_w_f1, L2_cond_b_f1, L2_cond_w_f2, L2_cond_b_f2, L2_cond_w_ada, L2_cond_b_ada)
    x = x + _L3_cond_ref(x, cond_1024, L3_cond_W_router, L3_cond_router_bias, L3_cond_s_w1, L3_cond_s_w3, L3_cond_s_w2, L3_cond_r_w1, L3_cond_r_w2)
    return x

_drawn_inputs = setup_inputs


def setup_inputs(seed=0):
    import zlib

    import numpy as np

    out = dict(_drawn_inputs(seed))
    spreads = {'L2_cond_b_q': (0.0, 0.8),
     'L2_cond_b_k': (0.0, 0.8),
     'L2_cond_b_v': (0.0, 0.375),
     'L2_cond_b_o': (0.0, 0.1),
     'L2_cond_b_f1': (0.0, 0.289),
     'L2_cond_b_f2': (0.0, 0.1),
     'L2_cond_b_ada': (0.0, 0.1),
     'L3_cond_router_bias': (0.0, 0.8)}
    factors = {'fside_Bx1x1024x16_0': 4.211,
     'L1_cond_fc_bias': 2.714,
     'L2_cond_w_q': 8.0,
     'L2_cond_w_k': 8.0,
     'L2_cond_w_v': 5.626,
     'L3_cond_W_router': 8.0,
     'L3_cond_s_w1': 8.0,
     'L3_cond_s_w3': 8.0,
     'L3_cond_s_w2': 8.0,
     'L3_cond_r_w1': 8.0,
     'L3_cond_r_w2': 8.0}
    for name, (base, spread) in spreads.items():
        noise = np.random.default_rng([zlib.crc32(name.encode()), seed]).standard_normal(out[name].shape)
        drawn = base * np.exp(spread * noise) if base else spread * noise
        out[name] = jnp.asarray(drawn.astype(out[name].dtype))
    for name, factor in factors.items():
        out[name] = (out[name] * factor).astype(out[name].dtype)
    return out
```

```python
import math
from contextlib import ExitStack

import concourse.bass as bass
from concourse import mybir

FP32 = mybir.dt.float32
FP16 = mybir.dt.float16
ALU = mybir.AluOpType
ACT = mybir.ActivationFunctionType
AX = mybir.AxisListType

BATCH = 32
TOK = 128
D = 128
RANK = 16
HEADS, HD = 16, 8
FF = 512
EXPERTS, TOP_K = 8, 2
SHARED_CHUNKS = 4
G = 4
GROUPS = BATCH // G
PAIRS = GROUPS // 2
NG = G * TOK
ADA = 6 * D + EXPERTS

MAX_NORM = 0.9999899864196777
CAP = math.atanh(MAX_NORM)
_beta = lambda a, b: math.exp(math.lgamma(a) + math.lgamma(b) - math.lgamma(a + b))
HEAD_SCALE = _beta(HD / 2, 0.5) / _beta(D / 2, 0.5)
ROW_OPS = 26
ROUTE_OPS = 16
MOB_OPS = 22
TINY = 1e-18


def build(nc, ins, out):
    ctx = ExitStack()
    with ctx:
        def sb(name, shape, dt=FP32):
            return ctx.enter_context(nc.sbuf_tensor(name + "_sb", shape, dt))

        def sem(name):
            return ctx.enter_context(nc.semaphore(name))

        X = sb("X", [TOK, BATCH, D])
        X3 = sb("X3", [TOK, BATCH, D])
        BR = sb("BR", [TOK, BATCH, D])
        ident = sb("ident", [128, 128])
        ident16 = sb("ident16", [128, 128], FP16)
        zero = sb("zero", [128, 1])
        tiny = sb("tiny", [128, 1])

        bank = [ctx.enter_context(nc.psum_tensor(f"bank{k}", [128, 512], FP32)) for k in range(4)]
        wide = ctx.enter_context(nc.psum_tensor("wide", [128, 2048], FP32))
        bank += [wide[:, 512 * k:512 * (k + 1)] for k in range(4)]

        dram_ada = nc.dram_tensor("ada_rows", (BATCH, ADA), FP32, kind="Internal").ap()

        condT = sb("condT", [D, BATCH])
        score_w = sb("score_w", [D, 1])
        score_b = sb("score_b", [128, 1])
        w1T = sb("w1T", [D, D])
        fc_bias = sb("fc_bias", [D, 1])
        w_ada = sb("w_ada", [D, 6 * D])
        b_ada = sb("b_ada", [BATCH, 6 * D])
        w_router = sb("w_router", [D, 2, EXPERTS])
        ada_sb = sb("ada_sb", [BATCH, ADA])
        bias1 = sb("bias1", [D, BATCH])
        keep = sb("keep", [TOK, BATCH])
        mv = sb("mv", [TOK, BATCH, 2])

        nsq = [sb(f"nsq{q}", [TOK, G]) for q in range(2)]
        above = [sb(f"above{q}", [TOK, G]) for q in range(2)]
        factor = [sb(f"factor{q}", [TOK, G]) for q in range(2)]
        junkA = [sb(f"junkA{q}", [TOK, G, D]) for q in range(2)]
        junkV = [sb(f"junkV{q}", [TOK, G, D]) for q in range(2)]
        early = sb("early", [128, 8 * NG])
        X1, X1T, MB, YT = [[early[:, (2 * k + q) * NG:(2 * k + q + 1) * NG].rearrange("p (g n) -> p g n", g=G) for q in range(2)] for k in range(4)]
        fT = [sb(f"fT{q}", [RANK, G, D]) for q in range(2)]
        st6 = [sb(f"st6{q}", [TOK, G, 6]) for q in range(2)]

        w_qkv = sb("w_qkv", [D, 3 * D])
        wqkv_hl = [sb(f"wqkv_{n}", [D, 3 * D], FP16) for n in ("hi", "lo")]
        w_o = sb("w_o", [D, D])
        b_qkv = sb("b_qkv", [128, 3 * D])
        b_o = sb("b_o", [128, D])
        row_r = sb("row_r", [TOK, BATCH])
        row_n2 = sb("row_n2", [TOK, BATCH])
        sm = [sb(f"sm{k}", [TOK, BATCH]) for k in range(10)]
        ADR = [sb(f"ADR{q}", [128, G, 2 * D]) for q in range(2)]
        ADG = [sb(f"ADG{q}", [128, G, D]) for q in range(2)]
        U = [sb(f"U{q}", [TOK, G, D]) for q in range(2)]
        junkU = w_ada[:, 0:NG].rearrange("p (g n) -> p g n", g=G)
        n2u = [sb(f"n2u{q}", [TOK, G]) for q in range(2)]
        su = [sb(f"su{q}", [TOK, G]) for q in range(2)]
        UHL = [[sb(f"UT{n}{q}", [D, NG], FP16) for n in ("hi", "lo")] for q in range(2)]
        big = sb("big", [128, 16 * NG])
        P = [big[:, q * 4 * NG:(q + 1) * 4 * NG].rearrange("p (i c n) -> p i c n", i=4, c=4) for q in range(2)]
        QKV = [big[:, (8 + 3 * q) * NG:(11 + 3 * q) * NG].rearrange("p (g n) -> p g n", g=G) for q in range(2)]
        OS = [big[:, (14 + q) * NG:(15 + q) * NG].rearrange("p (c n) -> p c n", c=4) for q in range(2)]
        SQ = [sb(f"SQ{q}", [TOK, 3 * D]) for q in range(2)]
        ST = [sb(f"ST{q}", [TOK, G * 51]) for q in range(2)]
        FC = [sb(f"FC{q}", [TOK, G, 48]) for q in range(2)]
        FP = [sb(f"FP{q}", [TOK, G * 3]) for q in range(2)]
        SC = [sb(f"SC{q}", [TOK, 2 * D]) for q in range(2)]
        QS = [sb(f"QS{q}", [TOK, HEADS, 4, HD], FP16) for q in range(2)]
        KS = [sb(f"KS{q}", [TOK, HEADS, 4, HD], FP16) for q in range(2)]
        V = [sb(f"V{q}", [TOK, G, HEADS, HD + 1]) for q in range(2)]
        QKT = [sb(f"QKT{q}", [128, 2, 4, TOK], FP16) for q in range(2)]
        RD = [sb(f"RD{q}", [TOK, HEADS]) for q in range(2)]
        ON = [sb(f"ON{q}", [TOK, D]) for q in range(2)]
        OT = [sb(f"OT{q}", [D, TOK]) for q in range(2)]
        AO = [sb(f"AO{q}", [TOK, D]) for q in range(2)]
        junkD = [junkV[q][:, 0, :] for q in range(2)]
        junkS = [sb(f"junkS{q}", [TOK, 2, D]) for q in range(2)]
        n2a, n2g, dxg = sb("n2a", [TOK, BATCH]), sb("n2g", [TOK, BATCH]), sb("dxg", [TOK, BATCH])
        al, be = sb("al", [TOK, BATCH]), sb("be", [TOK, BATCH])
        w_f1 = sb("w_f1", [D, FF])
        wf1_hl = [sb(f"wf1_{n}", [D, FF], FP16) for n in ("hi", "lo")]
        w_f1Tb = sb("w_f1Tb", [128, 4, D + 1])
        gram_hl = [sb(f"gram_{n}", [D, D + 1], FP16) for n in ("hi", "lo")]
        bb_f1 = sb("bb_f1", [128, 1])
        w_f2 = sb("w_f2", [128, 4, D])
        b_f2 = sb("b_f2", [128, D])
        C = [sb(f"C{q}", [TOK, G, D]) for q in range(2)]
        HT = [early[:, q * 4 * NG:(q + 1) * 4 * NG].rearrange("p (k n) -> p k n", k=4) for q in range(2)]
        hq = [sb(f"hq{q}", [TOK, G]) for q in range(2)]
        sh = [sb(f"sh{q}", [TOK, G]) for q in range(2)]
        FO = [sb(f"FO{q}", [TOK, G, D]) for q in range(2)]
        UP = 4 * FF
        w_up = big[:, 0:UP]
        wup_hl = [sb(f"wup_{n}", [D, UP], FP16) for n in ("hi", "lo")]
        wr_hl = [sb(f"wr_{n}", [D, EXPERTS], FP16) for n in ("hi", "lo")]
        w_sd = sb("w_sd", [128, SHARED_CHUNKS, D])
        w_rd = sb("w_rd", [128, EXPERTS, D])
        b_router = sb("b_router", [128, EXPERTS])
        ADT = [sb(f"ADT{q}", [128, G, EXPERTS]) for q in range(2)]
        before = sb("before", [128, EXPERTS, EXPERTS])
        S1 = [junkA[q][:, :, :].rearrange("p g n -> p (g n)") for q in range(2)]
        HS = HT
        HR = [big[:, q * 8 * NG:(q + 1) * 8 * NG].rearrange("p (e n) -> p e n", e=EXPERTS) for q in range(2)]
        sg = [sb(f"sg{q}", [TOK, G, EXPERTS]) for q in range(2)]
        gates = [sb(f"gates{q}", [TOK, G, EXPERTS]) for q in range(2)]
        cmpb = [junkS[k][:, :, :].rearrange("p a (g x y) -> p (a g) x y", x=EXPERTS, y=EXPERTS) for k in range(2)]
        rt = [sb(f"rt{k}", [TOK, G, EXPERTS]) for k in range(3)]
        rs = [sb(f"rs{k}", [TOK, G]) for k in range(3)]
        OUT = FO
        X4 = C

        mvq = [sb(f"mvq{q}", [TOK, G, 2]) for q in range(2)]
        held_pool = sb("held_pool", [128, 1])
        held = sb("held", [128, 64])

        aggrA, mvA = sem("aggrA"), sem("mvA")
        wB_in, wB_split = sem("wB_in"), sem("wB_split")
        chain, chain_act = sem("chain"), sem("chain_act")
        rows_ready, bank3_clear = sem("rows_ready"), sem("bank3_clear")
        adr_in, adg_in = sem("adr_in"), sem("adg_in")
        (u_half, u_done, n2u_done, su_ln, su_rs, su_done, uT_mm, uT_hi, uT_lo, qkv_mm, qkv_done, sq_done, hsum_done, psum_done,
         st_ln, st_rs, fp_a, fac_b, scaled, v_done, hi_done, lo_done, t16_mm, t16_out, score_a, score_b2, exp_a, exp_b, av_mm, os_done,
         ot_mm, rd_done, on_done, onT_mm, onT_out, wo_mm, ao_done, ga_done, n2a_done, n2g_done, dx_done, br_done) = [sem(n) for n in (
             "u_half u_done n2u_done su_ln su_rs su_done uT_mm uT_hi uT_lo qkv_mm qkv_done sq_done hsum_done psum_done "
             "st_ln st_rs fp_a fac_b scaled v_done hi_done lo_done t16_mm t16_out score_a score_b2 exp_a exp_b av_mm os_done "
             "ot_mm rd_done on_done onT_mm onT_out wo_mm ao_done ga_done n2a_done n2g_done dx_done br_done").split()]

        wC_in, wD_in, wC_split, wD_split, gram2_mm, gram2_done = [sem(n) for n in "wC_in wD_in wC_split wD_split gram2_mm gram2_done".split()]
        coef_ready = sem("coef_ready")
        wup_in = sem("wup_in")
        xa_done, x3_done, stC, agC, mvC = [sem(n) for n in "xa_done x3_done stC agC mvC".split()]
        (cdr_in, cdg_in, cu_half, cu_done, cn2u, csu_ln, csu_rs, csu, c_done, cT_mm, cT_hi, cT_lo, f1_mm, h_out, g_mm, hdot, hq2, hq3, hln, hrs, hs_done,
         f2_mm, ff_done, cga, cn2a, cn2g, cdx) = [sem("c_" + n) for n in (
             "cdr_in cdg_in cu_half cu_done cn2u csu_ln csu_rs csu c_done cT_mm cT_hi cT_lo f1_mm h_out g_mm hdot hq2 hq3 hln hrs hs_done "
             "f2_mm ff_done cga cn2a cn2g cdx").split()]
        (dt_in, x4a, x4_done, x4_copy, x4T_mm, x4_hi, x4_lo, rl_mm, rl_done, sig_done, rchain, gates_done, up_mm, silu_done, hs_mul, gelu_done,
         sd_mm, rd_a, rd_b, acc_done, out_done, acc_shared, acc_half) = [sem("d_" + n) for n in (
             "dt_in x4a x4_done x4_copy x4T_mm x4_hi x4_lo rl_mm rl_done sig_done rchain gates_done up_mm silu_done hs_mul gelu_done "
             "sd_mm rd_a rd_b acc_done out_done acc_shared acc_half").split()]
        out_stored = [sem(f"out_stored{q}") for q in range(2)]

        def need(eng, semaphore, value):
            if not (isinstance(value, int) and value <= 0):
                eng.wait_ge(semaphore, value)

        pair = [0]

        def run_steps(eng, step):
            pair[0] = 0
            step(0, 0)
            with eng.Fori(0, PAIRS - 1) as i:
                pair[0] = i
                step(2 * i + 1, 1)
                step(2 * i + 2, 0)
            pair[0] = PAIRS - 1
            step(GROUPS - 1, 1)
        consts = sem("consts")
        x_first, x_rest = sem("x_first"), sem("x_rest")
        wA_in = sem("wA_in")
        f_in = [sem(f"f_in{q}") for q in range(2)]
        ada_mm, ada_done, ada_stored = sem("ada_mm"), sem("ada_done"), sem("ada_stored")
        keep_mm, keep_lin, keep_sig, keep_done = sem("keep_mm"), sem("keep_lin"), sem("keep_sig"), sem("keep_done")
        norm_done, norm_bc, rank_done, fac_done, x1_done = sem("norm_done"), sem("norm_bc"), sem("rank_done"), sem("fac_done"), sem("x1_done")
        x1T_mm, x1T_done, gram_mm, mb_done, y_mm, yT_done, yT_mm, x2_done, statA = (
            sem("x1T_mm"), sem("x1T_done"), sem("gram_mm"), sem("mb_done"), sem("y_mm"), sem("yT_done"), sem("yT_mm"), sem("x2_done"), sem("statA"))
        stored = sem("stored")
        block = ctx.enter_context(nc.Block())

        x_v = ins["x"].rearrange("b t d -> t b d")
        out_v = out.rearrange("b t d -> t b d")
        f_v = ins["fT"]

        def row(name, parts):
            return ins[name].rearrange("(a n) -> a n", a=1).broadcast_to([parts, ins[name].shape[0]])

        WA = 10
        mob_at = [ROW_OPS - 1, 2 * (ROW_OPS - 1) + MOB_OPS]
        NORM2_AT = ROW_OPS - 1 + MOB_OPS

        @block.sync
        def _(sp):
            sp.dma_start(X[:, 0:2 * G, :], x_v[:, 0:2 * G, :]).then_inc(x_first, 16)
            sp.dma_start(condT[:, :], ins["condT"]).then_inc(wA_in, 16)
            sp.dma_start(score_w[:, :], ins["score_w"]).then_inc(wA_in, 16)
            sp.dma_start(score_b[:, :], row("score_b", 128)).then_inc(wA_in, 16)
            sp.dma_start(w1T[:, :], ins["w1T"]).then_inc(wA_in, 16)
            sp.dma_start(fc_bias[:, :], ins["fc_bias"].rearrange("(p a) -> p a", a=1)).then_inc(wA_in, 16)
            for q in range(2):
                sp.dma_start(fT[q][:, :, :], f_v[:, q * G:(q + 1) * G, :]).then_inc(f_in[q], 16)
            sp.dma_start(w_ada[:, :], ins["w_ada"]).then_inc(wA_in, 16)
            sp.dma_start(b_ada[:, :], row("b_ada", BATCH)).then_inc(wA_in, 16)
            sp.dma_start(w_router[:, 0, :], ins["w_routerT"][0:D, :]).then_inc(wA_in, 16)
            sp.dma_start(w_router[:, 1, :], ins["w_routerT"][D:2 * D, :]).then_inc(wA_in, 16)
            for c in range(1, PAIRS):
                sp.dma_start(X[:, 2 * G * c:2 * G * (c + 1), :], x_v[:, 2 * G * c:2 * G * (c + 1), :]).then_inc(x_rest, 16)
            sp.wait_ge(ada_done, 3)
            sp.dma_start(dram_ada, ada_sb[:, :]).then_inc(ada_stored, 16)
            with sp.Fori(0, PAIRS - 1) as i:
                for q in range(2):
                    sp.wait_ge(gram_mm, 2 * i + q + 1)
                    sp.dma_start(fT[q][:, :, :], f_v[:, bass.ds(2 * G * i + (2 + q) * G, G), :]).then_inc(f_in[q], 16)
            sp.dma_start(w_qkv[:, :], ins["w_qkv"]).then_inc(wB_in, 16)
            sp.dma_start(w_o[:, :], ins["w_o"]).then_inc(wB_in, 16)
            sp.dma_start(b_qkv[:, :], row("b_qkv", 128)).then_inc(wB_in, 16)
            sp.dma_start(b_o[:, :], row("b_o", 128)).then_inc(wB_in, 16)
            sp.dma_start(w_f1[:, :], ins["w_f1"]).then_inc(wC_in, 16)
            sp.dma_start(w_f1Tb[:, :, :], ins["w_f1Tb"]).then_inc(wC_in, 16)
            sp.dma_start(w_f2[:, :, :], ins["w_f2"].rearrange("(k p) n -> p k n", p=128)).then_inc(wC_in, 16)
            sp.dma_start(b_f2[:, :], row("b_f2", 128)).then_inc(wC_in, 16)
            sp.dma_start(w_sd[:, :, :], ins["w_sd"].rearrange("(k p) n -> p k n", p=128)).then_inc(wD_in, 16)
            sp.dma_start(w_rd[:, :, :], ins["w_rd"].rearrange("(k p) n -> p k n", p=128)).then_inc(wD_in, 16)
            sp.dma_start(b_router[:, :], row("b_router", 128)).then_inc(wD_in, 16)
            sp.wait_ge(ada_stored, 16)
            ada_v = dram_ada.rearrange("b n -> () b n")

            def load_rows(s, q):
                sp.dma_start(ADR[q][:, :, :], ada_v[:, bass.ds(s * G, G), 0:2 * D].broadcast_to([128, G, 2 * D])).then_inc(adr_in, 16)

            def load_gates(s, q):
                sp.dma_start(ADG[q][:, :, :], ada_v[:, bass.ds(s * G, G), 2 * D:3 * D].broadcast_to([128, G, D])).then_inc(adg_in, 16)
            load_rows(0, 0)
            load_gates(0, 0)

            def step_b(s, q):
                if isinstance(s, int) and s == GROUPS - 1:
                    return
                need(sp, u_done, s * G)
                sp.wait_ge(adr_in, 16 * (s + 1))
                load_rows(s + 1, 1 - q)
                need(sp, ga_done, s * G)
                sp.wait_ge(adg_in, 16 * (s + 1))
                load_gates(s + 1, 1 - q)
            run_steps(sp, step_b)

            sp.wait_ge(os_done, BATCH)
            sp.wait_ge(v_done, BATCH)
            sp.wait_ge(scaled, BATCH)
            sp.wait_ge(ot_mm, BATCH)
            sp.dma_start(w_up[:, :], ins["w_up"]).then_inc(wup_in, 16)

            def load_c(s, q):
                sp.dma_start(ADR[q][:, :, :], ada_v[:, bass.ds(s * G, G), 3 * D:5 * D].broadcast_to([128, G, 2 * D])).then_inc(cdr_in, 16)

            def load_cg(s, q):
                sp.dma_start(ADG[q][:, :, :], ada_v[:, bass.ds(s * G, G), 5 * D:6 * D].broadcast_to([128, G, D])).then_inc(cdg_in, 16)
            sp.wait_ge(u_done, BATCH)
            load_c(0, 0)
            sp.wait_ge(ga_done, BATCH)
            load_cg(0, 0)

            def step_c(s, q):
                if isinstance(s, int) and s == GROUPS - 1:
                    return
                need(sp, cu_done, s * G)
                sp.wait_ge(cdr_in, 16 * (s + 1))
                load_c(s + 1, 1 - q)
                need(sp, cga, s)
                sp.wait_ge(cdg_in, 16 * (s + 1))
                load_cg(s + 1, 1 - q)
            run_steps(sp, step_c)

            def load_t(s, q):
                sp.dma_start(ADT[q][:, :, :], ada_v[:, bass.ds(s * G, G), 6 * D:ADA].broadcast_to([128, G, EXPERTS])).then_inc(dt_in, 16)
            load_t(0, 0)

            def store(s, q):
                sp.wait_ge(out_done, (s + 1) * G)
                sp.dma_start(out_v[:, bass.ds(s * G, G), :], OUT[q][:, :, :]).then_inc(out_stored[q], 16)

            def step_d(s, q):
                last = isinstance(s, int) and s == GROUPS - 1
                if not last:
                    need(sp, rl_done, s)
                    sp.wait_ge(dt_in, 16 * (s + 1))
                    load_t(s + 1, 1 - q)
                if not (isinstance(s, int) and s == 0):
                    store(s - 1, 1 - q)
            run_steps(sp, step_d)
            store(GROUPS - 1, 1)
            for q in range(2):
                sp.wait_ge(out_stored[q], 16 * PAIRS)

        @block.gpsimd
        def _(pool):
            pool.memset(ident[:, :], 0.0).then_inc(consts, 1)
            pool.memset(ident16[:, :], 0.0).then_inc(consts, 1)
            pool.memset(tiny[:, :], TINY)
            pool.memset(zero[:, :], 0.0).then_inc(consts, 1)
            pool.wait_ge(consts, 3)
            for m in (ident, ident16):
                pool.affine_select(out=m[:, :], in_=m[:, :], compare_op=ALU.not_equal, fill=1.0, base=0,
                                   pattern=[[-1, 128]], channel_multiplier=1).then_inc(consts, 1)
            def phase_a(i):
                for q in range(2):
                    s = 2 * i + q
                    pool.wait_ge(fac_done, s + 1)
                    pool.wait_ge(x2_done, 2 * i)
                    pool.tensor_tensor(X1[q][:, :, :], X[:, bass.ds(s * G, G), :],
                                       factor[q][:, :].unsqueeze(2).broadcast_to([TOK, G, D]), ALU.mult).then_inc(x1_done, 1)
            for q in range(2):
                pool.memset(QS[q][:, :, :, :], 0.0)
                pool.memset(KS[q][:, :, :, :], 0.0)
                pool.memset(V[q][:, :, :, HD:HD + 1], HEAD_SCALE).then_inc(consts, 1)
            pool.memset(before[:, :, :], 1.0).then_inc(consts, 1)
            pool.wait_ge(consts, 8)
            pool.affine_select(out=before[:, :, :], in_=before[:, :, :], compare_op=ALU.is_gt, fill=0.0, base=0,
                               pattern=[[1, EXPERTS], [-1, EXPERTS]], channel_multiplier=0).then_inc(consts, 1)
            with pool.Fori(0, PAIRS) as i:
                phase_a(i)
            pool.wait_ge(wB_in, 64)
            pool.tensor_copy(wqkv_hl[0][:, :], w_qkv[:, :]).then_inc(wB_split, 1)
            pool.wait_ge(wB_split, 1)
            pool.tensor_tensor(wqkv_hl[1][:, :], w_qkv[:, :], wqkv_hl[0][:, :], ALU.subtract).then_inc(wB_split, 1)

            def v_scale(T, s, q, j, av_before):
                need(pool, fac_b, s + 1)
                need(pool, av_mm, av_before)
                pool.tensor_tensor(V[q][:, j, :, 0:HD], QKV[q][:, j, 2 * D:3 * D].rearrange("p (h d) -> p h d", d=HD),
                                   FC[q][:, j, 32:48].unsqueeze(2).broadcast_to([TOK, HEADS, HD]), ALU.mult).then_inc(v_done, 1)

            def gate(T, q, j):
                need(pool, ao_done, T + 1)
                if j == 0:
                    need(pool, adg_in, 4 * T + 16)
                pool.tensor_tensor(BR[:, bass.ds(T, 1), :], AO[j % 2][:, :].unsqueeze(1), ADG[q][:, j:j + 1, :], ALU.mult).then_inc(ga_done, 1)

            def step_b(s, q):
                last = isinstance(s, int) and s == GROUPS - 1
                for j in range(G):
                    T = s * G + j
                    if j < 3:
                        v_scale(T + 1, s, q, j + 1, (s - 1) * G)
                    elif not last:
                        v_scale(T + 1, s + 1, 1 - q, 0, s * G - 3)
                    if not (isinstance(T, int) and T == 0):
                        gate(T - 1, q if j else 1 - q, (j - 1) % G)
            v_scale(0, 0, 0, 0, 0)
            run_steps(pool, step_b)
            gate(BATCH - 1, 1, 3)

            def split(hl, w, count):
                pool.tensor_copy(hl[0], w).then_inc(wC_split, 1)
                pool.wait_ge(wC_split, count)
                pool.tensor_tensor(hl[1], w, hl[0], ALU.subtract)
            pool.wait_ge(wC_in, 64)
            split([h[:, :] for h in wf1_hl], w_f1[:, :], 1)
            split([h[:, :] for h in wr_hl], w_router[:, 0, :], 2)
            pool.wait_ge(wup_in, 16)
            for k in range(4):
                part = slice(k * FF, (k + 1) * FF)
                split([h[:, part] for h in wup_hl], w_up[:, part], 3 + k)

            def step_c(s, q):
                pool.wait_ge(ff_done, (s + 1) * G)
                pool.wait_ge(cdg_in, 16 * s + 16)
                pool.tensor_tensor(BR[:, bass.ds(s * G, G), :], FO[q][:, :, :], ADG[q][:, :, :], ALU.mult).then_inc(cga, 1)
            pool.wait_ge(wC_split, 6)
            pool.tensor_scalar(held_pool[:, :], zero[:, :], 1.0, 0.0, ALU.mult, ALU.add).then_inc(wD_split, 1)
            pool.wait_ge(x3_done, BATCH)
            run_steps(pool, step_c)

        @block.scalar
        def _(act):
            act.wait_ge(consts, 5)
            act.wait_ge(keep_lin, 1)
            act.activation(keep[:, :], keep[:, :], ACT.Sigmoid, bias=zero[:, 0:1]).then_inc(keep_sig, 1)
            act.preload_act_table_set("gelu_and_others")

            def phase_a(i):
                act.wait_ge(rank_done, 2 * i)
                act.wait_ge(norm_done, 8 * i)
                for q in range(2):
                    for j in range(G):
                        act.activation(junkA[q][:, j, :], X[:, bass.ds((2 * i + q) * G + j, 1), :], ACT.Square,
                                       accum_out=nsq[q][:, j:j + 1]).then_inc(norm_done, 1)
                for q in range(2):
                    act.wait_ge(x1T_mm, 2 * i + q + 1)
                    act.activation(X1T[q][:, :, :], bank[2 + q][:, :], ACT.Copy).then_inc(x1T_done, 1)
                for q in range(2):
                    act.wait_ge(y_mm, 2 * i + q + 1)
                    act.wait_ge(yT_mm, 2 * i)
                    for j in range(G):
                        act.activation(YT[q][:, j, :], bank[6 + q][:, j * TOK:(j + 1) * TOK], ACT.Gelu,
                                       bias=bias1[:, bass.ds((2 * i + q) * G + j, 1)]).then_inc(yT_done, 1)
            act.wait_ge(ada_done, 1)
            act.wait_ge(x_first, 16)
            phase_a(0)
            act.wait_ge(x_rest, 16 * (PAIRS - 1))
            with act.Fori(1, PAIRS) as i:
                phase_a(i)
            act.preload_act_table_set("natural_log_exp_and_others")

            def small(out_, in_, func, at, **more):
                act.wait_ge(chain, at)
                act.activation(out_[:, :], in_[:, :], func, **more).then_inc(chain_act, 1)

            def norm_rows(at):
                small(sm[1], sm[0], ACT.Ln, at + 4)
                act.wait_ge(chain_act, at_act[0] + 1)
                act.activation(sm[2][:, :], sm[1][:, :], ACT.Exp, scale=0.5, bias=zero[:, 0:1]).then_inc(chain_act, 1)
                act.activation(sm[3][:, :], sm[1][:, :], ACT.Exp, scale=-0.5, bias=zero[:, 0:1]).then_inc(chain_act, 1)
                small(sm[5], sm[4], ACT.Ln, at + 5, bias=1.0)
                act.activation(sm[6][:, :], sm[4][:, :], ACT.Ln, scale=-1.0, bias=1.0).then_inc(chain_act, 1)
                small(sm[8], sm[7], ACT.Ln, at + ROW_OPS - 1)
                act.wait_ge(chain_act, at_act[0] + 6)
                act.activation(row_r[:, :], sm[8][:, :], ACT.Exp, scale=-0.5, bias=zero[:, 0:1]).then_inc(rows_ready, 1)
                at_act[0] += 6
            at_act = [0]
            norm_rows(0)

            def act_mobius(k):
                small(sm[2], sm[0], ACT.Ln, mob_at[k] + 2)
                act.activation(sm[4][:, :], sm[1][:, :], ACT.Ln).then_inc(chain_act, 1)
                act.wait_ge(chain_act, at_act[0] + 2)
                act.activation(sm[3][:, :], sm[2][:, :], ACT.Exp, scale=-0.5).then_inc(chain_act, 1)
                act.activation(sm[5][:, :], sm[4][:, :], ACT.Exp, scale=0.5).then_inc(chain_act, 1)
                small(sm[7], sm[6], ACT.Tanh, mob_at[k] + 5)
                at_act[0] += 5
                act.wait_ge(coef_ready, k + 1)

            def front1(s, q):
                need(act, u_done, (s + 1) * G)
                need(act, n2u_done, s * G)
                for j in range(G):
                    act.activation(junkU[:, j, :], U[q][:, j, :], ACT.Square, accum_out=n2u[q][:, j:j + 1]).then_inc(n2u_done, 1)
                need(act, n2u_done, (s + 1) * G)
                act.activation(n2u[q][:, :], n2u[q][:, :], ACT.Ln, bias=tiny[:, 0:1]).then_inc(su_ln, 1)
                need(act, su_ln, s + 1)
                act.activation(n2u[q][:, :], n2u[q][:, :], ACT.Exp, scale=-0.5).then_inc(su_rs, 1)
                need(act, uT_mm, s + 1)
                act.activation(UHL[q][0][:, :], bank[0][:, :], ACT.Copy).then_inc(uT_hi, 1)

            def squares(T, q, j):
                need(act, qkv_done, T + 1)
                need(act, hsum_done, T - 1)
                act.activation(SQ[j % 2][:, :], QKV[q][:, j, :], ACT.Square).then_inc(sq_done, 1)

            def stats(s, q):
                need(act, psum_done, s + 1)
                act.activation(ST[q][:, :], ST[q][:, :], ACT.Ln, bias=tiny[:, 0:1]).then_inc(st_ln, 1)
                need(act, st_ln, s + 1)
                act.activation(ST[q][:, :], ST[q][:, :], ACT.Exp, scale=-0.5).then_inc(st_rs, 1)

            def high_parts(T, j):
                need(act, scaled, T + 1)
                need(act, t16_mm, T - 1)
                sc = SC[j % 2][:, :].rearrange("p (a h d) -> p a h d", a=2, d=HD)
                act.activation(QS[j % 2][:, :, 0:3:2, :], sc[:, 0, :, :].unsqueeze(2).broadcast_to([TOK, HEADS, 2, HD]), ACT.Copy).then_inc(hi_done, 1)
                act.activation(KS[j % 2][:, :, 0:2, :], sc[:, 1, :, :].unsqueeze(2).broadcast_to([TOK, HEADS, 2, HD]), ACT.Copy).then_inc(hi_done, 1)

            def qk_out(T, j):
                need(act, t16_mm, T + 1)
                need(act, score_b2, T - 1)
                act.activation(QKT[j % 2][:, :, :, :].rearrange("p a c n -> p (a c n)"), bank[2][:, :].bitcast(FP16), ACT.Copy).then_inc(t16_out, 1)

            def exps(T, j, half):
                need(act, score_b2 if half else score_a, T + 1)
                need(act, av_mm, T - 1)
                act.activation(P[j % 2][:, 2 * half:2 * half + 2, :, :].rearrange("p i c n -> p (i c n)"), wide[:, 1024 * half:1024 * half + 1024],
                               ACT.Exp, scale=HD ** -0.5).then_inc(exp_b if half else exp_a, 1)

            def o_out(T, j):
                need(act, av_mm, T + 1)
                need(act, ot_mm, T - 1)
                act.activation(OS[j % 2][:, :, :].rearrange("p c n -> p (c n)"), bank[3][:, :], ACT.Copy).then_inc(os_done, 1)

            def on_out(T, j):
                need(act, onT_mm, T + 1)
                need(act, wo_mm, T - 1)
                act.activation(OT[j % 2][:, :], bank[1][:, 0:TOK], ACT.Copy).then_inc(onT_out, 1)

            def norms(T, j):
                need(act, n2a_done, T)
                need(act, ao_done, T + 1)
                act.activation(junkS[j % 2][:, 0, :], AO[j % 2][:, :], ACT.Square, accum_out=n2a[:, bass.ds(T, 1)]).then_inc(n2a_done, 1)
                need(act, ga_done, T + 1)
                need(act, n2g_done, T)
                act.activation(junkS[j % 2][:, 1:2, :], BR[:, bass.ds(T, 1), :], ACT.Square, accum_out=n2g[:, bass.ds(T, 1)]).then_inc(n2g_done, 1)

            def step_b(s, q):
                last = isinstance(s, int) and s == GROUPS - 1
                for j in range(G):
                    T = s * G + j
                    start = isinstance(T, int) and T == 0
                    exps(T, j, 0)
                    if j < 3:
                        high_parts(T + 1, j + 1)
                    elif not last:
                        stats(s + 1, 1 - q)
                        high_parts(T + 1, 0)
                    exps(T, j, 1)
                    if not start:
                        on_out(T - 1, (j - 1) % G)
                    if not (last and j == 3):
                        qk_out(T + 1, (j + 1) % G)
                    if not last:
                        if j == 0:
                            front1(s + 1, 1 - q)
                        elif j == 1:
                            squares((s + 1) * G, 1 - q, 0)
                            squares((s + 1) * G + 1, 1 - q, 1)
                        elif j == 2:
                            squares((s + 1) * G + 2, 1 - q, 2)
                            squares((s + 1) * G + 3, 1 - q, 3)
                    if not start:
                        norms(T - 1, (j - 1) % G)
                    o_out(T, j)
            front1(0, 0)
            for j in range(G):
                squares(j, 0, j)
            stats(0, 0)
            high_parts(0, 0)
            qk_out(0, 0)
            run_steps(act, step_b)
            on_out(BATCH - 1, 3)
            norms(BATCH - 1, 3)

            act_mobius(0)
            act.preload_act_table_set("natural_log_exp_and_others")

            def step_x3(s, q):
                for j in range(G):
                    T = s * G + j
                    act.activation(X3[:, bass.ds(T, 1), :], X[:, bass.ds(T, 1), :], ACT.Copy, scale=al[:, bass.ds(T, 1)]).then_inc(xa_done, 1)
            run_steps(act, step_x3)
            norm_rows(NORM2_AT)

            def c_front_norm(s, q):
                need(act, cu_done, (s + 1) * G)
                need(act, cn2u, s * G)
                for j in range(G):
                    act.activation(junkU[:, j, :], U[q][:, j, :], ACT.Square, accum_out=n2u[q][:, j:j + 1]).then_inc(cn2u, 1)
                need(act, cn2u, (s + 1) * G)
                act.activation(n2u[q][:, :], n2u[q][:, :], ACT.Ln, bias=tiny[:, 0:1]).then_inc(csu_ln, 1)
                need(act, csu_ln, s + 1)
                act.activation(n2u[q][:, :], n2u[q][:, :], ACT.Exp, scale=-0.5).then_inc(csu_rs, 1)

            def c_front_high(s, q):
                need(act, cT_mm, s + 1)
                act.activation(UHL[q][0][:, :], bank[0][:, :], ACT.Copy).then_inc(cT_hi, 1)

            def h_evacuate(s, q, k):
                need(act, f1_mm, 4 * s + k + 1)
                act.activation(HT[q][:, k, :], bank[4 + k], ACT.Identity, bias=w_f1Tb[:, k, D:D + 1]).then_inc(h_out, 1)

            def h_norm(s, q):
                need(act, hq3, s + 1)
                act.activation(hq[q][:, :], hq[q][:, :], ACT.Ln).then_inc(hln, 1)
                need(act, hln, s + 1)
                act.activation(hq[q][:, :], hq[q][:, :], ACT.Exp, scale=-0.5).then_inc(hrs, 1)

            def c_norms(s, q):
                need(act, cn2a, s * G)
                need(act, ff_done, (s + 1) * G)
                need(act, cn2g, s * G)
                for j in range(G):
                    T = s * G + j
                    act.activation(junkA[1][:, j, :], FO[q][:, j, :], ACT.Square, accum_out=n2a[:, bass.ds(T, 1)]).then_inc(cn2a, 1)
                need(act, cga, s + 1)
                for j in range(G):
                    T = s * G + j
                    act.activation(junkA[0][:, j:j + 1, :], BR[:, bass.ds(T, 1), :], ACT.Square, accum_out=n2g[:, bass.ds(T, 1)]).then_inc(cn2g, 1)

            def step_c(s, q):
                last = isinstance(s, int) and s == GROUPS - 1
                h_evacuate(s, q, 0)
                h_evacuate(s, q, 1)
                if not last:
                    c_front_norm(s + 1, 1 - q)
                h_evacuate(s, q, 2)
                h_evacuate(s, q, 3)
                if not last:
                    c_front_high(s + 1, 1 - q)
                h_norm(s, q)
                if not (isinstance(s, int) and s == 0):
                    c_norms(s - 1, 1 - q)
            c_front_norm(0, 0)
            c_front_high(0, 0)
            run_steps(act, step_c)
            c_norms(GROUPS - 1, 1)
            act_mobius(1)

            def d_front(s, q):
                need(act, x4T_mm, s + 1)
                act.activation(UHL[q][0][:, :], bank[0][:, :], ACT.Copy).then_inc(x4_hi, 1)
                need(act, x4_done, (s + 1) * G)
                act.activation(X[:, bass.ds(s * G, G), :], X4[q][:, :, :], ACT.Copy).then_inc(x4_copy, 1)

            def d_router(s, q):
                need(act, rl_done, s + 1)
                act.activation(sg[q][:, :, :], sg[q][:, :, :], ACT.Sigmoid).then_inc(sig_done, 1)

            def step_d(s, q):
                last = isinstance(s, int) and s == GROUPS - 1
                for k in range(SHARED_CHUNKS):
                    need(act, up_mm, 16 * s + 2 * k + 1)
                    need(act, hs_mul, 4 * s + k - 1)
                    act.activation(S1[k % 2][:, :], bank[4 + (2 * k) % 4], ACT.Silu).then_inc(silu_done, 1)
                for e in range(EXPERTS):
                    need(act, up_mm, 16 * s + 8 + e + 1)
                    if e == 0:
                        need(act, rd_b, (s - 1) * G)
                    act.activation(HR[q][:, e, :], bank[4 + e % 4], ACT.Gelu).then_inc(gelu_done, 1)
                    if e == 3 and not last:
                        d_front(s + 1, 1 - q)
                if not last:
                    d_router(s + 1, 1 - q)
            d_front(0, 0)
            d_router(0, 0)
            run_steps(act, step_d)

        @block.tensor
        def _(pe):
            mm = nc.tensor.matmul
            pe.wait_ge(wA_in, 16 * (WA - 1))
            mm(bank[0][:, 0:BATCH], score_w[:, 0:1].to_broadcast([D, 128]), condT[:, :], start=True, stop=True).then_inc(keep_mm, 1)
            mm(bank[4][0:BATCH, :], condT[:, :], w_ada[:, 0:512], start=True, stop=True)
            mm(bank[5][0:BATCH, 0:256], condT[:, :], w_ada[:, 512:768], start=True, stop=True)
            mm(bank[5][0:BATCH, 256:256 + EXPERTS], condT[:, :], w_router[:, 1, :], start=True, stop=True).then_inc(ada_mm, 1)
            pe.wait_ge(consts, 5)
            pe.wait_ge(ada_done, 3)
            pe.wait_ge(keep_lin, 1)

            def phase_a(i):
                for q in range(2):
                    pe.wait_ge(norm_done, 8 * i + 4 * q + 4)
                    pe.wait_ge(x2_done, 2 * i)
                    for j in range(G):
                        last = nc.tensor.transpose(bank[q][:, j * TOK:(j + 1) * TOK], nsq[q][:, j:j + 1].to_broadcast([TOK, TOK]), ident[:, :])
                    last.then_inc(norm_bc, 1)
                for q in range(2):
                    pe.wait_ge(f_in[q], 16 * i + 16)
                    pe.wait_ge(mb_done, 2 * i)
                    for j in range(G):
                        last = mm(bank[4 + q][:, j * D:(j + 1) * D], fT[q][:, j, :], fT[q][:, j, :], start=True, stop=True)
                    last.then_inc(gram_mm, 1)
                for q in range(2):
                    pe.wait_ge(x1_done, 2 * i + q + 1)
                    pe.wait_ge(x1T_done, 2 * i)
                    for j in range(G):
                        last = nc.tensor.transpose(bank[2 + q][:, j * TOK:(j + 1) * TOK], X1[q][:, j, :], ident[:, :])
                    last.then_inc(x1T_mm, 1)
                for q in range(2):
                    pe.wait_ge(mb_done, 2 * i + q + 1)
                    pe.wait_ge(x1T_done, 2 * i + q + 1)
                    pe.wait_ge(yT_done, 8 * i)
                    for j in range(G):
                        last = mm(bank[6 + q][:, j * TOK:(j + 1) * TOK], MB[q][:, j, :], X1T[q][:, j, :], start=True, stop=True)
                    last.then_inc(y_mm, 1)
                for q in range(2):
                    pe.wait_ge(yT_done, 8 * i + 4 * q + 4)
                    pe.wait_ge(rank_done, 2 * i + q + 1)
                    for j in range(G):
                        last = nc.tensor.transpose(bank[q][:, j * TOK:(j + 1) * TOK], YT[q][:, j, :], ident[:, :])
                    last.then_inc(yT_mm, 1)
            with pe.Fori(0, PAIRS) as i:
                phase_a(i)
            pe.wait_ge(wB_split, 2)
            pe.wait_ge(bank3_clear, 1)

            def product(out_, left, right, start=True, stop=True):
                mm(out_, left[0], right[0], start=start, stop=False)
                mm(out_, left[0], right[1], start=False, stop=False)
                return mm(out_, left[1], right[0], start=False, stop=stop)

            def u_transpose(s, q):
                need(pe, u_done, (s + 1) * G)
                need(pe, qkv_done, s * G)
                for j in range(G):
                    last = nc.tensor.transpose(bank[0][:, j * TOK:(j + 1) * TOK], U[q][:, j, :], ident[:, :])
                last.then_inc(uT_mm, 1)

            def qkv(T, s, q, j):
                need(pe, uT_lo, s + 1)
                need(pe, qkv_done, T)
                part = slice(j * TOK, (j + 1) * TOK)
                product(bank[0][:, 0:3 * D], [h[:, part] for h in UHL[q]], [w[:, :] for w in wqkv_hl]).then_inc(qkv_mm, 1)

            def qk_transpose(T, j):
                need(pe, lo_done, T + 1)
                need(pe, t16_out, T)
                b16 = bank[2][:, :].bitcast(FP16)
                for a, src in enumerate((QS, KS)):
                    flat = src[j % 2][:, :, :, :].rearrange("p h s d -> p (h s d)")
                    for c in range(4):
                        last = nc.tensor.transpose(b16[:, (4 * a + c) * TOK:(4 * a + c + 1) * TOK], flat[:, c * 128:(c + 1) * 128], ident16[:, :])
                last.then_inc(t16_mm, 1)

            def scores(T, j, half):
                need(pe, t16_out, T + 1)
                need(pe, exp_b if half else exp_a, T)
                t = QKT[j % 2]
                for c in range(4):
                    for i in (2 * half, 2 * half + 1):
                        r = slice(32 * i, 32 * i + 32)
                        last = mm(bank[4 + i][:, c * TOK:(c + 1) * TOK], t[r, 1, c, :], t[r, 0, c, :], start=True, stop=True)
                last.then_inc(score_b2 if half else score_a, 1)

            def attend(T, q, j):
                need(pe, exp_b, T + 1)
                need(pe, v_done, T + 1)
                need(pe, os_done, T)
                for c in range(4):
                    for i in range(4):
                        last = mm(bank[3][32 * i:32 * i + HD + 1, c * TOK:(c + 1) * TOK], V[q][:, j, 4 * c + i, :], P[j % 2][:, i, c, :], start=True, stop=True)
                last.then_inc(av_mm, 1)

            def o_transpose(T, j):
                need(pe, os_done, T + 1)
                need(pe, ao_done, T)
                for c in range(4):
                    last = nc.tensor.transpose(bank[1][:, c * 128:(c + 1) * 128], OS[j % 2][:, c, :], ident[:, :])
                last.then_inc(ot_mm, 1)

            def on_transpose(T, j):
                need(pe, on_done, T + 1)
                nc.tensor.transpose(bank[1][:, 0:TOK], ON[j % 2][:, :], ident[:, :]).then_inc(onT_mm, 1)

            def project(T, j):
                need(pe, onT_out, T + 1)
                mm(bank[1][:, TOK:2 * TOK], OT[j % 2][:, :], w_o[:, :], start=True, stop=True).then_inc(wo_mm, 1)

            def step_b(s, q):
                last = isinstance(s, int) and s == GROUPS - 1
                for j in range(G):
                    T = s * G + j
                    start = isinstance(T, int) and T == 0
                    scores(T, j, 0)
                    scores(T, j, 1)
                    if not start:
                        o_transpose(T - 1, (j - 1) % G)
                    if not last:
                        if j == 0:
                            u_transpose(s + 1, 1 - q)
                        elif j < 3:
                            qkv((s + 1) * G + 2 * j - 2, s + 1, 1 - q, 2 * j - 2)
                    if not (last and j == 3):
                        qk_transpose(T + 1, (j + 1) % G)
                    if not start:
                        on_transpose(T - 1, (j - 1) % G)
                    if not last and 0 < j < 3:
                        qkv((s + 1) * G + 2 * j - 1, s + 1, 1 - q, 2 * j - 1)
                    attend(T, q, j)
                    if not start:
                        project(T - 1, (j - 1) % G)
            u_transpose(0, 0)
            for j in range(G):
                qkv(j, 0, 0, j)
            qk_transpose(0, 0)
            run_steps(pe, step_b)
            o_transpose(BATCH - 1, 3)
            on_transpose(BATCH - 1, 3)
            project(BATCH - 1, 3)


            pe.wait_ge(wC_in, 64)
            pe.wait_ge(ao_done, BATCH)
            for k in range(4):
                mm(bank[1][:, 0:D + 1], w_f1Tb[:, k, 0:D], w_f1Tb[:, k, :], start=k == 0, stop=k == 3)
            for k in range(4):
                last = mm(bank[0][:, 0:1], w_f1Tb[:, k, D:D + 1].to_broadcast([128, 128]), w_f1Tb[:, k, D:D + 1], start=k == 0, stop=k == 3)
            last.then_inc(gram2_mm, 1)
            pe.wait_ge(gram2_done, 3)

            def c_transpose(s, q):
                need(pe, c_done, s + 1)
                need(pe, cT_lo, s)
                for j in range(G):
                    last = nc.tensor.transpose(bank[0][:, j * TOK:(j + 1) * TOK], C[q][:, j, :], ident[:, :])
                last.then_inc(cT_mm, 1)

            def step_c(s, q):
                last_step = isinstance(s, int) and s == GROUPS - 1
                need(pe, cT_lo, s + 1)
                for k in range(4):
                    need(pe, h_out, 4 * s + k - 3)
                    product(bank[4 + k], [w[:, k * 128:(k + 1) * 128] for w in wf1_hl], [h[:, :] for h in UHL[q]]).then_inc(f1_mm, 1)
                need(pe, hq2, s)
                for j in range(G):
                    last = product(bank[1 + j // 2][:, (j % 2) * (D + 1):(j % 2 + 1) * (D + 1)], [h[:, j * TOK:(j + 1) * TOK] for h in UHL[q]], [g[:, :] for g in gram_hl])
                last.then_inc(g_mm, 1)
                if not last_step:
                    c_transpose(s + 1, 1 - q)
                need(pe, h_out, 4 * s + 4)
                need(pe, ff_done, s * G)
                for j in range(G):
                    for k in range(4):
                        last = mm(bank[3][:, j * D:(j + 1) * D], HT[q][:, k, j * TOK:(j + 1) * TOK], w_f2[:, k, :], start=k == 0, stop=k == 3)
                last.then_inc(f2_mm, 1)
            pe.wait_ge(wC_split, 2)
            c_transpose(0, 0)
            run_steps(pe, step_c)

            pe.wait_ge(wD_in, 48)
            pe.wait_ge(ff_done, BATCH)

            def d_front(s, q):
                need(pe, x4_done, (s + 1) * G)
                need(pe, rl_done, s)
                for j in range(G):
                    last = nc.tensor.transpose(bank[0][:, j * TOK:(j + 1) * TOK], X4[q][:, j, :], ident[:, :])
                last.then_inc(x4T_mm, 1)

            def d_router(s, q):
                need(pe, x4_lo, s + 1)
                for j in range(G):
                    last = product(bank[0][:, j * EXPERTS:(j + 1) * EXPERTS], [h[:, j * TOK:(j + 1) * TOK] for h in UHL[q]], [w[:, :] for w in wr_hl])
                last.then_inc(rl_mm, 1)

            def up(s, q, n):
                col = (n % 2) * FF + (n // 2) * 128 if n < 8 else 2 * FF + (n - 8) * 128
                if n == 0:
                    need(pe, x4_lo, s + 1)
                if n < 4:
                    need(pe, gelu_done, 8 * s - 4 + n + 1)
                elif n < 12:
                    k = (n - 4) // 2
                    if n % 2 == 0:
                        need(pe, silu_done, 4 * s + k + 1)
                    else:
                        need(pe, hs_mul, 4 * s + k + 1)
                else:
                    need(pe, gelu_done, 8 * s + n - 12 + 1)
                product(bank[4 + n % 4], [w[:, col:col + 128] for w in wup_hl], [h[:, :] for h in UHL[q]]).then_inc(up_mm, 1)

            def down(s, q, j):
                T = s * G + j
                part = slice(j * TOK, (j + 1) * TOK)
                if j == 0:
                    need(pe, hs_mul, 4 * s + 4)
                    need(pe, gelu_done, 8 * s + 8)
                need(pe, acc_shared, T)
                for k in range(SHARED_CHUNKS):
                    last = mm(bank[2][:, 0:D], HS[q][:, k, part], w_sd[:, k, :], start=k == 0, stop=k == SHARED_CHUNKS - 1)
                last.then_inc(sd_mm, 1)
                need(pe, acc_half, T)
                for e in range(4):
                    last = mm(bank[3][:, e * D:(e + 1) * D], HR[q][:, e, part], w_rd[:, e, :], start=True, stop=True)
                last.then_inc(rd_a, 1)
                need(pe, out_done, T)
                for e in range(4):
                    last = mm(bank[1][:, e * D:(e + 1) * D], HR[q][:, 4 + e, part], w_rd[:, 4 + e, :], start=True, stop=True)
                last.then_inc(rd_b, 1)

            def step_d(s, q):
                first = isinstance(s, int) and s == 0
                last_step = isinstance(s, int) and s == GROUPS - 1
                for j in range(G):
                    for n in range(4 * j, 4 * j + 4):
                        up(s, q, n)
                    if not first:
                        down(s - 1, 1 - q, j)
                    if j == 1 and not last_step:
                        d_front(s + 1, 1 - q)
                    if j == 2 and not last_step:
                        d_router(s + 1, 1 - q)
            pe.wait_ge(wC_split, 6)
            pe.wait_ge(wD_split, 1)
            d_front(0, 0)
            d_router(0, 0)
            run_steps(pe, step_d)
            for j in range(G):
                down(GROUPS - 1, 1, j)

        @block.vector
        def _(dve):
            places = iter(range(64))

            def hold(semaphore, value):
                dve.wait_ge(semaphore, value)
                place = next(places)
                nc.vector.tensor_scalar(held[:, place:place + 1], zero[:, 0:1], 1.0, None, ALU.mult)

            dve.wait_ge(consts, 5)
            dve.wait_ge(wA_in, 16 * (WA - 1))
            dve.wait_ge(keep_mm, 1)
            nc.vector.tensor_scalar(keep[:, :], bank[0][:, 0:BATCH], score_b[:, 0:1], None, ALU.add).then_inc(keep_lin, 1)
            nc.vector.tensor_scalar(bias1[:, :], condT[:, :], fc_bias[:, 0:1], None, ALU.add).then_inc(ada_done, 1)
            dve.wait_ge(ada_mm, 1)
            nc.vector.tensor_tensor(ada_sb[:, 0:512], bank[4][0:BATCH, :], b_ada[:, 0:512], ALU.add)
            nc.vector.tensor_tensor(ada_sb[:, 512:768], bank[5][0:BATCH, 0:256], b_ada[:, 512:768], ALU.add)
            nc.vector.tensor_copy(ada_sb[:, 768:ADA], bank[5][0:BATCH, 256:256 + EXPERTS]).then_inc(ada_done, 1)
            dve.wait_ge(ada_done, 2)
            sc = ada_sb[:, 0:768].rearrange("b (k n) -> b k n", k=2)[:, :, D:2 * D]
            nc.vector.tensor_scalar(sc, sc, 1.0, None, ALU.add).then_inc(ada_done, 1)
            dve.wait_ge(keep_sig, 1)
            nc.vector.tensor_scalar(keep[:, :], keep[:, :], float(TOK), 1.0, ALU.mult, ALU.max).then_inc(keep_done, 1)
            dve.wait_ge(keep_done, 1)

            def phase_a(i):
                dve.wait_ge(mvA, 2 * i)
                dve.wait_ge(x1_done, 2 * i)
                for q in range(2):
                    s = 2 * i + q
                    dve.wait_ge(norm_bc, s + 1)
                    for j in range(G):
                        last = nc.vector.tensor_scalar(junkV[q][:, j, :], bank[q][:, j * TOK:(j + 1) * TOK], nsq[q][:, j:j + 1], 0.0,
                                                       ALU.is_gt, ALU.add, accum_out=above[q][:, j:j + 1])
                    last.then_inc(rank_done, 1)
                for q in range(2):
                    s = 2 * i + q
                    dve.wait_ge(rank_done, s + 1)
                    nc.vector.scalar_tensor_tensor(above[q][:, :], above[q][:, :], 1.0, keep[:, bass.ds(s * G, G)], ALU.add, ALU.is_le).then_inc(keep_done, 1)
                    dve.wait_ge(keep_done, 2 * i + q + 2)
                    nc.vector.tensor_scalar(factor[q][:, :], above[q][:, :], 1.0, None, ALU.add).then_inc(fac_done, 1)
                for q in range(2):
                    s = 2 * i + q
                    dve.wait_ge(gram_mm, s + 1)
                    dve.wait_ge(y_mm, 2 * i)
                    nc.vector.scalar_tensor_tensor(MB[q][:, :, :], bank[4 + q][:, :].rearrange("p (g n) -> p g n", g=G), 1.0 / (D * RANK),
                                                   w1T[:, :].unsqueeze(1).broadcast_to([D, G, D]), ALU.mult, ALU.add).then_inc(mb_done, 1)
                for q in range(2):
                    s = 2 * i + q
                    dve.wait_ge(yT_mm, s + 1)
                    nc.vector.tensor_tensor(X[:, bass.ds(s * G, G), :], bank[q][:, :].rearrange("p (g n) -> p g n", g=G), X1[q][:, :, :], ALU.add).then_inc(x2_done, 1)
                for q in range(2):
                    s = 2 * i + q
                    hold(x2_done, s + 1)
                    for j in range(G):
                        last = nc.vector.bn_stats(st6[q][:, j, :], X[:, bass.ds(s * G + j, 1), :])
                    last.then_inc(statA, 1)
                for q in range(2):
                    s = 2 * i + q
                    hold(statA, s + 1)
                    for j in range(G):
                        last = nc.vector.bn_aggr(mvq[q][:, j, :], st6[q][:, j, :])
                    last.then_inc(aggrA, 1)
                for q in range(2):
                    s = 2 * i + q
                    dve.wait_ge(aggrA, s + 1)
                    nc.vector.tensor_scalar(mv[:, bass.ds(s * G, G), :], mvq[q][:, :, :], 1.0, None, ALU.mult).then_inc(mvA, 1)
            with dve.Fori(0, PAIRS) as i:
                phase_a(i)
            nc.vector.memset(bank[3][:, :], 0.0).then_inc(bank3_clear, 1)

            links = [0]

            def link(instruction):
                links[0] += 1
                instruction.then_inc(chain, 1)
                dve.wait_ge(chain, links[0])

            def norm_rows(acts):
                vec, m, v = nc.vector, mv[:, :, 0], mv[:, :, 1]
                at = links[0]
                link(vec.tensor_tensor(row_n2[:, :], m, m, ALU.mult))
                link(vec.tensor_tensor(row_n2[:, :], row_n2[:, :], v, ALU.add))
                link(vec.tensor_scalar(row_n2[:, :], row_n2[:, :], float(D), None, ALU.mult))
                link(vec.tensor_scalar(sm[0][:, :], row_n2[:, :], TINY, None, ALU.max))
                dve.wait_ge(chain_act, acts + 3)
                link(vec.tensor_scalar(sm[4][:, :], sm[2][:, :], MAX_NORM, None, ALU.min))
                link(vec.tensor_scalar(sm[0][:, :], sm[0][:, :], 0.0625, None, ALU.min))
                link(vec.tensor_scalar(sm[7][:, :], sm[0][:, :], 1 / 11, 1 / 9, ALU.mult, ALU.add))
                for k in (7, 5, 3, 1):
                    link(vec.tensor_tensor(sm[7][:, :], sm[7][:, :], sm[0][:, :], ALU.mult))
                    link(vec.tensor_scalar(sm[7][:, :], sm[7][:, :], 1 / k, None, ALU.add))
                link(vec.tensor_scalar(sm[8][:, :], sm[2][:, :], 0.25, None, ALU.is_lt))
                link(vec.tensor_tensor(sm[7][:, :], sm[7][:, :], sm[8][:, :], ALU.mult))
                link(vec.tensor_scalar(sm[8][:, :], sm[8][:, :], -0.5, 0.5, ALU.mult, ALU.add))
                dve.wait_ge(chain_act, acts + 5)
                link(vec.tensor_tensor(sm[5][:, :], sm[5][:, :], sm[6][:, :], ALU.subtract))
                link(vec.tensor_tensor(sm[5][:, :], sm[5][:, :], sm[3][:, :], ALU.mult))
                link(vec.tensor_tensor(sm[5][:, :], sm[5][:, :], sm[8][:, :], ALU.mult))
                link(vec.tensor_tensor(sm[5][:, :], sm[5][:, :], sm[7][:, :], ALU.add))
                link(vec.reciprocal(sm[5][:, :], sm[5][:, :]))
                link(vec.tensor_tensor(sm[5][:, :], sm[5][:, :], sm[5][:, :], ALU.mult))
                link(vec.scalar_tensor_tensor(sm[7][:, :], sm[5][:, :], 1e-6, v, ALU.mult, ALU.add))
                assert links[0] == at + ROW_OPS - 1
            dve.wait_ge(mvA, GROUPS)
            norm_rows(0)
            dve.wait_ge(rows_ready, 1)
            dve.wait_ge(wB_in, 64)

            def front1(s, q):
                dve.wait_ge(adr_in, 16 * (s + 1))
                need(dve, u_done, s * G)
                need(dve, uT_mm, s - 1)
                need(dve, n2u_done, (s - 1) * G)
                for j in range(G):
                    T = s * G + j
                    nc.vector.scalar_tensor_tensor(U[q][:, j:j + 1, :], X[:, bass.ds(T, 1), :], mv[:, bass.ds(T, 1), 0], ADR[q][:, j:j + 1, D:2 * D], ALU.subtract, ALU.mult).then_inc(u_half, 1)
                for j in range(G):
                    T = s * G + j
                    need(dve, u_half, T + 1)
                    nc.vector.scalar_tensor_tensor(U[q][:, j, :], U[q][:, j, :], row_r[:, bass.ds(T, 1)], ADR[q][:, j, 0:D], ALU.mult, ALU.add).then_inc(u_done, 1)
                need(dve, su_rs, s + 1)
                nc.vector.tensor_scalar(su[q][:, :], n2u[q][:, :], CAP, 1.0, ALU.mult, ALU.min).then_inc(su_done, 1)
                need(dve, uT_hi, s + 1)
                nc.vector.tensor_tensor(UHL[q][1][:, :], bank[0][:, :], UHL[q][0][:, :], ALU.subtract).then_inc(uT_lo, 1)

            def qkv_out(T, s, q, j):
                need(dve, su_done, s + 1)
                need(dve, qkv_mm, T + 1)
                nc.vector.scalar_tensor_tensor(QKV[q][:, j, :], bank[0][:, 0:3 * D], su[q][:, j:j + 1], b_qkv[:, :], ALU.mult, ALU.add).then_inc(qkv_done, 1)

            def head_sums(T, q, j):
                need(dve, sq_done, T + 1)
                nc.vector.tensor_reduce(ST[q][:, j * 48:(j + 1) * 48], SQ[j % 2][:, :].rearrange("p (a d) -> p a d", d=HD), AX.X, ALU.add).then_inc(hsum_done, 1)

            def projection_sums(s, q):
                need(dve, hsum_done, (s + 1) * G)
                nc.vector.tensor_reduce(ST[q][:, G * 48:G * 51], ST[q][:, 0:G * 48].rearrange("p (a h) -> p a h", h=HEADS), AX.X, ALU.add).then_inc(psum_done, 1)

            def factors(s, q):
                need(dve, st_rs, s + 1)
                nc.vector.tensor_scalar(FP[q][:, :], ST[q][:, G * 48:G * 51], CAP * HEAD_SCALE, HEAD_SCALE, ALU.mult, ALU.min).then_inc(fp_a, 1)
                need(dve, fp_a, s + 1)
                nc.vector.scalar_tensor_tensor(FC[q][:, :, :].rearrange("p g (a h) -> p (g a) h", h=HEADS), ST[q][:, 0:G * 48].rearrange("p (a h) -> p a h", h=HEADS), CAP,
                                               FP[q][:, :].unsqueeze(2).broadcast_to([TOK, G * 3, HEADS]), ALU.mult, ALU.min).then_inc(fac_b, 1)

            def scale_qk(T, s, q, j):
                need(dve, fac_b, s + 1)
                need(dve, hi_done, 2 * T - 2)
                need(dve, scaled, T)
                nc.vector.tensor_tensor(SC[j % 2][:, :].rearrange("p (h d) -> p h d", d=HD), QKV[q][:, j, 0:2 * D].rearrange("p (h d) -> p h d", d=HD),
                                        FC[q][:, j, 0:32].unsqueeze(2).broadcast_to([TOK, 32, HD]), ALU.mult).then_inc(scaled, 1)

            def low_parts(T, j):
                sc = SC[j % 2][:, :].rearrange("p (a h d) -> p a h d", a=2, d=HD)
                need(dve, hi_done, 2 * T + 2)
                nc.vector.tensor_tensor(QS[j % 2][:, :, 1, :], sc[:, 0, :, :], QS[j % 2][:, :, 0, :], ALU.subtract)
                nc.vector.tensor_tensor(KS[j % 2][:, :, 2, :], sc[:, 1, :, :], KS[j % 2][:, :, 0, :], ALU.subtract).then_inc(lo_done, 1)

            def normalise(T, j):
                need(dve, ot_mm, T + 1)
                heads = bank[1][:, :].rearrange("p (h e) -> p h e", e=32)
                nc.vector.reciprocal(RD[j % 2][:, :], heads[:, :, HD]).then_inc(rd_done, 1)
                need(dve, rd_done, T + 1)
                nc.vector.tensor_tensor(ON[j % 2][:, :].rearrange("p (h d) -> p h d", d=HD), heads[:, :, 0:HD],
                                        RD[j % 2][:, :].unsqueeze(2).broadcast_to([TOK, HEADS, HD]), ALU.mult).then_inc(on_done, 1)

            def ao_out(T, j):
                need(dve, wo_mm, T + 1)
                need(dve, ga_done, T - 1)
                need(dve, n2a_done, T - 1)
                nc.vector.tensor_tensor(AO[j % 2][:, :], bank[1][:, TOK:2 * TOK], b_o[:, :], ALU.add).then_inc(ao_done, 1)

            def dot_x(T, j):
                need(dve, ga_done, T + 1)
                need(dve, dx_done, T)
                nc.vector.scalar_tensor_tensor(junkD[j % 2][:, :].unsqueeze(1), BR[:, bass.ds(T, 1), :], 1.0, X[:, bass.ds(T, 1), :], ALU.mult, ALU.mult,
                                               accum_out=dxg[:, bass.ds(T, 1)]).then_inc(dx_done, 1)

            def step_b(s, q):
                last = isinstance(s, int) and s == GROUPS - 1
                for j in range(G):
                    T = s * G + j
                    start = isinstance(T, int) and T == 0
                    if j < 3:
                        scale_qk(T + 1, s, q, j + 1)
                        low_parts(T + 1, j + 1)
                    elif not last:
                        head_sums((s + 1) * G + 2, 1 - q, 2)
                        head_sums((s + 1) * G + 3, 1 - q, 3)
                        projection_sums(s + 1, 1 - q)
                        factors(s + 1, 1 - q)
                        scale_qk(T + 1, s + 1, 1 - q, 0)
                        low_parts(T + 1, 0)
                    if not start:
                        normalise(T - 1, (j - 1) % G)
                    if not last:
                        if j == 0:
                            front1(s + 1, 1 - q)
                        elif j < 3:
                            qkv_out((s + 1) * G + 2 * j - 2, s + 1, 1 - q, 2 * j - 2)
                            qkv_out((s + 1) * G + 2 * j - 1, s + 1, 1 - q, 2 * j - 1)
                        if j == 2:
                            head_sums((s + 1) * G, 1 - q, 0)
                            head_sums((s + 1) * G + 1, 1 - q, 1)
                    if not start:
                        ao_out(T - 1, (j - 1) % G)
                        dot_x(T - 1, (j - 1) % G)
            front1(0, 0)
            for j in range(G):
                qkv_out(j, 0, 0, j)
                head_sums(j, 0, j)
            projection_sums(0, 0)
            factors(0, 0)
            scale_qk(0, 0, 0, 0)
            low_parts(0, 0)
            run_steps(dve, step_b)
            normalise(BATCH - 1, 3)
            ao_out(BATCH - 1, 3)
            dot_x(BATCH - 1, 3)

            def mobius(k, acts):
                vec = nc.vector
                assert links[0] == mob_at[k]
                link(vec.tensor_scalar(sm[0][:, :], n2a[:, :], TINY, None, ALU.max))
                link(vec.tensor_scalar(sm[1][:, :], n2g[:, :], TINY, None, ALU.max))
                dve.wait_ge(chain_act, acts + 4)
                link(vec.tensor_scalar(sm[3][:, :], sm[3][:, :], CAP, 1.0, ALU.mult, ALU.min))
                link(vec.tensor_tensor(sm[6][:, :], sm[3][:, :], sm[5][:, :], ALU.mult))
                link(vec.tensor_scalar(sm[6][:, :], sm[6][:, :], 1e-7, None, ALU.max))
                dve.wait_ge(chain_act, acts + 5)
                link(vec.reciprocal(sm[8][:, :], sm[6][:, :]))
                link(vec.tensor_tensor(sm[7][:, :], sm[7][:, :], sm[8][:, :], ALU.mult))
                link(vec.tensor_tensor(sm[7][:, :], sm[7][:, :], sm[3][:, :], ALU.mult))
                link(vec.tensor_tensor(sm[4][:, :], sm[7][:, :], dxg[:, :], ALU.mult))
                link(vec.tensor_tensor(sm[5][:, :], sm[7][:, :], sm[7][:, :], ALU.mult))
                link(vec.tensor_tensor(sm[5][:, :], sm[5][:, :], n2g[:, :], ALU.mult))
                link(vec.tensor_scalar(sm[4][:, :], sm[4][:, :], 2.0, 1.0, ALU.mult, ALU.add))
                link(vec.tensor_tensor(al[:, :], sm[4][:, :], sm[5][:, :], ALU.add))
                link(vec.tensor_tensor(sm[5][:, :], sm[5][:, :], row_n2[:, :], ALU.mult))
                link(vec.tensor_tensor(sm[5][:, :], sm[5][:, :], sm[4][:, :], ALU.add))
                link(vec.tensor_scalar(sm[5][:, :], sm[5][:, :], 1e-7, None, ALU.max))
                link(vec.reciprocal(sm[5][:, :], sm[5][:, :]))
                link(vec.tensor_scalar(sm[4][:, :], row_n2[:, :], -1.0, 1.0, ALU.mult, ALU.add))
                link(vec.tensor_tensor(sm[4][:, :], sm[4][:, :], sm[7][:, :], ALU.mult))
                link(vec.tensor_tensor(be[:, :], sm[4][:, :], sm[5][:, :], ALU.mult))
                link(vec.tensor_tensor(al[:, :], al[:, :], sm[5][:, :], ALU.mult))
                nc.vector.tensor_scalar(held[:, 60 + k:61 + k], zero[:, 0:1], 1.0, None, ALU.mult).then_inc(coef_ready, 1)
                link(vec.tensor_scalar(held[:, 62 + k:63 + k], zero[:, 0:1], 1.0, None, ALU.mult))
                assert links[0] == mob_at[k] + MOB_OPS
            dve.wait_ge(n2g_done, BATCH)
            dve.wait_ge(n2a_done, BATCH)
            dve.wait_ge(dx_done, BATCH)
            dve.wait_ge(gram2_mm, 1)
            nc.vector.tensor_copy(bb_f1[:, :], bank[0][:, 0:1])
            nc.vector.tensor_copy(gram_hl[0][:, :], bank[1][:, 0:D + 1]).then_inc(gram2_done, 1)
            dve.wait_ge(gram2_done, 1)
            nc.vector.tensor_tensor(gram_hl[1][:, :], bank[1][:, 0:D + 1], gram_hl[0][:, :], ALU.subtract).then_inc(gram2_done, 2)
            mobius(0, 6)

            def step_x3(s, q):
                dve.wait_ge(xa_done, (s + 1) * G)
                need(dve, x3_done, s * G)
                need(dve, mvC, (s - 1) if isinstance(s, int) else s - 1)
                for j in range(G):
                    T = s * G + j
                    nc.vector.scalar_tensor_tensor(X3[:, bass.ds(T, 1), :], BR[:, bass.ds(T, 1), :], be[:, bass.ds(T, 1)], X3[:, bass.ds(T, 1), :], ALU.mult, ALU.add).then_inc(x3_done, 1)
                for j in range(G):
                    T = s * G + j
                    hold(x3_done, T + 1)
                    nc.vector.bn_stats(st6[q][:, j, :], X3[:, bass.ds(T, 1), :]).then_inc(stC, 1)
                for j in range(G):
                    hold(stC, s * G + j + 1)
                    nc.vector.bn_aggr(mvq[q][:, j, :], st6[q][:, j, :]).then_inc(agC, 1)
                dve.wait_ge(agC, (s + 1) * G)
                nc.vector.tensor_scalar(mv[:, bass.ds(s * G, G), :], mvq[q][:, :, :], 1.0, None, ALU.mult).then_inc(mvC, 1)
            run_steps(dve, step_x3)
            dve.wait_ge(mvC, GROUPS)
            norm_rows(11)
            dve.wait_ge(rows_ready, 2)

            def c_front(s, q):
                dve.wait_ge(cdr_in, 16 * (s + 1))
                need(dve, cu_done, s * G)
                need(dve, cn2u, (s - 1) * G)
                for j in range(G):
                    T = s * G + j
                    nc.vector.scalar_tensor_tensor(U[q][:, j:j + 1, :], X3[:, bass.ds(T, 1), :], mv[:, bass.ds(T, 1), 0], ADR[q][:, j:j + 1, D:2 * D], ALU.subtract, ALU.mult).then_inc(cu_half, 1)
                for j in range(G):
                    T = s * G + j
                    need(dve, cu_half, T + 1)
                    nc.vector.scalar_tensor_tensor(U[q][:, j, :], U[q][:, j, :], row_r[:, bass.ds(T, 1)], ADR[q][:, j, 0:D], ALU.mult, ALU.add).then_inc(cu_done, 1)
                need(dve, csu_rs, s + 1)
                nc.vector.tensor_scalar(su[q][:, :], n2u[q][:, :], CAP, 1.0, ALU.mult, ALU.min).then_inc(csu, 1)
                need(dve, csu, s + 1)
                need(dve, hdot, (s - 1) * G)
                need(dve, cT_mm, s - 1)
                nc.vector.tensor_tensor(C[q][:, :, :], U[q][:, :, :], su[q][:, :].unsqueeze(2).broadcast_to([TOK, G, D]), ALU.mult).then_inc(c_done, 1)

            def c_low(s, q):
                need(dve, cT_hi, s + 1)
                nc.vector.tensor_tensor(UHL[q][1][:, :], bank[0][:, :], UHL[q][0][:, :], ALU.subtract).then_inc(cT_lo, 1)

            def h_norm(s, q):
                need(dve, g_mm, s + 1)
                need(dve, hdot, s * G)
                for j in range(G):
                    nc.vector.tensor_tensor_reduce(out=junkV[0][:, j, :], in0=bank[1 + j // 2][:, (j % 2) * (D + 1):(j % 2) * (D + 1) + D], in1=C[q][:, j, :],
                                                   scale=1.0, scalar=0.0, op0=ALU.mult, op1=ALU.add, accum_out=hq[q][:, j:j + 1]).then_inc(hdot, 1)
                need(dve, hdot, (s + 1) * G)
                for k in range(2):
                    last = nc.vector.scalar_tensor_tensor(hq[q][:, 2 * k:2 * k + 2], bank[1 + k][:, 0:2 * (D + 1)].rearrange("p (j n) -> p j n", n=D + 1)[:, :, D], 2.0,
                                                          hq[q][:, 2 * k:2 * k + 2], ALU.mult, ALU.add)
                last.then_inc(hq2, 1)
                need(dve, hq2, s + 1)
                nc.vector.tensor_scalar(hq[q][:, :], hq[q][:, :], bb_f1[:, 0:1], TINY, ALU.add, ALU.max).then_inc(hq3, 1)

            def h_scale(s, q):
                need(dve, hrs, s + 1)
                nc.vector.tensor_scalar(sh[q][:, :], hq[q][:, :], CAP, 1.0, ALU.mult, ALU.min).then_inc(hs_done, 1)

            def ff_out(s, q):
                need(dve, hs_done, s + 1)
                need(dve, f2_mm, s + 1)
                need(dve, cga, s - 1)
                need(dve, cn2a, (s - 1) * G)
                for j in range(G):
                    nc.vector.scalar_tensor_tensor(FO[q][:, j, :], bank[3][:, j * D:(j + 1) * D], sh[q][:, j:j + 1], b_f2[:, :], ALU.mult, ALU.add).then_inc(ff_done, 1)

            def c_dot(s, q):
                need(dve, cga, s + 1)
                need(dve, cdx, s * G)
                for j in range(G):
                    T = s * G + j
                    nc.vector.scalar_tensor_tensor(junkV[1][:, j:j + 1, :], BR[:, bass.ds(T, 1), :], 1.0, X3[:, bass.ds(T, 1), :], ALU.mult, ALU.mult,
                                                   accum_out=dxg[:, bass.ds(T, 1)]).then_inc(cdx, 1)

            def step_c(s, q):
                last = isinstance(s, int) and s == GROUPS - 1
                if not last:
                    c_front(s + 1, 1 - q)
                h_norm(s, q)
                if not last:
                    c_low(s + 1, 1 - q)
                h_scale(s, q)
                if not (isinstance(s, int) and s == 0):
                    c_dot(s - 1, 1 - q)
                ff_out(s, q)
            c_front(0, 0)
            c_low(0, 0)
            run_steps(dve, step_c)
            c_dot(GROUPS - 1, 1)
            dve.wait_ge(cdx, BATCH)
            dve.wait_ge(cn2a, BATCH)
            dve.wait_ge(cn2g, BATCH)
            mobius(1, 17)

            def d_front(s, q):
                need(dve, x4_done, s * G)
                need(dve, x4T_mm, s - 1)
                need(dve, x4_copy, s - 1)
                for j in range(G):
                    T = s * G + j
                    nc.vector.scalar_tensor_tensor(X4[q][:, j:j + 1, :], X3[:, bass.ds(T, 1), :], al[:, bass.ds(T, 1)], X[:, bass.ds(T, 1), :], ALU.mult, ALU.add).then_inc(x4a, 1)
                for j in range(G):
                    T = s * G + j
                    need(dve, x4a, T + 1)
                    nc.vector.scalar_tensor_tensor(X4[q][:, j:j + 1, :], BR[:, bass.ds(T, 1), :], be[:, bass.ds(T, 1)], X4[q][:, j:j + 1, :], ALU.mult, ALU.add).then_inc(x4_done, 1)

            def d_low(s, q):
                need(dve, x4_hi, s + 1)
                nc.vector.tensor_tensor(UHL[q][1][:, :], bank[0][:, :], UHL[q][0][:, :], ALU.subtract).then_inc(x4_lo, 1)

            def logits(s, q):
                need(dve, rl_mm, s + 1)
                need(dve, dt_in, 16 * (s + 1))
                nc.vector.tensor_tensor(sg[q][:, :, :], bank[0][:, 0:G * EXPERTS].rearrange("p (g e) -> p g e", e=EXPERTS), ADT[q][:, :, :], ALU.add).then_inc(rl_done, 1)

            def route(s, q):
                vec = nc.vector
                need(dve, sig_done, s + 1)
                ops = [0]

                def rlink(instruction):
                    ops[0] += 1
                    instruction.then_inc(rchain, 1)
                    dve.wait_ge(rchain, ROUTE_OPS * s + ops[0])
                sel = rt[0][:, :, :]
                rlink(vec.tensor_tensor(sel, sg[q][:, :, :], b_router[:, :].unsqueeze(1).broadcast_to([TOK, G, EXPERTS]), ALU.add))
                full = [TOK, G, EXPERTS, EXPERTS]
                mine, other = sel.unsqueeze(3).broadcast_to(full), sel.unsqueeze(2).broadcast_to(full)
                for g in range(G):
                    last = vec.tensor_tensor(cmpb[0][:, g, :, :], other[:, g], mine[:, g], ALU.is_gt)
                rlink(last)
                for g in range(G):
                    last = vec.tensor_tensor(cmpb[1][:, g, :, :], other[:, g], mine[:, g], ALU.is_equal)
                rlink(last)
                for g in range(G):
                    last = vec.tensor_tensor(cmpb[1][:, g, :, :], cmpb[1][:, g, :, :], before[:, :, :], ALU.mult)
                rlink(last)
                rlink(vec.tensor_tensor(cmpb[0][:, :, :, :].rearrange("p g a b -> p (g a b)"), cmpb[0][:, :, :, :].rearrange("p g a b -> p (g a b)"),
                                        cmpb[1][:, :, :, :].rearrange("p g a b -> p (g a b)"), ALU.add))
                rlink(vec.tensor_reduce(rt[1][:, :, :].rearrange("p g e -> p (g e)"), cmpb[0][:, :, :, :].rearrange("p g a b -> p (g a) b"), AX.X, ALU.add))
                rlink(vec.tensor_scalar(rt[1][:, :, :], rt[1][:, :, :], float(TOP_K), None, ALU.is_lt))
                rlink(vec.tensor_tensor(rt[2][:, :, :], rt[1][:, :, :], sg[q][:, :, :], ALU.mult))
                rlink(vec.tensor_reduce(rs[0][:, :], rt[2][:, :, :], AX.X, ALU.add))
                rlink(vec.tensor_scalar(rs[1][:, :], rs[0][:, :], 1e-9, None, ALU.is_gt))
                rlink(vec.tensor_scalar(rs[0][:, :], rs[0][:, :], 1e-9, None, ALU.add))
                rlink(vec.reciprocal(rs[0][:, :], rs[0][:, :]))
                rlink(vec.scalar_tensor_tensor(rs[0][:, :], rs[0][:, :], 1.0 / (2 + TOP_K), rs[1][:, :], ALU.mult, ALU.mult))
                rlink(vec.tensor_scalar(rs[2][:, :], rs[1][:, :], -1.0 / (TOP_K * (2 + TOP_K)), 1.0 / (TOP_K * (2 + TOP_K)), ALU.mult, ALU.add))
                rlink(vec.tensor_tensor(rt[2][:, :, :], rt[2][:, :, :], rs[0][:, :].unsqueeze(2).broadcast_to([TOK, G, EXPERTS]), ALU.mult))
                rlink(vec.tensor_tensor(rt[1][:, :, :], rt[1][:, :, :], rs[2][:, :].unsqueeze(2).broadcast_to([TOK, G, EXPERTS]), ALU.mult))
                need(dve, out_done, (s - 1) * G)
                vec.tensor_tensor(gates[q][:, :, :], rt[1][:, :, :], rt[2][:, :, :], ALU.add).then_inc(gates_done, 1)
                assert ops[0] == ROUTE_OPS

            def gate_shared(s, q, k):
                need(dve, silu_done, 4 * s + k + 1)
                need(dve, up_mm, 16 * s + 2 * k + 2)
                if k == 0:
                    need(dve, rd_b, (s - 1) * G)
                nc.vector.tensor_tensor(HS[q][:, k, :], bank[4 + (2 * k + 1) % 4], S1[k % 2][:, :], ALU.mult).then_inc(hs_mul, 1)

            def combine(s, q, j):
                T = s * G + j
                acc = OUT[q][:, j:j + 1, :]
                need(dve, sd_mm, T + 1)
                need(dve, gates_done, s + 1)
                nc.vector.scalar_tensor_tensor(acc, bank[2][:, 0:D].unsqueeze(1), 1.0 / (2 * (2 + TOP_K)), X[:, bass.ds(T, 1), :], ALU.mult, ALU.add).then_inc(acc_shared, 1)
                for e in range(EXPERTS):
                    if e % 4 == 0:
                        need(dve, rd_b if e else rd_a, T + 1)
                        need(dve, acc_half if e else acc_shared, T + 1)
                    else:
                        need(dve, acc_done, 6 * T + e - e // 4)
                    last = nc.vector.scalar_tensor_tensor(acc, bank[1 if e >= 4 else 3][:, (e % 4) * D:(e % 4 + 1) * D].unsqueeze(1), gates[q][:, j, e:e + 1], acc, ALU.mult, ALU.add)
                    last.then_inc({3: acc_half, 7: out_done}.get(e, acc_done), 1)

            def step_d(s, q):
                first = isinstance(s, int) and s == 0
                last = isinstance(s, int) and s == GROUPS - 1
                for j in range(G):
                    if j == 0 and not last:
                        d_front(s + 1, 1 - q)
                    if j < 2:
                        gate_shared(s, q, 2 * j)
                        gate_shared(s, q, 2 * j + 1)
                    if not first:
                        if j == 0:
                            need(dve, out_stored[1 - q], 16 * pair[0])
                        combine(s - 1, 1 - q, j)
                    if j == 2 and not last:
                        d_low(s + 1, 1 - q)
                    if j == 3 and not last:
                        logits(s + 1, 1 - q)
                if not last:
                    route(s + 1, 1 - q)
            dve.wait_ge(wD_in, 48)
            d_front(0, 0)
            d_low(0, 0)
            logits(0, 0)
            route(0, 0)
            run_steps(dve, step_d)
            need(dve, out_stored[1], 16 * (PAIRS - 1))
            for j in range(G):
                combine(GROUPS - 1, 1, j)


def host_layout(inputs):
    import numpy as np
    t = lambda a: np.ascontiguousarray(a)
    f = np.asarray(inputs["fside_Bx1x1024x16_0"])[:, 0]
    return {
        "x": t(inputs["x"]),
        "condT": t(np.asarray(inputs["cond_1024"]).T),
        "score_w": t(inputs["L0_cond_score_w"]),
        "score_b": t(inputs["L0_cond_score_b"]),
        "w1T": t(np.asarray(inputs["L1_cond_W"]).T),
        "fc_bias": t(inputs["L1_cond_fc_bias"]),
        "fT": t(f.transpose(2, 0, 1)),
        "w_ada": t(inputs["L2_cond_w_ada"]),
        "b_ada": t(inputs["L2_cond_b_ada"]),
        "w_qkv": t(np.concatenate([np.asarray(inputs["L2_cond_w_" + n]) for n in "qkv"], axis=1)),
        "b_qkv": t(np.concatenate([np.asarray(inputs["L2_cond_b_" + n]) for n in "qkv"])),
        "w_o": t(inputs["L2_cond_w_o"]),
        "b_o": t(inputs["L2_cond_b_o"]),
        "w_f1": t(inputs["L2_cond_w_f1"]),
        "w_f1Tb": t(np.concatenate([np.asarray(inputs["L2_cond_w_f1"]).T.reshape(4, 128, D), np.asarray(inputs["L2_cond_b_f1"]).reshape(4, 128, 1)],
                                   axis=2).transpose(1, 0, 2)),
        "w_f2": t(inputs["L2_cond_w_f2"]),
        "b_f2": t(inputs["L2_cond_b_f2"]),
        "w_up": t(np.concatenate([np.asarray(inputs[n]).reshape(-1, D).T for n in ("L3_cond_s_w1", "L3_cond_s_w3", "L3_cond_r_w1")], axis=1)),
        "w_sd": t(np.asarray(inputs["L3_cond_s_w2"]).transpose(0, 2, 1).reshape(FF, D)),
        "w_rd": t(np.asarray(inputs["L3_cond_r_w2"]).transpose(0, 2, 1).reshape(EXPERTS * 128, D)),
        "b_router": t(inputs["L3_cond_router_bias"]),
        "w_routerT": t(np.asarray(inputs["L3_cond_W_router"]).T),
    }


def kernel(**inputs):
    import concourse.bacc as bacc
    from concourse.bass_utils import run_bass_kernel_spmd

    nc = bacc.Bacc("TRN2", target_bir_lowering=False, num_devices=1)
    arrays = host_layout(inputs)
    ins = {n: nc.dram_tensor(n, a.shape, mybir.dt.from_np(a.dtype), kind="ExternalInput").ap() for n, a in arrays.items()}
    out = nc.dram_tensor("out", (BATCH, TOK, D), FP32, kind="ExternalOutput").ap()
    build(nc, ins, out)
    return run_bass_kernel_spmd(nc, [arrays], core_ids=[0]).results[0]["out"]
```

```python
import math
from contextlib import ExitStack

import concourse.bass as bass
from concourse import mybir

FP32 = mybir.dt.float32
FP16 = mybir.dt.float16
ALU = mybir.AluOpType
ACT = mybir.ActivationFunctionType
AX = mybir.AxisListType

BATCH = 32
TOK = 128
D = 128
RANK = 16
HEADS, HD = 16, 8
FF = 512
EXPERTS, TOP_K = 8, 2
SHARED_CHUNKS = 4
G = 4
GROUPS = BATCH // G
PAIRS = GROUPS // 2
NG = G * TOK
ADA = 6 * D + EXPERTS

MAX_NORM = 0.9999899864196777
CAP = math.atanh(MAX_NORM)
_beta = lambda a, b: math.exp(math.lgamma(a) + math.lgamma(b) - math.lgamma(a + b))
HEAD_SCALE = _beta(HD / 2, 0.5) / _beta(D / 2, 0.5)
ROW_OPS = 26
ROUTE_OPS = 16
MOB_OPS = 22
STAT_OPS = 16
TINY = 1e-18


def build(nc, ins, out):
    ctx = ExitStack()
    with ctx:
        def sb(name, shape, dt=FP32):
            return ctx.enter_context(nc.sbuf_tensor(name + "_sb", shape, dt))

        def sem(name):
            return ctx.enter_context(nc.semaphore(name))

        X = sb("X", [TOK, BATCH, D])
        X3 = sb("X3", [TOK, BATCH, D])
        BR = sb("BR", [TOK, BATCH, D])
        ident = sb("ident", [128, 128])
        ident16 = sb("ident16", [128, 128], FP16)
        zero = sb("zero", [128, 1])
        tiny = sb("tiny", [128, 1])

        bank = [ctx.enter_context(nc.psum_tensor(f"bank{k}", [128, 512], FP32)) for k in range(4)]
        wide = ctx.enter_context(nc.psum_tensor("wide", [128, 2048], FP32))
        bank += [wide[:, 512 * k:512 * (k + 1)] for k in range(4)]

        dram_ada = nc.dram_tensor("ada_rows", (BATCH, ADA), FP32, kind="Internal").ap()

        condT = sb("condT", [D, BATCH])
        score_w = sb("score_w", [D, 1])
        score_b = sb("score_b", [128, 1])
        w1T = sb("w1T", [D, D])
        fc_bias = sb("fc_bias", [D, 1])
        w_ada = sb("w_ada", [D, 6 * D])
        b_ada = sb("b_ada", [BATCH, 6 * D])
        w_router = sb("w_router", [D, 2, EXPERTS])
        ada_sb = sb("ada_sb", [BATCH, ADA])
        bias1 = sb("bias1", [D, BATCH])
        keep = sb("keep", [TOK, BATCH])
        mv = sb("mv", [TOK, BATCH, 2])

        nsq = [sb(f"nsq{q}", [TOK, G]) for q in range(2)]
        above = [sb(f"above{q}", [TOK, G]) for q in range(2)]
        factor = [sb(f"factor{q}", [TOK, G]) for q in range(2)]
        junkA = [sb(f"junkA{q}", [TOK, G, D]) for q in range(2)]
        junkV = [sb(f"junkV{q}", [TOK, G, D]) for q in range(2)]
        early = sb("early", [128, 8 * NG])
        X1, X1T, MB, YT = [[early[:, (2 * k + q) * NG:(2 * k + q + 1) * NG].rearrange("p (g n) -> p g n", g=G) for q in range(2)] for k in range(4)]
        fT = [sb(f"fT{q}", [RANK, G, D]) for q in range(2)]
        st6 = [sb(f"st6{q}", [TOK, G, 6]) for q in range(2)]

        w_qkv = sb("w_qkv", [D, 3 * D])
        wqkv_hl = [sb(f"wqkv_{n}", [D, 3 * D], FP16) for n in ("hi", "lo")]
        w_o = sb("w_o", [D, D])
        b_qkv = sb("b_qkv", [128, 3 * D])
        b_o = sb("b_o", [128, D])
        row_r = sb("row_r", [TOK, BATCH])
        row_n2 = sb("row_n2", [TOK, BATCH])
        sm = [sb(f"sm{k}", [TOK, BATCH]) for k in range(10)]
        ADR = [sb(f"ADR{q}", [128, G, 2 * D]) for q in range(2)]
        ADG = [sb(f"ADG{q}", [128, G, D]) for q in range(2)]
        U = [sb(f"U{q}", [TOK, G, D]) for q in range(2)]
        junkU = w_ada[:, 0:NG].rearrange("p (g n) -> p g n", g=G)
        n2u = [sb(f"n2u{q}", [TOK, G]) for q in range(2)]
        su = [sb(f"su{q}", [TOK, G]) for q in range(2)]
        UHL = [[sb(f"UT{n}{q}", [D, NG], FP16) for n in ("hi", "lo")] for q in range(2)]
        big = sb("big", [128, 16 * NG])
        P = [big[:, q * 4 * NG:(q + 1) * 4 * NG].rearrange("p (i c n) -> p i c n", i=4, c=4) for q in range(2)]
        QKV = [big[:, (8 + 3 * q) * NG:(11 + 3 * q) * NG].rearrange("p (g n) -> p g n", g=G) for q in range(2)]
        OS = [big[:, (14 + q) * NG:(15 + q) * NG].rearrange("p (c n) -> p c n", c=4) for q in range(2)]
        SQ = [sb(f"SQ{q}", [TOK, 3 * D]) for q in range(2)]
        ST = [sb(f"ST{q}", [TOK, G * 51]) for q in range(2)]
        FC = [sb(f"FC{q}", [TOK, G, 48]) for q in range(2)]
        FP = [sb(f"FP{q}", [TOK, G * 3]) for q in range(2)]
        SC = [sb(f"SC{q}", [TOK, 2 * D]) for q in range(2)]
        QS = [sb(f"QS{q}", [TOK, HEADS, 4, HD], FP16) for q in range(2)]
        KS = [sb(f"KS{q}", [TOK, HEADS, 4, HD], FP16) for q in range(2)]
        V = [sb(f"V{q}", [TOK, G, HEADS, HD + 1]) for q in range(2)]
        QKT = [sb(f"QKT{q}", [128, 2, 4, TOK], FP16) for q in range(2)]
        RD = [sb(f"RD{q}", [TOK, HEADS]) for q in range(2)]
        ON = [sb(f"ON{q}", [TOK, D]) for q in range(2)]
        OT = [sb(f"OT{q}", [D, TOK]) for q in range(2)]
        AO = [sb(f"AO{q}", [TOK, D]) for q in range(2)]
        junkD, junkG, junkX = [[junkV[q][:, k, :] for q in range(2)] for k in range(3)]
        junkS = [sb(f"junkS{q}", [TOK, 2, D]) for q in range(2)]
        junkM = [junkV[q][:, 3, :] for q in range(2)]
        sbr = sb("sbr", [TOK, BATCH])
        n2a, n2g, dxg = sb("n2a", [TOK, BATCH]), sb("n2g", [TOK, BATCH]), sb("dxg", [TOK, BATCH])
        al, be = sb("al", [TOK, BATCH]), sb("be", [TOK, BATCH])
        w_f1 = sb("w_f1", [D, FF])
        wf1_hl = [sb(f"wf1_{n}", [D, FF], FP16) for n in ("hi", "lo")]
        w_f1Tb = sb("w_f1Tb", [128, 4, D + 1])
        gram_hl = [sb(f"gram_{n}", [D, D + 1], FP16) for n in ("hi", "lo")]
        bb_f1 = sb("bb_f1", [128, 1])
        w_f2 = sb("w_f2", [128, 4, D])
        b_f2 = sb("b_f2", [128, D])
        C = [sb(f"C{q}", [TOK, G, D]) for q in range(2)]
        HT = [early[:, q * 4 * NG:(q + 1) * 4 * NG].rearrange("p (k n) -> p k n", k=4) for q in range(2)]
        hq = [sb(f"hq{q}", [TOK, G]) for q in range(2)]
        sh = [sb(f"sh{q}", [TOK, G]) for q in range(2)]
        FO = [sb(f"FO{q}", [TOK, G, D]) for q in range(2)]
        UP = 4 * FF
        w_up = big[:, 0:UP]
        wup_hl = [sb(f"wup_{n}", [D, UP], FP16) for n in ("hi", "lo")]
        wr_hl = [sb(f"wr_{n}", [D, EXPERTS], FP16) for n in ("hi", "lo")]
        w_sd = sb("w_sd", [128, SHARED_CHUNKS, D])
        w_rd = sb("w_rd", [128, EXPERTS, D])
        b_router = sb("b_router", [128, EXPERTS])
        ADT = [sb(f"ADT{q}", [128, G, EXPERTS]) for q in range(2)]
        before = sb("before", [128, EXPERTS, EXPERTS])
        S1 = [junkA[q][:, :, :].rearrange("p g n -> p (g n)") for q in range(2)]
        HS = HT
        HR = [big[:, q * 8 * NG:(q + 1) * 8 * NG].rearrange("p (e n) -> p e n", e=EXPERTS) for q in range(2)]
        sg = [sb(f"sg{q}", [TOK, G, EXPERTS]) for q in range(2)]
        gates = [sb(f"gates{q}", [TOK, G, EXPERTS]) for q in range(2)]
        cmpb = [junkS[k][:, :, :].rearrange("p a (g x y) -> p (a g) x y", x=EXPERTS, y=EXPERTS) for k in range(2)]
        rt = [sb(f"rt{k}", [TOK, G, EXPERTS]) for k in range(3)]
        rs = [sb(f"rs{k}", [TOK, G]) for k in range(3)]
        OUT = FO
        X4 = C

        mvq = [sb(f"mvq{q}", [TOK, G, 2]) for q in range(2)]
        held_pool = sb("held_pool", [128, 1])
        held = sb("held", [128, 64])

        aggrA, mvA = sem("aggrA"), sem("mvA")
        wB_in, wB_split = sem("wB_in"), sem("wB_split")
        chain, chain_act = sem("chain"), sem("chain_act")
        rows_ready, bank3_clear = sem("rows_ready"), sem("bank3_clear")
        adr_in, adg_in = sem("adr_in"), sem("adg_in")
        (u_half, u_done, n2u_done, su_ln, su_rs, su_done, uT_mm, uT_hi, uT_lo, qkv_mm, qkv_done, sq_done, hsum_done, psum_done,
         st_ln, st_rs, fp_a, fac_b, scaled, v_done, hi_done, lo_done, t16_mm, t16_out, score_a, score_b2, exp_a, exp_b, av_mm, os_done,
         ot_mm, rd_done, on_done, onT_mm, onT_out, wo_mm, ao_done, ga_done, n2a_done, n2g_done, dx_done, br_done) = [sem(n) for n in (
             "u_half u_done n2u_done su_ln su_rs su_done uT_mm uT_hi uT_lo qkv_mm qkv_done sq_done hsum_done psum_done "
             "st_ln st_rs fp_a fac_b scaled v_done hi_done lo_done t16_mm t16_out score_a score_b2 exp_a exp_b av_mm os_done "
             "ot_mm rd_done on_done onT_mm onT_out wo_mm ao_done ga_done n2a_done n2g_done dx_done br_done").split()]

        wC_in, wD_in, split_high, split_low, gram2_mm, gram2_done = [sem(n) for n in "wC_in wD_in split_high split_low gram2_mm gram2_done".split()]
        coef_ready = sem("coef_ready")
        wup_in = sem("wup_in")
        x3a, x3b, x3_done = [sem(n) for n in "x3a x3b x3_done".split()]
        (cdr_in, cdg_in, cu_half, cu_done, cn2u, csu_ln, csu_rs, csu, c_done, cT_mm, cT_hi, cT_lo, f1_mm, h_out, g_mm, hdot, hq2, hq3, hln, hrs, hs_done,
         f2_mm, ff_done, cga, cn2a, cn2g, cdx) = [sem("c_" + n) for n in (
             "cdr_in cdg_in cu_half cu_done cn2u csu_ln csu_rs csu c_done cT_mm cT_hi cT_lo f1_mm h_out g_mm hdot hq2 hq3 hln hrs hs_done "
             "f2_mm ff_done cga cn2a cn2g cdx").split()]
        (dt_in, x4a, x4_done, x4_copy, x4T_mm, x4_hi, x4_lo, rl_mm, rl_done, sig_done, rchain, gates_done, up_mm, silu_done, hs_mul, gelu_done,
         sd_mm, rd_a, rd_b, acc_done, out_done, bank2_free, bank3_free, bank1_free, x4b, x4c) = [sem("d_" + n) for n in (
             "dt_in x4a x4_done x4_copy x4T_mm x4_hi x4_lo rl_mm rl_done sig_done rchain gates_done up_mm silu_done hs_mul gelu_done "
             "sd_mm rd_a rd_b acc_done out_done bank2_free bank3_free bank1_free x4b x4c").split()]
        out_stored = [sem(f"out_stored{q}") for q in range(2)]

        def need(eng, semaphore, value):
            if not (isinstance(value, int) and value <= 0):
                eng.wait_ge(semaphore, value)

        pair = [0]

        def run_steps(eng, step):
            pair[0] = 0
            step(0, 0)
            with eng.Fori(0, PAIRS - 1) as i:
                pair[0] = i
                step(2 * i + 1, 1)
                step(2 * i + 2, 0)
            pair[0] = PAIRS - 1
            step(GROUPS - 1, 1)

        def tile(s, q, r, k=0):
            group, place = s + (r - 2 + k) // G, (r - 2 + k) % G
            number = group * G + place
            if isinstance(number, int) and not 0 <= number < BATCH:
                return None
            return number, group, (q + (r - 2 + k) // G) % 2, place

        def run_slots(eng, slot):
            run_steps(eng, lambda s, q: [slot(s, q, r) for r in range(G)])
            slot(GROUPS, 0, 0)
            slot(GROUPS, 0, 1)
        consts = sem("consts")
        x_first, x_rest = sem("x_first"), sem("x_rest")
        wA_in = sem("wA_in")
        f_in = [sem(f"f_in{q}") for q in range(2)]
        ada_mm, ada_done, ada_stored = sem("ada_mm"), sem("ada_done"), sem("ada_stored")
        keep_mm, keep_lin, keep_sig, keep_done = sem("keep_mm"), sem("keep_lin"), sem("keep_sig"), sem("keep_done")
        norm_done, norm_bc, rank_done, fac_done, x1_done = sem("norm_done"), sem("norm_bc"), sem("rank_done"), sem("fac_done"), sem("x1_done")
        x1T_mm, x1T_done, gram_mm, mb_done, y_mm, yT_done, yT_mm, x2_done, statA = (
            sem("x1T_mm"), sem("x1T_done"), sem("gram_mm"), sem("mb_done"), sem("y_mm"), sem("yT_done"), sem("yT_mm"), sem("x2_done"), sem("statA"))
        stored = sem("stored")
        block = ctx.enter_context(nc.Block())

        x_v = ins["x"].rearrange("b t d -> t b d")
        out_v = out.rearrange("b t d -> t b d")
        f_v = ins["fT"]

        def row(name, parts):
            return ins[name].rearrange("(a n) -> a n", a=1).broadcast_to([parts, ins[name].shape[0]])

        WA = 10
        mob_at = [ROW_OPS - 1, 2 * (ROW_OPS - 1) + MOB_OPS + STAT_OPS]
        NORM2_AT = ROW_OPS - 1 + MOB_OPS + STAT_OPS

        @block.sync
        def _(sp):
            sp.dma_start(X[:, 0:2 * G, :], x_v[:, 0:2 * G, :]).then_inc(x_first, 16)
            sp.dma_start(condT[:, :], ins["condT"]).then_inc(wA_in, 16)
            sp.dma_start(score_w[:, :], ins["score_w"]).then_inc(wA_in, 16)
            sp.dma_start(score_b[:, :], row("score_b", 128)).then_inc(wA_in, 16)
            sp.dma_start(w1T[:, :], ins["w1T"]).then_inc(wA_in, 16)
            sp.dma_start(fc_bias[:, :], ins["fc_bias"].rearrange("(p a) -> p a", a=1)).then_inc(wA_in, 16)
            for q in range(2):
                sp.dma_start(fT[q][:, :, :], f_v[:, q * G:(q + 1) * G, :]).then_inc(f_in[q], 16)
            sp.dma_start(w_ada[:, :], ins["w_ada"]).then_inc(wA_in, 16)
            sp.dma_start(b_ada[:, :], row("b_ada", BATCH)).then_inc(wA_in, 16)
            sp.dma_start(w_router[:, 0, :], ins["w_routerT"][0:D, :]).then_inc(wA_in, 16)
            sp.dma_start(w_router[:, 1, :], ins["w_routerT"][D:2 * D, :]).then_inc(wA_in, 16)
            for c in range(1, PAIRS):
                sp.dma_start(X[:, 2 * G * c:2 * G * (c + 1), :], x_v[:, 2 * G * c:2 * G * (c + 1), :]).then_inc(x_rest, 16)
            sp.wait_ge(ada_done, 3)
            sp.dma_start(dram_ada, ada_sb[:, :]).then_inc(ada_stored, 16)
            with sp.Fori(0, PAIRS - 1) as i:
                for q in range(2):
                    sp.wait_ge(gram_mm, 2 * i + q + 1)
                    sp.dma_start(fT[q][:, :, :], f_v[:, bass.ds(2 * G * i + (2 + q) * G, G), :]).then_inc(f_in[q], 16)
            sp.dma_start(w_qkv[:, :], ins["w_qkv"]).then_inc(wB_in, 16)
            sp.dma_start(w_o[:, :], ins["w_o"]).then_inc(wB_in, 16)
            sp.dma_start(b_qkv[:, :], row("b_qkv", 128)).then_inc(wB_in, 16)
            sp.dma_start(b_o[:, :], row("b_o", 128)).then_inc(wB_in, 16)
            sp.dma_start(w_f1[:, :], ins["w_f1"]).then_inc(wC_in, 16)
            sp.dma_start(w_f1Tb[:, :, :], ins["w_f1Tb"]).then_inc(wC_in, 16)
            sp.dma_start(w_f2[:, :, :], ins["w_f2"].rearrange("(k p) n -> p k n", p=128)).then_inc(wC_in, 16)
            sp.dma_start(b_f2[:, :], row("b_f2", 128)).then_inc(wC_in, 16)
            sp.dma_start(w_sd[:, :, :], ins["w_sd"].rearrange("(k p) n -> p k n", p=128)).then_inc(wD_in, 16)
            sp.dma_start(w_rd[:, :, :], ins["w_rd"].rearrange("(k p) n -> p k n", p=128)).then_inc(wD_in, 16)
            sp.dma_start(b_router[:, :], row("b_router", 128)).then_inc(wD_in, 16)
            sp.wait_ge(ada_stored, 16)
            ada_v = dram_ada.rearrange("b n -> () b n")

            def load_rows(s, q):
                sp.dma_start(ADR[q][:, :, :], ada_v[:, bass.ds(s * G, G), 0:2 * D].broadcast_to([128, G, 2 * D])).then_inc(adr_in, 16)

            def load_gates(s, q):
                sp.dma_start(ADG[q][:, :, :], ada_v[:, bass.ds(s * G, G), 2 * D:3 * D].broadcast_to([128, G, D])).then_inc(adg_in, 16)
            load_rows(0, 0)
            load_gates(0, 0)

            def step_b(s, q):
                if isinstance(s, int) and s == GROUPS - 1:
                    return
                need(sp, u_done, s * G)
                sp.wait_ge(adr_in, 16 * (s + 1))
                load_rows(s + 1, 1 - q)
                need(sp, ga_done, s * G + 2 if not (isinstance(s, int) and s == 0) else 0)
                sp.wait_ge(adg_in, 16 * (s + 1))
                load_gates(s + 1, 1 - q)
            run_steps(sp, step_b)
            sp.wait_ge(os_done, BATCH)
            sp.wait_ge(v_done, BATCH)
            sp.wait_ge(scaled, BATCH)
            sp.wait_ge(ot_mm, BATCH)
            sp.dma_start(w_up[:, :], ins["w_up"]).then_inc(wup_in, 16)

            def load_c(s, q):
                sp.dma_start(ADR[q][:, :, :], ada_v[:, bass.ds(s * G, G), 3 * D:5 * D].broadcast_to([128, G, 2 * D])).then_inc(cdr_in, 16)

            def load_cg(s, q):
                sp.dma_start(ADG[q][:, :, :], ada_v[:, bass.ds(s * G, G), 5 * D:6 * D].broadcast_to([128, G, D])).then_inc(cdg_in, 16)
            sp.wait_ge(u_done, BATCH)
            load_c(0, 0)
            sp.wait_ge(ga_done, BATCH + 2)
            load_cg(0, 0)

            def step_c(s, q):
                if isinstance(s, int) and s == GROUPS - 1:
                    return
                need(sp, cu_done, s * G)
                sp.wait_ge(cdr_in, 16 * (s + 1))
                load_c(s + 1, 1 - q)
                need(sp, cga, s)
                sp.wait_ge(cdg_in, 16 * (s + 1))
                load_cg(s + 1, 1 - q)
            run_steps(sp, step_c)

            def load_t(s, q):
                sp.dma_start(ADT[q][:, :, :], ada_v[:, bass.ds(s * G, G), 6 * D:ADA].broadcast_to([128, G, EXPERTS])).then_inc(dt_in, 16)
            load_t(0, 0)

            def store(s, q):
                sp.wait_ge(out_done, (s + 1) * G)
                sp.dma_start(out_v[:, bass.ds(s * G, G), :], OUT[q][:, :, :]).then_inc(out_stored[q], 16)

            def step_d(s, q):
                last = isinstance(s, int) and s == GROUPS - 1
                if not last:
                    need(sp, rl_done, s)
                    sp.wait_ge(dt_in, 16 * (s + 1))
                    load_t(s + 1, 1 - q)
                if not (isinstance(s, int) and s == 0):
                    store(s - 1, 1 - q)
            run_steps(sp, step_d)
            store(GROUPS - 1, 1)
            for q in range(2):
                sp.wait_ge(out_stored[q], 16 * PAIRS + 16)

        @block.gpsimd
        def _(pool):
            pool.memset(ident[:, :], 0.0).then_inc(consts, 1)
            pool.memset(ident16[:, :], 0.0).then_inc(consts, 1)
            pool.memset(tiny[:, :], TINY)
            pool.memset(zero[:, :], 0.0).then_inc(consts, 1)
            pool.wait_ge(consts, 3)
            for m in (ident, ident16):
                pool.affine_select(out=m[:, :], in_=m[:, :], compare_op=ALU.not_equal, fill=1.0, base=0,
                                   pattern=[[-1, 128]], channel_multiplier=1).then_inc(consts, 1)
            def phase_a(i):
                for q in range(2):
                    s = 2 * i + q
                    pool.wait_ge(fac_done, s + 1)
                    need(pool, x2_done, 2 * i)
                    pool.tensor_tensor(X1[q][:, :, :], X[:, bass.ds(s * G, G), :],
                                       factor[q][:, :].unsqueeze(2).broadcast_to([TOK, G, D]), ALU.mult).then_inc(x1_done, 1)
            for q in range(2):
                pool.memset(AO[q][:, :], 0.0).then_inc(ga_done, 1)
                pool.memset(QS[q][:, :, :, :], 0.0)
                pool.memset(KS[q][:, :, :, :], 0.0)
                pool.memset(V[q][:, :, :, HD:HD + 1], HEAD_SCALE).then_inc(consts, 1)
            pool.memset(before[:, :, :], 1.0).then_inc(consts, 1)
            pool.wait_ge(consts, 8)
            pool.affine_select(out=before[:, :, :], in_=before[:, :, :], compare_op=ALU.is_gt, fill=0.0, base=0,
                               pattern=[[1, EXPERTS], [-1, EXPERTS]], channel_multiplier=0).then_inc(consts, 1)
            phase_a(0)
            with pool.Fori(1, PAIRS) as i:
                phase_a(i)
            pool.wait_ge(wB_in, 64)
            pool.tensor_copy(wqkv_hl[0][:, :], w_qkv[:, :]).then_inc(wB_split, 1)
            pool.wait_ge(wB_split, 1)
            pool.tensor_tensor(wqkv_hl[1][:, :], w_qkv[:, :], wqkv_hl[0][:, :], ALU.subtract).then_inc(wB_split, 1)

            def split(hl, w, count):
                pool.tensor_copy(hl[0], w).then_inc(split_high, 1)
                pool.wait_ge(split_high, count)
                pool.tensor_tensor(hl[1], w, hl[0], ALU.subtract).then_inc(split_low, 1)
            pool.wait_ge(wC_in, 64)
            split([h[:, :] for h in wf1_hl], w_f1[:, :], 1)
            split([h[:, :] for h in wr_hl], w_router[:, 0, :], 2)


            def v_scale(T, s, q, j):
                need(pool, fac_b, s + 1)
                need(pool, av_mm, T - 2)
                pool.tensor_tensor(V[q][:, j, :, 0:HD], QKV[q][:, j, 2 * D:3 * D].rearrange("p (h d) -> p h d", d=HD),
                                   FC[q][:, j, 32:48].unsqueeze(2).broadcast_to([TOK, HEADS, HD]), ALU.mult).then_inc(v_done, 1)

            def gate(T, s, q, j):
                need(pool, ao_done, T + 1)
                if j == 0:
                    need(pool, adg_in, 4 * T + 16)
                pool.tensor_tensor(BR[:, bass.ds(T, 1), :], AO[j % 2][:, :].unsqueeze(1), ADG[q][:, j:j + 1, :], ALU.mult).then_inc(ga_done, 1)

            def slot(s, q, r):
                ahead, behind = tile(s, q, r, 1), tile(s, q, r, -2)
                if ahead:
                    v_scale(*ahead)
                if behind:
                    gate(*behind)
            run_slots(pool, slot)
            gate(BATCH - 2, GROUPS - 1, 1, 2)
            gate(BATCH - 1, GROUPS - 1, 1, 3)

            pool.wait_ge(wup_in, 16)
            for k in range(4):
                part = slice(k * FF, (k + 1) * FF)
                split([h[:, part] for h in wup_hl], w_up[:, part], 3 + k)

            def pool_hold(semaphore, value):
                need(pool, semaphore, value)
                pool.tensor_tensor(held_pool[:, :], zero[:, :], zero[:, :], ALU.add)

            def per_row(t, rows):
                return t[:, rows].unsqueeze(2).broadcast_to([TOK, G, D])

            def sum3(s):
                rows = bass.ds(s * G, G)
                pool.tensor_tensor(X3[:, rows, :], X[:, rows, :], per_row(al, rows), ALU.mult).then_inc(x3a, 1)
                pool.tensor_tensor(BR[:, rows, :], BR[:, rows, :], per_row(be, rows), ALU.mult).then_inc(x3b, 1)
                need(pool, x3a, s + 1)
                pool_hold(x3b, s + 1)
                pool.tensor_tensor(X3[:, rows, :], X3[:, rows, :], BR[:, rows, :], ALU.add).then_inc(x3_done, 1)

            def gate_c(s, q):
                pool.wait_ge(ff_done, (s + 1) * G)
                pool.wait_ge(cdg_in, 16 * s + 16)
                pool.tensor_tensor(BR[:, bass.ds(s * G, G), :], FO[q][:, :, :], ADG[q][:, :, :], ALU.mult).then_inc(cga, 1)

            def step_c(s, q):
                if not (isinstance(s, int) and s == GROUPS - 1):
                    sum3(s + 1)
                if not (isinstance(s, int) and s == 0):
                    gate_c(s - 1, 1 - q)
            pool.wait_ge(coef_ready, 1)
            sum3(0)
            run_steps(pool, step_c)
            gate_c(GROUPS - 1, 1)
            def step_d(s, q):
                rows = bass.ds(s * G, G)
                need(pool, x4T_mm, s)
                need(pool, x4_copy, s)
                pool.tensor_tensor(X4[q][:, :, :], X3[:, rows, :], per_row(al, rows), ALU.mult).then_inc(x4a, 1)
                pool.tensor_tensor(BR[:, rows, :], BR[:, rows, :], per_row(be, rows), ALU.mult).then_inc(x4b, 1)
                pool_hold(x4a, s + 1)
                pool.tensor_tensor(X4[q][:, :, :], X4[q][:, :, :], X[:, rows, :], ALU.add).then_inc(x4c, 1)
                need(pool, x4b, s + 1)
                pool_hold(x4c, s + 1)
                pool.tensor_tensor(X4[q][:, :, :], X4[q][:, :, :], BR[:, rows, :], ALU.add).then_inc(x4_done, 1)
            pool.wait_ge(coef_ready, 2)
            run_steps(pool, step_d)

        @block.scalar
        def _(act):
            act.wait_ge(consts, 5)
            act.wait_ge(keep_lin, 1)
            act.activation(keep[:, :], keep[:, :], ACT.Sigmoid, bias=zero[:, 0:1]).then_inc(keep_sig, 1)
            act.preload_act_table_set("gelu_and_others")

            def phase_a(i):
                need(act, rank_done, 2 * i)
                need(act, norm_done, 8 * i)
                for q in range(2):
                    for j in range(G):
                        act.activation(junkA[q][:, j, :], X[:, bass.ds((2 * i + q) * G + j, 1), :], ACT.Square,
                                       accum_out=nsq[q][:, j:j + 1]).then_inc(norm_done, 1)
                for q in range(2):
                    act.wait_ge(x1T_mm, 2 * i + q + 1)
                    act.activation(X1T[q][:, :, :], bank[2 + q][:, :], ACT.Copy).then_inc(x1T_done, 1)
                for q in range(2):
                    act.wait_ge(y_mm, 2 * i + q + 1)
                    need(act, yT_mm, 2 * i)
                    for j in range(G):
                        act.activation(YT[q][:, j, :], bank[6 + q][:, j * TOK:(j + 1) * TOK], ACT.Gelu,
                                       bias=bias1[:, bass.ds((2 * i + q) * G + j, 1)]).then_inc(yT_done, 1)
            act.wait_ge(ada_done, 1)
            act.wait_ge(x_first, 16)
            phase_a(0)
            act.wait_ge(x_rest, 16 * (PAIRS - 1))
            with act.Fori(1, PAIRS) as i:
                phase_a(i)
            act.preload_act_table_set("natural_log_exp_and_others")

            def small(out_, in_, func, at, **more):
                act.wait_ge(chain, at)
                act.activation(out_[:, :], in_[:, :], func, **more).then_inc(chain_act, 1)

            def norm_rows(at):
                small(sm[1], sm[0], ACT.Ln, at + 4)
                act.wait_ge(chain_act, at_act[0] + 1)
                act.activation(sm[2][:, :], sm[1][:, :], ACT.Exp, scale=0.5, bias=zero[:, 0:1]).then_inc(chain_act, 1)
                act.activation(sm[3][:, :], sm[1][:, :], ACT.Exp, scale=-0.5, bias=zero[:, 0:1]).then_inc(chain_act, 1)
                small(sm[5], sm[4], ACT.Ln, at + 5, bias=1.0)
                act.activation(sm[6][:, :], sm[4][:, :], ACT.Ln, scale=-1.0, bias=1.0).then_inc(chain_act, 1)
                small(sm[8], sm[7], ACT.Ln, at + ROW_OPS - 1)
                act.wait_ge(chain_act, at_act[0] + 6)
                act.activation(row_r[:, :], sm[8][:, :], ACT.Exp, scale=-0.5, bias=zero[:, 0:1]).then_inc(rows_ready, 1)
                at_act[0] += 6
            at_act = [0]
            norm_rows(0)

            def act_mobius(k):
                small(sm[2], sm[0], ACT.Ln, mob_at[k] + 2)
                act.activation(sm[4][:, :], sm[1][:, :], ACT.Ln).then_inc(chain_act, 1)
                act.wait_ge(chain_act, at_act[0] + 2)
                act.activation(sm[3][:, :], sm[2][:, :], ACT.Exp, scale=-0.5).then_inc(chain_act, 1)
                act.activation(sm[5][:, :], sm[4][:, :], ACT.Exp, scale=0.5).then_inc(chain_act, 1)
                small(sm[7], sm[6], ACT.Tanh, mob_at[k] + 5)
                at_act[0] += 5
                act.wait_ge(coef_ready, k + 1)

            def front_norm(s, q):
                need(act, u_done, (s + 1) * G)
                need(act, n2u_done, s * G)
                for j in range(G):
                    act.activation(junkU[:, j, :], U[q][:, j, :], ACT.Square, accum_out=n2u[q][:, j:j + 1]).then_inc(n2u_done, 1)
                need(act, n2u_done, (s + 1) * G)
                act.activation(n2u[q][:, :], n2u[q][:, :], ACT.Ln, bias=tiny[:, 0:1]).then_inc(su_ln, 1)
                need(act, su_ln, s + 1)
                act.activation(n2u[q][:, :], n2u[q][:, :], ACT.Exp, scale=-0.5).then_inc(su_rs, 1)

            def front_high(s, q):
                need(act, uT_mm, s + 1)
                act.activation(UHL[q][0][:, :], bank[0][:, :], ACT.Copy).then_inc(uT_hi, 1)

            def squares(T, q, j):
                need(act, qkv_done, T + 1)
                need(act, hsum_done, T - 1)
                act.activation(SQ[j % 2][:, :], QKV[q][:, j, :], ACT.Square).then_inc(sq_done, 1)

            def stats(s, q):
                need(act, psum_done, s + 1)
                act.activation(ST[q][:, :], ST[q][:, :], ACT.Ln, bias=tiny[:, 0:1]).then_inc(st_ln, 1)
                need(act, st_ln, s + 1)
                act.activation(ST[q][:, :], ST[q][:, :], ACT.Exp, scale=-0.5).then_inc(st_rs, 1)

            def high_parts(T, j):
                need(act, scaled, T + 1)
                need(act, t16_mm, T - 1)
                sc = SC[j % 2][:, :].rearrange("p (a h d) -> p a h d", a=2, d=HD)
                act.activation(QS[j % 2][:, :, 0:3:2, :], sc[:, 0, :, :].unsqueeze(2).broadcast_to([TOK, HEADS, 2, HD]), ACT.Copy).then_inc(hi_done, 1)
                act.activation(KS[j % 2][:, :, 0:2, :], sc[:, 1, :, :].unsqueeze(2).broadcast_to([TOK, HEADS, 2, HD]), ACT.Copy).then_inc(hi_done, 1)

            def qk_out(T, j):
                need(act, t16_mm, T + 1)
                need(act, score_b2, T - 1)
                act.activation(QKT[j % 2][:, :, :, :].rearrange("p a c n -> p (a c n)"), bank[2][:, :].bitcast(FP16), ACT.Copy).then_inc(t16_out, 1)

            def exps(T, j, half):
                need(act, score_b2 if half else score_a, T + 1)
                need(act, av_mm, T - 1)
                act.activation(P[j % 2][:, 2 * half:2 * half + 2, :, :].rearrange("p i c n -> p (i c n)"), wide[:, 1024 * half:1024 * half + 1024],
                               ACT.Exp, scale=HD ** -0.5).then_inc(exp_b if half else exp_a, 1)

            def o_out(T, j):
                need(act, av_mm, T + 1)
                need(act, ot_mm, T)
                act.activation(OS[j % 2][:, :, :].rearrange("p c n -> p (c n)"), bank[3][:, :], ACT.Copy).then_inc(os_done, 1)

            def on_out(T, j):
                need(act, onT_mm, T + 1)
                need(act, wo_mm, T)
                act.activation(OT[j % 2][:, :], bank[1][:, 0:TOK], ACT.Copy).then_inc(onT_out, 1)

            def norms(T, j):
                need(act, exp_a, T + 3 if not isinstance(T, int) else min(T + 3, BATCH))
                need(act, ga_done, T + 3)
                act.activation(junkS[j % 2][:, 1:2, :], BR[:, bass.ds(T, 1), :], ACT.Square, accum_out=n2g[:, bass.ds(T, 1)]).then_inc(n2g_done, 1)

            def slot(s, q, r):
                now, after, back, before = tile(s, q, r), tile(s, q, r, 2), tile(s, q, r, -1), tile(s, q, r, -2)
                have = not (isinstance(s, int) and s in (0, GROUPS))
                front = not (isinstance(s, int) and s >= GROUPS - 1)
                F = (s + 1) * G
                if isinstance(s, int) and s == 0 and r < 2:
                    after = None
                if now:
                    exps(now[0], now[3], 0)
                if front and r == 1:
                    front_norm(s + 1, 1 - q)
                if r == 0 and have:
                    stats(s, q)
                if front and r == 3:
                    squares(F, 1 - q, 0)
                if after and r > 0:
                    high_parts(after[0], after[3])
                if back:
                    o_out(back[0], back[3])
                if after and r == 0:
                    high_parts(after[0], after[3])
                if now:
                    exps(now[0], now[3], 1)
                if front and r == 3:
                    squares(F + 1, 1 - q, 1)
                if before:
                    norms(before[0], before[3])
                if after:
                    qk_out(after[0], after[3])
                if back:
                    on_out(back[0], back[3])
                if front:
                    if r == 1:
                        front_high(s + 1, 1 - q)
                    elif r == 3:
                        squares(F + 2, 1 - q, 2)
                        squares(F + 3, 1 - q, 3)
            front_norm(0, 0)
            front_high(0, 0)
            for j in range(G):
                squares(j, 0, j)
            stats(0, 0)
            for j in range(2):
                high_parts(j, j)
                qk_out(j, j)
            run_slots(act, slot)
            o_out(BATCH - 1, 3)
            on_out(BATCH - 1, 3)
            for T in (BATCH - 2, BATCH - 1):
                norms(T, T % G)

            act_mobius(0)
            act.preload_act_table_set("natural_log_exp_and_others")

            norm_rows(NORM2_AT)

            def c_front_norm(s, q):
                need(act, cu_done, (s + 1) * G)
                need(act, cn2u, s * G)
                for j in range(G):
                    act.activation(junkU[:, j, :], U[q][:, j, :], ACT.Square, accum_out=n2u[q][:, j:j + 1]).then_inc(cn2u, 1)
                need(act, cn2u, (s + 1) * G)
                act.activation(n2u[q][:, :], n2u[q][:, :], ACT.Ln, bias=tiny[:, 0:1]).then_inc(csu_ln, 1)
                need(act, csu_ln, s + 1)
                act.activation(n2u[q][:, :], n2u[q][:, :], ACT.Exp, scale=-0.5).then_inc(csu_rs, 1)

            def c_front_high(s, q):
                need(act, cT_mm, s + 1)
                act.activation(UHL[q][0][:, :], bank[0][:, :], ACT.Copy).then_inc(cT_hi, 1)

            def h_evacuate(s, q, k):
                need(act, f1_mm, 4 * s + k + 1)
                act.activation(HT[q][:, k, :], bank[4 + k], ACT.Identity, bias=w_f1Tb[:, k, D:D + 1]).then_inc(h_out, 1)

            def h_norm(s, q):
                need(act, hq3, s + 1)
                act.activation(hq[q][:, :], hq[q][:, :], ACT.Ln).then_inc(hln, 1)
                need(act, hln, s + 1)
                act.activation(hq[q][:, :], hq[q][:, :], ACT.Exp, scale=-0.5).then_inc(hrs, 1)

            def c_norms(s, q):
                if isinstance(s, int) and s == GROUPS - 1:
                    act.wait_ge(cn2g, s * G)
                else:
                    act.wait_ge(h_out, 4 * s + 5)
                need(act, ff_done, (s + 1) * G)
                for j in range(G):
                    T = s * G + j
                    act.activation(junkA[1][:, j, :], FO[q][:, j, :], ACT.Square, accum_out=n2a[:, bass.ds(T, 1)]).then_inc(cn2a, 1)
                need(act, cga, s + 1)
                for j in range(G):
                    T = s * G + j
                    act.activation(junkA[0][:, j:j + 1, :], BR[:, bass.ds(T, 1), :], ACT.Square, accum_out=n2g[:, bass.ds(T, 1)]).then_inc(cn2g, 1)

            def step_c(s, q):
                last = isinstance(s, int) and s == GROUPS - 1
                for k in range(4):
                    h_evacuate(s, q, k)
                if not last:
                    c_front_norm(s + 1, 1 - q)
                h_norm(s, q)
                if not last:
                    c_front_high(s + 1, 1 - q)
                if not (isinstance(s, int) and s == 0):
                    c_norms(s - 1, 1 - q)
            c_front_norm(0, 0)
            c_front_high(0, 0)
            run_steps(act, step_c)
            c_norms(GROUPS - 1, 1)
            act_mobius(1)

            def d_front(s, q):
                need(act, x4T_mm, s + 1)
                act.activation(UHL[q][0][:, :], bank[0][:, :], ACT.Copy).then_inc(x4_hi, 1)
                need(act, x4_done, s + 1)
                act.activation(X[:, bass.ds(s * G, G), :], X4[q][:, :, :], ACT.Copy).then_inc(x4_copy, 1)

            def d_router(s, q):
                need(act, rl_done, s + 1)
                act.activation(sg[q][:, :, :], sg[q][:, :, :], ACT.Sigmoid).then_inc(sig_done, 1)

            def step_d(s, q):
                last = isinstance(s, int) and s == GROUPS - 1
                for k in range(SHARED_CHUNKS):
                    need(act, up_mm, 16 * s + 2 * k + 1)
                    need(act, hs_mul, 4 * s + k - 1)
                    act.activation(S1[k % 2][:, :], bank[4 + (2 * k) % 4], ACT.Silu).then_inc(silu_done, 1)
                for e in range(EXPERTS):
                    need(act, up_mm, 16 * s + 8 + e + 1)
                    if e == 0:
                        need(act, rd_b, s * G - 3)
                    act.activation(HR[q][:, e, :], bank[4 + e % 4], ACT.Gelu).then_inc(gelu_done, 1)
                    if e == 1 and not last:
                        d_front(s + 1, 1 - q)
                if not last:
                    d_router(s + 1, 1 - q)
            d_front(0, 0)
            d_router(0, 0)
            run_steps(act, step_d)

        @block.tensor
        def _(pe):
            mm = nc.tensor.matmul
            pe.wait_ge(wA_in, 16 * (WA - 1))
            mm(bank[0][:, 0:BATCH], score_w[:, 0:1].to_broadcast([D, 128]), condT[:, :], start=True, stop=True).then_inc(keep_mm, 1)
            mm(bank[4][0:BATCH, :], condT[:, :], w_ada[:, 0:512], start=True, stop=True)
            mm(bank[5][0:BATCH, 0:256], condT[:, :], w_ada[:, 512:768], start=True, stop=True)
            mm(bank[5][0:BATCH, 256:256 + EXPERTS], condT[:, :], w_router[:, 1, :], start=True, stop=True).then_inc(ada_mm, 1)
            pe.wait_ge(consts, 5)
            pe.wait_ge(ada_done, 3)
            pe.wait_ge(keep_lin, 1)

            def phase_a(i):
                for q in range(2):
                    pe.wait_ge(norm_done, 8 * i + 4 * q + 4)
                    need(pe, x2_done, 2 * i)
                    for j in range(G):
                        last = nc.tensor.transpose(bank[q][:, j * TOK:(j + 1) * TOK], nsq[q][:, j:j + 1].to_broadcast([TOK, TOK]), ident[:, :])
                    last.then_inc(norm_bc, 1)
                for q in range(2):
                    pe.wait_ge(f_in[q], 16 * i + 16)
                    need(pe, mb_done, 2 * i)
                    for j in range(G):
                        last = mm(bank[4 + q][:, j * D:(j + 1) * D], fT[q][:, j, :], fT[q][:, j, :], start=True, stop=True)
                    last.then_inc(gram_mm, 1)
                for q in range(2):
                    pe.wait_ge(x1_done, 2 * i + q + 1)
                    need(pe, x1T_done, 2 * i)
                    for j in range(G):
                        last = nc.tensor.transpose(bank[2 + q][:, j * TOK:(j + 1) * TOK], X1[q][:, j, :], ident[:, :])
                    last.then_inc(x1T_mm, 1)
                for q in range(2):
                    pe.wait_ge(mb_done, 2 * i + q + 1)
                    pe.wait_ge(x1T_done, 2 * i + q + 1)
                    need(pe, yT_done, 8 * i)
                    for j in range(G):
                        last = mm(bank[6 + q][:, j * TOK:(j + 1) * TOK], MB[q][:, j, :], X1T[q][:, j, :], start=True, stop=True)
                    last.then_inc(y_mm, 1)
                for q in range(2):
                    pe.wait_ge(yT_done, 8 * i + 4 * q + 4)
                    pe.wait_ge(rank_done, 2 * i + q + 1)
                    for j in range(G):
                        last = nc.tensor.transpose(bank[q][:, j * TOK:(j + 1) * TOK], YT[q][:, j, :], ident[:, :])
                    last.then_inc(yT_mm, 1)
            phase_a(0)
            with pe.Fori(1, PAIRS) as i:
                phase_a(i)
            pe.wait_ge(wC_in, 64)
            pe.wait_ge(x2_done, GROUPS)
            for k in range(4):
                mm(bank[1][:, 0:D + 1], w_f1Tb[:, k, 0:D], w_f1Tb[:, k, :], start=k == 0, stop=k == 3)
            for k in range(4):
                last = mm(bank[0][:, 0:1], w_f1Tb[:, k, D:D + 1].to_broadcast([128, 128]), w_f1Tb[:, k, D:D + 1], start=k == 0, stop=k == 3)
            last.then_inc(gram2_mm, 1)
            pe.wait_ge(gram2_done, 3)
            pe.wait_ge(wB_split, 2)
            pe.wait_ge(bank3_clear, 1)

            def product(out_, left, right, start=True, stop=True):
                mm(out_, left[0], right[0], start=start, stop=False)
                mm(out_, left[0], right[1], start=False, stop=False)
                return mm(out_, left[1], right[0], start=False, stop=stop)

            def u_transpose(s, q):
                need(pe, u_done, (s + 1) * G)
                need(pe, qkv_done, s * G)
                for j in range(G):
                    last = nc.tensor.transpose(bank[0][:, j * TOK:(j + 1) * TOK], U[q][:, j, :], ident[:, :])
                last.then_inc(uT_mm, 1)

            def qkv(T, s, q, j):
                need(pe, uT_lo, s + 1)
                need(pe, qkv_done, T)
                part = slice(j * TOK, (j + 1) * TOK)
                product(bank[0][:, 0:3 * D], [h[:, part] for h in UHL[q]], [w[:, :] for w in wqkv_hl]).then_inc(qkv_mm, 1)

            def qk_transpose(T, j):
                need(pe, lo_done, T + 1)
                need(pe, t16_out, T)
                b16 = bank[2][:, :].bitcast(FP16)
                for a, src in enumerate((QS, KS)):
                    flat = src[j % 2][:, :, :, :].rearrange("p h s d -> p (h s d)")
                    for c in range(4):
                        last = nc.tensor.transpose(b16[:, (4 * a + c) * TOK:(4 * a + c + 1) * TOK], flat[:, c * 128:(c + 1) * 128], ident16[:, :])
                last.then_inc(t16_mm, 1)

            def scores(T, j, half):
                need(pe, t16_out, T + 1)
                need(pe, exp_b if half else exp_a, T)
                t = QKT[j % 2]
                for c in range(4):
                    for i in (2 * half, 2 * half + 1):
                        r = slice(32 * i, 32 * i + 32)
                        last = mm(bank[4 + i][:, c * TOK:(c + 1) * TOK], t[r, 1, c, :], t[r, 0, c, :], start=True, stop=True)
                last.then_inc(score_b2 if half else score_a, 1)

            def attend(T, q, j):
                need(pe, exp_b, T + 1)
                need(pe, v_done, T + 1)
                need(pe, os_done, T)
                for c in range(4):
                    for i in range(4):
                        last = mm(bank[3][32 * i:32 * i + HD + 1, c * TOK:(c + 1) * TOK], V[q][:, j, 4 * c + i, :], P[j % 2][:, i, c, :], start=True, stop=True)
                last.then_inc(av_mm, 1)

            def o_transpose(T, j):
                need(pe, os_done, T + 1)
                need(pe, ao_done, T)
                for c in range(4):
                    last = nc.tensor.transpose(bank[1][:, c * 128:(c + 1) * 128], OS[j % 2][:, c, :], ident[:, :])
                last.then_inc(ot_mm, 1)

            def on_transpose(T, j):
                need(pe, on_done, T + 1)
                nc.tensor.transpose(bank[1][:, 0:TOK], ON[j % 2][:, :], ident[:, :]).then_inc(onT_mm, 1)

            def project(T, j):
                need(pe, onT_out, T + 1)
                mm(bank[1][:, TOK:2 * TOK], OT[j % 2][:, :], w_o[:, :], start=True, stop=True).then_inc(wo_mm, 1)

            def slot(s, q, r):
                now, nxt, after, back = tile(s, q, r), tile(s, q, r, 1), tile(s, q, r, 2), tile(s, q, r, -1)
                front = not (isinstance(s, int) and s >= GROUPS - 1)
                first = isinstance(s, int) and s == 0 and r < 2
                F = (s + 1) * G
                if nxt and not first:
                    scores(nxt[0], nxt[3], 0)
                if front:
                    if r == 1:
                        u_transpose(s + 1, 1 - q)
                    elif r > 1:
                        qkv(F + 2 * r - 4, s + 1, 1 - q, 2 * r - 4)
                if back:
                    o_transpose(back[0], back[3])
                if after and not first:
                    qk_transpose(after[0], after[3])
                if nxt and not first:
                    scores(nxt[0], nxt[3], 1)
                if front and r > 1:
                    qkv(F + 2 * r - 3, s + 1, 1 - q, 2 * r - 3)
                if back:
                    on_transpose(back[0], back[3])
                if now:
                    attend(now[0], now[2], now[3])
                if back:
                    project(back[0], back[3])
            u_transpose(0, 0)
            for j in range(G):
                qkv(j, 0, 0, j)
            qk_transpose(0, 0)
            qk_transpose(1, 1)
            scores(0, 0, 0)
            scores(0, 0, 1)
            run_slots(pe, slot)
            o_transpose(BATCH - 1, 3)
            on_transpose(BATCH - 1, 3)
            project(BATCH - 1, 3)

            pe.wait_ge(ao_done, BATCH)

            def c_transpose(s, q):
                need(pe, c_done, s + 1)
                need(pe, cT_lo, s)
                for j in range(G):
                    last = nc.tensor.transpose(bank[0][:, j * TOK:(j + 1) * TOK], C[q][:, j, :], ident[:, :])
                last.then_inc(cT_mm, 1)

            def step_c(s, q):
                last_step = isinstance(s, int) and s == GROUPS - 1
                need(pe, cT_lo, s + 1)
                for k in range(4):
                    need(pe, h_out, 4 * s + k - 3)
                    product(bank[4 + k], [w[:, k * 128:(k + 1) * 128] for w in wf1_hl], [h[:, :] for h in UHL[q]]).then_inc(f1_mm, 1)
                need(pe, hq2, s)
                for j in range(G):
                    last = product(bank[1 + j // 2][:, (j % 2) * (D + 1):(j % 2 + 1) * (D + 1)], [h[:, j * TOK:(j + 1) * TOK] for h in UHL[q]], [g[:, :] for g in gram_hl])
                last.then_inc(g_mm, 1)
                need(pe, h_out, 4 * s + 4)
                need(pe, ff_done, s * G)
                for j in range(G):
                    for k in range(4):
                        last = mm(bank[3][:, j * D:(j + 1) * D], HT[q][:, k, j * TOK:(j + 1) * TOK], w_f2[:, k, :], start=k == 0, stop=k == 3)
                last.then_inc(f2_mm, 1)
                if not last_step:
                    c_transpose(s + 1, 1 - q)
            pe.wait_ge(split_low, 1)
            c_transpose(0, 0)
            run_steps(pe, step_c)

            pe.wait_ge(wD_in, 48)
            pe.wait_ge(ff_done, BATCH)

            def d_front(s, q):
                need(pe, x4_done, s + 1)
                need(pe, rl_done, s)
                for j in range(G):
                    last = nc.tensor.transpose(bank[0][:, j * TOK:(j + 1) * TOK], X4[q][:, j, :], ident[:, :])
                last.then_inc(x4T_mm, 1)

            def d_router(s, q):
                need(pe, x4_lo, s + 1)
                for j in range(G):
                    last = product(bank[0][:, j * EXPERTS:(j + 1) * EXPERTS], [h[:, j * TOK:(j + 1) * TOK] for h in UHL[q]], [w[:, :] for w in wr_hl])
                last.then_inc(rl_mm, 1)

            def up(s, q, n):
                col = (n % 2) * FF + (n // 2) * 128 if n < 8 else 2 * FF + (n - 8) * 128
                if n == 0:
                    need(pe, x4_lo, s + 1)
                if n < 4:
                    need(pe, gelu_done, 8 * s - 4 + n + 1)
                elif n < 12:
                    k = (n - 4) // 2
                    if n % 2 == 0:
                        need(pe, silu_done, 4 * s + k + 1)
                    else:
                        need(pe, hs_mul, 4 * s + k + 1)
                else:
                    need(pe, gelu_done, 8 * s + n - 12 + 1)
                product(bank[4 + n % 4], [w[:, col:col + 128] for w in wup_hl], [h[:, :] for h in UHL[q]]).then_inc(up_mm, 1)

            def down(s, q, j):
                T = s * G + j
                part = slice(j * TOK, (j + 1) * TOK)
                if j == 0:
                    need(pe, hs_mul, 4 * s + 4)
                    need(pe, gelu_done, 8 * s + 8)
                need(pe, bank2_free, T + 1)
                for k in range(SHARED_CHUNKS):
                    last = mm(bank[2][:, 0:D], HS[q][:, k, part], w_sd[:, k, :], start=k == 0, stop=k == SHARED_CHUNKS - 1)
                last.then_inc(sd_mm, 1)
                need(pe, bank3_free, T + 1)
                for e in range(4):
                    last = mm(bank[3][:, e * D:(e + 1) * D], HR[q][:, e, part], w_rd[:, e, :], start=True, stop=True)
                last.then_inc(rd_a, 1)
                need(pe, bank1_free, T + 1)
                for e in range(4):
                    last = mm(bank[1][:, e * D:(e + 1) * D], HR[q][:, 4 + e, part], w_rd[:, 4 + e, :], start=True, stop=True)
                last.then_inc(rd_b, 1)

            def step_d(s, q):
                first = isinstance(s, int) and s == 0
                last_step = isinstance(s, int) and s == GROUPS - 1
                for j in range(G):
                    for n in range(4 * j, 4 * j + 4):
                        up(s, q, n)
                    if not first:
                        down(s - 1, 1 - q, j)
                    if j == 0 and not last_step:
                        d_front(s + 1, 1 - q)
                    if j == 2 and not last_step:
                        d_router(s + 1, 1 - q)
            pe.wait_ge(split_low, 6)
            d_front(0, 0)
            d_router(0, 0)
            run_steps(pe, step_d)
            for j in range(G):
                down(GROUPS - 1, 1, j)

        @block.vector
        def _(dve):
            places = iter(range(64))

            def hold(semaphore, value):
                dve.wait_ge(semaphore, value)
                place = next(places)
                nc.vector.tensor_scalar(held[:, place:place + 1], zero[:, 0:1], 1.0, None, ALU.mult)

            def mark(semaphore, count=1):
                place = next(places)
                nc.vector.tensor_scalar(held[:, place:place + 1], zero[:, 0:1], 1.0, None, ALU.mult).then_inc(semaphore, count)

            dve.wait_ge(consts, 5)
            dve.wait_ge(wA_in, 16 * (WA - 1))
            dve.wait_ge(keep_mm, 1)
            nc.vector.tensor_scalar(keep[:, :], bank[0][:, 0:BATCH], score_b[:, 0:1], None, ALU.add).then_inc(keep_lin, 1)
            nc.vector.tensor_scalar(bias1[:, :], condT[:, :], fc_bias[:, 0:1], None, ALU.add).then_inc(ada_done, 1)
            dve.wait_ge(ada_mm, 1)
            nc.vector.tensor_tensor(ada_sb[:, 0:512], bank[4][0:BATCH, :], b_ada[:, 0:512], ALU.add)
            nc.vector.tensor_tensor(ada_sb[:, 512:768], bank[5][0:BATCH, 0:256], b_ada[:, 512:768], ALU.add)
            nc.vector.tensor_copy(ada_sb[:, 768:ADA], bank[5][0:BATCH, 256:256 + EXPERTS]).then_inc(ada_done, 1)
            dve.wait_ge(ada_done, 2)
            sc = ada_sb[:, 0:768].rearrange("b (k n) -> b k n", k=2)[:, :, D:2 * D]
            nc.vector.tensor_scalar(sc, sc, 1.0, None, ALU.add).then_inc(ada_done, 1)
            dve.wait_ge(keep_sig, 1)
            nc.vector.tensor_scalar(keep[:, :], keep[:, :], float(TOK), 1.0, ALU.mult, ALU.max).then_inc(keep_done, 1)
            dve.wait_ge(keep_done, 1)

            def phase_a(i):
                need(dve, mvA, 2 * i)
                need(dve, x1_done, 2 * i)
                for q in range(2):
                    s = 2 * i + q
                    dve.wait_ge(norm_bc, s + 1)
                    for j in range(G):
                        last = nc.vector.tensor_scalar(junkV[q][:, j, :], bank[q][:, j * TOK:(j + 1) * TOK], nsq[q][:, j:j + 1], 0.0,
                                                       ALU.is_gt, ALU.add, accum_out=above[q][:, j:j + 1])
                    last.then_inc(rank_done, 1)
                for q in range(2):
                    s = 2 * i + q
                    dve.wait_ge(rank_done, s + 1)
                    nc.vector.scalar_tensor_tensor(above[q][:, :], above[q][:, :], 1.0, keep[:, bass.ds(s * G, G)], ALU.add, ALU.is_le).then_inc(keep_done, 1)
                    dve.wait_ge(keep_done, 2 * i + q + 2)
                    nc.vector.tensor_scalar(factor[q][:, :], above[q][:, :], 1.0, None, ALU.add).then_inc(fac_done, 1)
                for q in range(2):
                    s = 2 * i + q
                    dve.wait_ge(gram_mm, s + 1)
                    need(dve, y_mm, 2 * i)
                    nc.vector.scalar_tensor_tensor(MB[q][:, :, :], bank[4 + q][:, :].rearrange("p (g n) -> p g n", g=G), 1.0 / (D * RANK),
                                                   w1T[:, :].unsqueeze(1).broadcast_to([D, G, D]), ALU.mult, ALU.add).then_inc(mb_done, 1)
                for q in range(2):
                    s = 2 * i + q
                    dve.wait_ge(yT_mm, s + 1)
                    nc.vector.tensor_tensor(X[:, bass.ds(s * G, G), :], bank[q][:, :].rearrange("p (g n) -> p g n", g=G), X1[q][:, :, :], ALU.add).then_inc(x2_done, 1)
                for q in range(2):
                    s = 2 * i + q
                    hold(x2_done, s + 1)
                    for j in range(G):
                        last = nc.vector.bn_stats(st6[q][:, j, :], X[:, bass.ds(s * G + j, 1), :])
                    last.then_inc(statA, 1)
                for q in range(2):
                    s = 2 * i + q
                    hold(statA, s + 1)
                    for j in range(G):
                        last = nc.vector.bn_aggr(mvq[q][:, j, :], st6[q][:, j, :])
                    last.then_inc(aggrA, 1)
                for q in range(2):
                    s = 2 * i + q
                    dve.wait_ge(aggrA, s + 1)
                    nc.vector.tensor_scalar(mv[:, bass.ds(s * G, G), :], mvq[q][:, :, :], 1.0, None, ALU.mult).then_inc(mvA, 1)
            phase_a(0)
            with dve.Fori(1, PAIRS) as i:
                phase_a(i)
            dve.wait_ge(gram2_mm, 1)
            nc.vector.tensor_copy(bb_f1[:, :], bank[0][:, 0:1])
            nc.vector.tensor_copy(gram_hl[0][:, :], bank[1][:, 0:D + 1]).then_inc(gram2_done, 1)
            dve.wait_ge(gram2_done, 1)
            nc.vector.tensor_tensor(gram_hl[1][:, :], bank[1][:, 0:D + 1], gram_hl[0][:, :], ALU.subtract).then_inc(gram2_done, 2)
            nc.vector.memset(bank[3][:, :], 0.0).then_inc(bank3_clear, 1)

            links = [0]

            def link(instruction):
                links[0] += 1
                instruction.then_inc(chain, 1)
                dve.wait_ge(chain, links[0])

            def run(instruction):
                links[0] += 1
                instruction.then_inc(chain, 1)

            def norm_rows(acts):
                vec, m, v = nc.vector, mv[:, :, 0], mv[:, :, 1]
                at = links[0]
                link(vec.tensor_tensor(row_n2[:, :], m, m, ALU.mult))
                link(vec.tensor_tensor(row_n2[:, :], row_n2[:, :], v, ALU.add))
                link(vec.tensor_scalar(row_n2[:, :], row_n2[:, :], float(D), None, ALU.mult))
                link(vec.tensor_scalar(sm[0][:, :], row_n2[:, :], TINY, None, ALU.max))
                dve.wait_ge(chain_act, acts + 3)
                link(vec.tensor_scalar(sm[4][:, :], sm[2][:, :], MAX_NORM, None, ALU.min))
                link(vec.tensor_scalar(sm[0][:, :], sm[0][:, :], 0.0625, None, ALU.min))
                link(vec.tensor_scalar(sm[7][:, :], sm[0][:, :], 1 / 11, 1 / 9, ALU.mult, ALU.add))
                for k in (7, 5, 3, 1):
                    link(vec.tensor_tensor(sm[7][:, :], sm[7][:, :], sm[0][:, :], ALU.mult))
                    link(vec.tensor_scalar(sm[7][:, :], sm[7][:, :], 1 / k, None, ALU.add))
                link(vec.tensor_scalar(sm[8][:, :], sm[2][:, :], 0.25, None, ALU.is_lt))
                link(vec.tensor_tensor(sm[7][:, :], sm[7][:, :], sm[8][:, :], ALU.mult))
                link(vec.tensor_scalar(sm[8][:, :], sm[8][:, :], -0.5, 0.5, ALU.mult, ALU.add))
                dve.wait_ge(chain_act, acts + 5)
                link(vec.tensor_tensor(sm[5][:, :], sm[5][:, :], sm[6][:, :], ALU.subtract))
                link(vec.tensor_tensor(sm[5][:, :], sm[5][:, :], sm[3][:, :], ALU.mult))
                link(vec.tensor_tensor(sm[5][:, :], sm[5][:, :], sm[8][:, :], ALU.mult))
                link(vec.tensor_tensor(sm[5][:, :], sm[5][:, :], sm[7][:, :], ALU.add))
                link(vec.reciprocal(sm[5][:, :], sm[5][:, :]))
                link(vec.tensor_tensor(sm[5][:, :], sm[5][:, :], sm[5][:, :], ALU.mult))
                link(vec.scalar_tensor_tensor(sm[7][:, :], sm[5][:, :], 1e-6, v, ALU.mult, ALU.add))
                assert links[0] == at + ROW_OPS - 1
            dve.wait_ge(mvA, GROUPS)
            norm_rows(0)
            dve.wait_ge(rows_ready, 1)
            dve.wait_ge(wB_in, 64)

            def front1(s, q):
                dve.wait_ge(adr_in, 16 * (s + 1))
                need(dve, u_done, s * G)
                need(dve, uT_mm, s - 1)
                need(dve, n2u_done, (s - 1) * G)
                for j in range(G):
                    T = s * G + j
                    nc.vector.scalar_tensor_tensor(U[q][:, j:j + 1, :], X[:, bass.ds(T, 1), :], mv[:, bass.ds(T, 1), 0], ADR[q][:, j:j + 1, D:2 * D], ALU.subtract, ALU.mult).then_inc(u_half, 1)
                for j in range(G):
                    T = s * G + j
                    need(dve, u_half, T + 1)
                    nc.vector.scalar_tensor_tensor(U[q][:, j, :], U[q][:, j, :], row_r[:, bass.ds(T, 1)], ADR[q][:, j, 0:D], ALU.mult, ALU.add).then_inc(u_done, 1)

            def front2(s, q):
                need(dve, su_rs, s + 1)
                nc.vector.tensor_scalar(su[q][:, :], n2u[q][:, :], CAP, 1.0, ALU.mult, ALU.min).then_inc(su_done, 1)
                need(dve, uT_hi, s + 1)
                nc.vector.tensor_tensor(UHL[q][1][:, :], bank[0][:, :], UHL[q][0][:, :], ALU.subtract).then_inc(uT_lo, 1)

            def qkv_out(T, s, q, j):
                need(dve, su_done, s + 1)
                need(dve, qkv_mm, T + 1)
                nc.vector.scalar_tensor_tensor(QKV[q][:, j, :], bank[0][:, 0:3 * D], su[q][:, j:j + 1], b_qkv[:, :], ALU.mult, ALU.add).then_inc(qkv_done, 1)

            def head_sums(T, q, j):
                need(dve, sq_done, T + 1)
                nc.vector.tensor_reduce(ST[q][:, j * 48:(j + 1) * 48], SQ[j % 2][:, :].rearrange("p (a d) -> p a d", d=HD), AX.X, ALU.add).then_inc(hsum_done, 1)

            def projection_sums(s, q):
                need(dve, hsum_done, (s + 1) * G)
                nc.vector.tensor_reduce(ST[q][:, G * 48:G * 51], ST[q][:, 0:G * 48].rearrange("p (a h) -> p a h", h=HEADS), AX.X, ALU.add).then_inc(psum_done, 1)

            def factors(s, q):
                need(dve, st_rs, s + 1)
                nc.vector.tensor_scalar(FP[q][:, :], ST[q][:, G * 48:G * 51], CAP * HEAD_SCALE, HEAD_SCALE, ALU.mult, ALU.min).then_inc(fp_a, 1)
                need(dve, fp_a, s + 1)
                nc.vector.scalar_tensor_tensor(FC[q][:, :, :].rearrange("p g (a h) -> p (g a) h", h=HEADS), ST[q][:, 0:G * 48].rearrange("p (a h) -> p a h", h=HEADS), CAP,
                                               FP[q][:, :].unsqueeze(2).broadcast_to([TOK, G * 3, HEADS]), ALU.mult, ALU.min).then_inc(fac_b, 1)

            def scale_qk(T, s, q, j):
                need(dve, fac_b, s + 1)
                need(dve, hi_done, 2 * T - 2)
                need(dve, scaled, T)
                nc.vector.tensor_tensor(SC[j % 2][:, :].rearrange("p (h d) -> p h d", d=HD), QKV[q][:, j, 0:2 * D].rearrange("p (h d) -> p h d", d=HD),
                                        FC[q][:, j, 0:32].unsqueeze(2).broadcast_to([TOK, 32, HD]), ALU.mult).then_inc(scaled, 1)

            def low_parts(T, j):
                sc = SC[j % 2][:, :].rearrange("p (a h d) -> p a h d", a=2, d=HD)
                need(dve, hi_done, 2 * T + 2)
                nc.vector.tensor_tensor(QS[j % 2][:, :, 1, :], sc[:, 0, :, :], QS[j % 2][:, :, 0, :], ALU.subtract)
                nc.vector.tensor_tensor(KS[j % 2][:, :, 2, :], sc[:, 1, :, :], KS[j % 2][:, :, 0, :], ALU.subtract).then_inc(lo_done, 1)

            def normalise(T, j):
                need(dve, ot_mm, T + 1)
                heads = bank[1][:, :].rearrange("p (h e) -> p h e", e=32)
                nc.vector.reciprocal(RD[j % 2][:, :], heads[:, :, HD]).then_inc(rd_done, 1)
                need(dve, rd_done, T + 1)
                nc.vector.tensor_tensor(ON[j % 2][:, :].rearrange("p (h d) -> p h d", d=HD), heads[:, :, 0:HD],
                                        RD[j % 2][:, :].unsqueeze(2).broadcast_to([TOK, HEADS, HD]), ALU.mult).then_inc(on_done, 1)

            def ao_out(T, j):
                need(dve, wo_mm, T + 1)
                need(dve, ga_done, T + 1)
                nc.vector.tensor_tensor(AO[j % 2][:, :], bank[1][:, TOK:2 * TOK], b_o[:, :], ALU.add).then_inc(ao_done, 1)

            def row_sums(T, j):
                square = nc.vector.scalar_tensor_tensor
                need(dve, ao_done, T + 1)
                square(junkD[j % 2], AO[j % 2][:, :], 1.0, AO[j % 2][:, :], ALU.mult, ALU.mult, accum_out=n2a[:, bass.ds(T, 1)]).then_inc(n2a_done, 1)
                need(dve, ga_done, T + 3)
                branch = BR[:, bass.ds(T, 1), :]
                nc.vector.tensor_scalar(junkM[j % 2].unsqueeze(1), branch, 1.0, 0.0, ALU.mult, ALU.add, accum_out=sbr[:, bass.ds(T, 1)])
                square(junkX[j % 2].unsqueeze(1), branch, 1.0, X[:, bass.ds(T, 1), :], ALU.mult, ALU.mult,
                       accum_out=dxg[:, bass.ds(T, 1)]).then_inc(dx_done, 1)

            def slot(s, q, r):
                after, back, before = tile(s, q, r, 2), tile(s, q, r, -1), tile(s, q, r, -2)
                front = not (isinstance(s, int) and s >= GROUPS - 1)
                first = isinstance(s, int) and s == 0 and r < 2
                have = not (isinstance(s, int) and s in (0, GROUPS))
                F = (s + 1) * G
                if r == 0 and have:
                    factors(s, q)
                if after and not first:
                    scale_qk(*after)
                if before:
                    ao_out(before[0], before[3])
                if r == 3 and front:
                    head_sums(F, 1 - q, 0)
                if after and not first:
                    low_parts(after[0], after[3])
                if r > 1 and front:
                    qkv_out(F + 2 * r - 4, s + 1, 1 - q, 2 * r - 4)
                if back:
                    normalise(back[0], back[3])
                if front:
                    if r == 1:
                        front2(s + 1, 1 - q)
                    elif r > 1:
                        qkv_out(F + 2 * r - 3, s + 1, 1 - q, 2 * r - 3)
                if before:
                    row_sums(before[0], before[3])
                if r == 0 and front:
                    front1(s + 1, 1 - q)
                if front and r == 3:
                    for j in range(1, G):
                        head_sums(F + j, 1 - q, j)
                    projection_sums(s + 1, 1 - q)
            front1(0, 0)
            front2(0, 0)
            for j in range(G):
                qkv_out(j, 0, 0, j)
                head_sums(j, 0, j)
            projection_sums(0, 0)
            factors(0, 0)
            for j in range(2):
                scale_qk(j, 0, 0, j)
                low_parts(j, j)
            run_slots(dve, slot)
            ao_out(BATCH - 2, 2)
            normalise(BATCH - 1, 3)
            row_sums(BATCH - 2, 2)
            ao_out(BATCH - 1, 3)
            row_sums(BATCH - 1, 3)

            def mobius(k, acts):
                vec = nc.vector
                assert links[0] == mob_at[k]
                link(vec.tensor_scalar(sm[0][:, :], n2a[:, :], TINY, None, ALU.max))
                link(vec.tensor_scalar(sm[1][:, :], n2g[:, :], TINY, None, ALU.max))
                dve.wait_ge(chain_act, acts + 4)
                link(vec.tensor_scalar(sm[3][:, :], sm[3][:, :], CAP, 1.0, ALU.mult, ALU.min))
                link(vec.tensor_tensor(sm[6][:, :], sm[3][:, :], sm[5][:, :], ALU.mult))
                link(vec.tensor_scalar(sm[6][:, :], sm[6][:, :], 1e-7, None, ALU.max))
                dve.wait_ge(chain_act, acts + 5)
                link(vec.reciprocal(sm[8][:, :], sm[6][:, :]))
                link(vec.tensor_tensor(sm[7][:, :], sm[7][:, :], sm[8][:, :], ALU.mult))
                link(vec.tensor_tensor(sm[7][:, :], sm[7][:, :], sm[3][:, :], ALU.mult))
                link(vec.tensor_tensor(sm[4][:, :], sm[7][:, :], dxg[:, :], ALU.mult))
                link(vec.tensor_tensor(sm[5][:, :], sm[7][:, :], sm[7][:, :], ALU.mult))
                link(vec.tensor_tensor(sm[5][:, :], sm[5][:, :], n2g[:, :], ALU.mult))
                link(vec.tensor_scalar(sm[4][:, :], sm[4][:, :], 2.0, 1.0, ALU.mult, ALU.add))
                link(vec.tensor_tensor(al[:, :], sm[4][:, :], sm[5][:, :], ALU.add))
                link(vec.tensor_tensor(sm[5][:, :], sm[5][:, :], row_n2[:, :], ALU.mult))
                link(vec.tensor_tensor(sm[5][:, :], sm[5][:, :], sm[4][:, :], ALU.add))
                link(vec.tensor_scalar(sm[5][:, :], sm[5][:, :], 1e-7, None, ALU.max))
                link(vec.reciprocal(sm[5][:, :], sm[5][:, :]))
                link(vec.tensor_scalar(sm[4][:, :], row_n2[:, :], -1.0, 1.0, ALU.mult, ALU.add))
                link(vec.tensor_tensor(sm[4][:, :], sm[4][:, :], sm[7][:, :], ALU.mult))
                link(vec.tensor_tensor(be[:, :], sm[4][:, :], sm[5][:, :], ALU.mult))
                link(vec.tensor_tensor(al[:, :], al[:, :], sm[5][:, :], ALU.mult))
                nc.vector.tensor_scalar(held[:, 60 + k:61 + k], zero[:, 0:1], 1.0, None, ALU.mult).then_inc(coef_ready, 1)
                link(vec.tensor_scalar(held[:, 62 + k:63 + k], zero[:, 0:1], 1.0, None, ALU.mult))
                assert links[0] == mob_at[k] + MOB_OPS
            dve.wait_ge(n2g_done, BATCH)
            dve.wait_ge(n2a_done, BATCH)
            dve.wait_ge(dx_done, BATCH)
            mobius(0, 6)

            vec, mx, vx = nc.vector, mv[:, :, 0], mv[:, :, 1]
            mb, cov, vb, t = sm[0][:, :], sm[1][:, :], sm[2][:, :], sm[3][:, :]
            link(vec.tensor_scalar(mb, sbr[:, :], 1.0 / D, None, ALU.mult))
            run(vec.tensor_tensor(cov, mx, mb, ALU.mult))
            link(vec.tensor_tensor(vb, mb, mb, ALU.mult))
            run(vec.scalar_tensor_tensor(cov, dxg[:, :], 1.0 / D, cov, ALU.mult, ALU.subtract))
            run(vec.scalar_tensor_tensor(vb, n2g[:, :], 1.0 / D, vb, ALU.mult, ALU.subtract))
            run(vec.tensor_tensor(mx, mx, al[:, :], ALU.mult))
            link(vec.tensor_tensor(mb, mb, be[:, :], ALU.mult))
            run(vec.tensor_tensor(cov, cov, al[:, :], ALU.mult))
            run(vec.tensor_tensor(vb, vb, be[:, :], ALU.mult))
            run(vec.tensor_tensor(t, al[:, :], al[:, :], ALU.mult))
            link(vec.tensor_tensor(mx, mx, mb, ALU.add))
            run(vec.tensor_tensor(vx, vx, t, ALU.mult))
            link(vec.scalar_tensor_tensor(vb, cov, 2.0, vb, ALU.mult, ALU.add))
            link(vec.tensor_tensor(vb, vb, be[:, :], ALU.mult))
            link(vec.tensor_tensor(vx, vx, vb, ALU.add))
            link(vec.tensor_scalar(vx, vx, 0.0, None, ALU.max))
            assert links[0] == NORM2_AT, links
            norm_rows(11)
            dve.wait_ge(rows_ready, 2)

            def c_front(s, q):
                need(dve, x3_done, s + 1)
                dve.wait_ge(cdr_in, 16 * (s + 1))
                need(dve, cu_done, s * G)
                need(dve, cn2u, (s - 1) * G)
                for j in range(G):
                    T = s * G + j
                    nc.vector.scalar_tensor_tensor(U[q][:, j:j + 1, :], X3[:, bass.ds(T, 1), :], mv[:, bass.ds(T, 1), 0], ADR[q][:, j:j + 1, D:2 * D], ALU.subtract, ALU.mult).then_inc(cu_half, 1)
                for j in range(G):
                    T = s * G + j
                    need(dve, cu_half, T + 1)
                    nc.vector.scalar_tensor_tensor(U[q][:, j, :], U[q][:, j, :], row_r[:, bass.ds(T, 1)], ADR[q][:, j, 0:D], ALU.mult, ALU.add).then_inc(cu_done, 1)

            def c_scale(s, q):
                need(dve, csu_rs, s + 1)
                nc.vector.tensor_scalar(su[q][:, :], n2u[q][:, :], CAP, 1.0, ALU.mult, ALU.min).then_inc(csu, 1)
                need(dve, csu, s + 1)
                need(dve, hdot, (s - 1) * G)
                need(dve, cT_mm, s - 1)
                nc.vector.tensor_tensor(C[q][:, :, :], U[q][:, :, :], su[q][:, :].unsqueeze(2).broadcast_to([TOK, G, D]), ALU.mult).then_inc(c_done, 1)

            def c_low(s, q):
                need(dve, cT_hi, s + 1)
                nc.vector.tensor_tensor(UHL[q][1][:, :], bank[0][:, :], UHL[q][0][:, :], ALU.subtract).then_inc(cT_lo, 1)

            def h_norm(s, q):
                need(dve, g_mm, s + 1)
                need(dve, hdot, s * G)
                for j in range(G):
                    nc.vector.tensor_tensor_reduce(out=junkV[0][:, j, :], in0=bank[1 + j // 2][:, (j % 2) * (D + 1):(j % 2) * (D + 1) + D], in1=C[q][:, j, :],
                                                   scale=1.0, scalar=0.0, op0=ALU.mult, op1=ALU.add, accum_out=hq[q][:, j:j + 1]).then_inc(hdot, 1)
                need(dve, hdot, (s + 1) * G)
                for k in range(2):
                    last = nc.vector.scalar_tensor_tensor(hq[q][:, 2 * k:2 * k + 2], bank[1 + k][:, 0:2 * (D + 1)].rearrange("p (j n) -> p j n", n=D + 1)[:, :, D], 2.0,
                                                          hq[q][:, 2 * k:2 * k + 2], ALU.mult, ALU.add)
                last.then_inc(hq2, 1)
                need(dve, hq2, s + 1)
                nc.vector.tensor_scalar(hq[q][:, :], hq[q][:, :], bb_f1[:, 0:1], TINY, ALU.add, ALU.max).then_inc(hq3, 1)

            def h_scale(s, q):
                need(dve, hrs, s + 1)
                nc.vector.tensor_scalar(sh[q][:, :], hq[q][:, :], CAP, 1.0, ALU.mult, ALU.min).then_inc(hs_done, 1)

            def ff_out(s, q):
                need(dve, hs_done, s + 1)
                need(dve, f2_mm, s + 1)
                for j in range(G):
                    nc.vector.scalar_tensor_tensor(FO[q][:, j, :], bank[3][:, j * D:(j + 1) * D], sh[q][:, j:j + 1], b_f2[:, :], ALU.mult, ALU.add).then_inc(ff_done, 1)

            def c_dot(s, q):
                need(dve, cga, s + 1)
                need(dve, ff_done, (s + 1) * G)
                for j in range(G):
                    T = s * G + j
                    nc.vector.scalar_tensor_tensor(junkV[1][:, j:j + 1, :], BR[:, bass.ds(T, 1), :], 1.0, X3[:, bass.ds(T, 1), :], ALU.mult, ALU.mult,
                                                   accum_out=dxg[:, bass.ds(T, 1)]).then_inc(cdx, 1)

            def step_c(s, q):
                last = isinstance(s, int) and s == GROUPS - 1
                first = isinstance(s, int) and s == 0
                if not last:
                    c_front(s + 1, 1 - q)
                if not first:
                    ff_out(s - 1, 1 - q)
                if not last:
                    c_scale(s + 1, 1 - q)
                h_norm(s, q)
                h_scale(s, q)
                if not last:
                    c_low(s + 1, 1 - q)
                if not first:
                    c_dot(s - 1, 1 - q)
            c_front(0, 0)
            c_scale(0, 0)
            c_low(0, 0)
            run_steps(dve, step_c)
            ff_out(GROUPS - 1, 1)
            c_dot(GROUPS - 1, 1)
            dve.wait_ge(cdx, BATCH)
            dve.wait_ge(cn2a, BATCH)
            dve.wait_ge(cn2g, BATCH)
            mobius(1, 17)

            def d_low(s, q):
                need(dve, x4_hi, s + 1)
                nc.vector.tensor_tensor(UHL[q][1][:, :], bank[0][:, :], UHL[q][0][:, :], ALU.subtract).then_inc(x4_lo, 1)

            def logits(s, q):
                need(dve, rl_mm, s + 1)
                need(dve, dt_in, 16 * (s + 1))
                nc.vector.tensor_tensor(sg[q][:, :, :], bank[0][:, 0:G * EXPERTS].rearrange("p (g e) -> p g e", e=EXPERTS), ADT[q][:, :, :], ALU.add).then_inc(rl_done, 1)

            def route(s, q):
                vec = nc.vector
                need(dve, sig_done, s + 1)
                ops = [0]

                def runs(instruction):
                    ops[0] += 1
                    instruction.then_inc(rchain, 1)

                def rlink(instruction):
                    runs(instruction)
                    dve.wait_ge(rchain, ROUTE_OPS * s + ops[0])
                sel = rt[0][:, :, :]
                rlink(vec.tensor_tensor(sel, sg[q][:, :, :], b_router[:, :].unsqueeze(1).broadcast_to([TOK, G, EXPERTS]), ALU.add))
                full = [TOK, G, EXPERTS, EXPERTS]
                mine, other = sel.unsqueeze(3).broadcast_to(full), sel.unsqueeze(2).broadcast_to(full)
                for g in range(G):
                    last = vec.tensor_tensor(cmpb[0][:, g, :, :], other[:, g], mine[:, g], ALU.is_gt)
                runs(last)
                for g in range(G):
                    last = vec.tensor_tensor(cmpb[1][:, g, :, :], other[:, g], mine[:, g], ALU.is_equal)
                rlink(last)
                rlink(vec.tensor_tensor(cmpb[1][:, :, :, :], cmpb[1][:, :, :, :], before[:, :, :].unsqueeze(1).broadcast_to(full), ALU.mult))
                rlink(vec.tensor_tensor(cmpb[0][:, :, :, :].rearrange("p g a b -> p (g a b)"), cmpb[0][:, :, :, :].rearrange("p g a b -> p (g a b)"),
                                        cmpb[1][:, :, :, :].rearrange("p g a b -> p (g a b)"), ALU.add))
                rlink(vec.tensor_reduce(rt[1][:, :, :].rearrange("p g e -> p (g e)"), cmpb[0][:, :, :, :].rearrange("p g a b -> p (g a) b"), AX.X, ALU.add))
                rlink(vec.tensor_scalar(rt[1][:, :, :], rt[1][:, :, :], float(TOP_K), None, ALU.is_lt))
                rlink(vec.tensor_tensor(rt[2][:, :, :], rt[1][:, :, :], sg[q][:, :, :], ALU.mult))
                rlink(vec.tensor_reduce(rs[0][:, :], rt[2][:, :, :], AX.X, ALU.add))
                runs(vec.tensor_scalar(rs[1][:, :], rs[0][:, :], 1e-9, None, ALU.is_gt))
                rlink(vec.tensor_scalar(rs[0][:, :], rs[0][:, :], 1e-9, None, ALU.add))
                runs(vec.tensor_scalar(rs[2][:, :], rs[1][:, :], -1.0 / (TOP_K * (2 + TOP_K)), 1.0 / (TOP_K * (2 + TOP_K)), ALU.mult, ALU.add))
                rlink(vec.reciprocal(rs[0][:, :], rs[0][:, :]))
                runs(vec.scalar_tensor_tensor(rs[0][:, :], rs[0][:, :], 1.0 / (2 + TOP_K), rs[1][:, :], ALU.mult, ALU.mult))
                rlink(vec.tensor_tensor(rt[1][:, :, :], rt[1][:, :, :], rs[2][:, :].unsqueeze(2).broadcast_to([TOK, G, EXPERTS]), ALU.mult))
                rlink(vec.tensor_tensor(rt[2][:, :, :], rt[2][:, :, :], rs[0][:, :].unsqueeze(2).broadcast_to([TOK, G, EXPERTS]), ALU.mult))
                need(dve, out_done, (s - 1) * G)
                assert ops[0] == ROUTE_OPS, ops
                vec.tensor_tensor(gates[q][:, :, :], rt[1][:, :, :], rt[2][:, :, :], ALU.add).then_inc(gates_done, 1)

            def gate_shared(s, q, k):
                need(dve, silu_done, 4 * s + k + 1)
                need(dve, up_mm, 16 * s + 2 * k + 2)
                if k == 0:
                    need(dve, sd_mm, s * G - 3)
                nc.vector.tensor_tensor(HS[q][:, k, :], bank[4 + (2 * k + 1) % 4], S1[k % 2][:, :], ALU.mult).then_inc(hs_mul, 1)

            def combine(s, q, j):
                T = s * G + j
                stt = nc.vector.scalar_tensor_tensor
                low, high = OUT[q][:, j, :], AO[j % 2][:, :]
                low1 = OUT[q][:, j:j + 1, :]
                gate = lambda e: gates[q][:, j, e:e + 1]
                part = lambda e: bank[1 if e >= 4 else 3][:, (e % 4) * D:(e % 4 + 1) * D]
                at = 6 * T
                need(dve, sd_mm, T + 1)
                stt(low1, bank[2][:, 0:D].unsqueeze(1), 1.0 / (2 * (2 + TOP_K)), X[:, bass.ds(T, 1), :], ALU.mult, ALU.add).then_inc(bank2_free, 1)
                need(dve, rd_b, T + 1)
                need(dve, gates_done, s + 1)
                nc.vector.tensor_scalar(high, part(4), gate(4), None, ALU.mult).then_inc(acc_done, 1)
                dve.wait_ge(bank2_free, T + 2)
                stt(low, part(0), gate(0), low, ALU.mult, ALU.add).then_inc(acc_done, 1)
                dve.wait_ge(acc_done, at + 1)
                stt(high, part(5), gate(5), high, ALU.mult, ALU.add).then_inc(acc_done, 1)
                dve.wait_ge(acc_done, at + 2)
                stt(low, part(1), gate(1), low, ALU.mult, ALU.add).then_inc(acc_done, 1)
                dve.wait_ge(acc_done, at + 3)
                stt(high, part(6), gate(6), high, ALU.mult, ALU.add).then_inc(acc_done, 1)
                dve.wait_ge(acc_done, at + 4)
                stt(low, part(2), gate(2), low, ALU.mult, ALU.add).then_inc(acc_done, 1)
                dve.wait_ge(acc_done, at + 5)
                stt(high, part(7), gate(7), high, ALU.mult, ALU.add).then_inc(bank1_free, 1)
                dve.wait_ge(acc_done, at + 6)
                stt(low, part(3), gate(3), low, ALU.mult, ALU.add).then_inc(bank3_free, 1)
                dve.wait_ge(bank1_free, T + 2)
                dve.wait_ge(bank3_free, T + 2)
                nc.vector.tensor_tensor(low, low, high, ALU.add).then_inc(out_done, 1)

            def step_d(s, q):
                first = isinstance(s, int) and s == 0
                last = isinstance(s, int) and s == GROUPS - 1
                for j in range(G):
                    if j < 2:
                        gate_shared(s, q, 2 * j)
                        gate_shared(s, q, 2 * j + 1)
                    if not first:
                        if j == 0:
                            dve.wait_ge(out_stored[1 - q], 16 * pair[0] + 16)
                        combine(s - 1, 1 - q, j)
                    if j == 1 and not last:
                        d_low(s + 1, 1 - q)
                    if j == 3 and not last:
                        logits(s + 1, 1 - q)
                if not last:
                    route(s + 1, 1 - q)
            for semaphore in (bank1_free, bank2_free, bank3_free):
                mark(semaphore)
            for q in range(2):
                mark(out_stored[q], 16)
            dve.wait_ge(wD_in, 48)
            d_low(0, 0)
            logits(0, 0)
            route(0, 0)
            run_steps(dve, step_d)
            dve.wait_ge(out_stored[1], 16 * PAIRS)
            for j in range(G):
                combine(GROUPS - 1, 1, j)


def host_layout(inputs):
    import numpy as np
    t = lambda a: np.ascontiguousarray(a)
    f = np.asarray(inputs["fside_Bx1x1024x16_0"])[:, 0]
    return {
        "x": t(inputs["x"]),
        "condT": t(np.asarray(inputs["cond_1024"]).T),
        "score_w": t(inputs["L0_cond_score_w"]),
        "score_b": t(inputs["L0_cond_score_b"]),
        "w1T": t(np.asarray(inputs["L1_cond_W"]).T),
        "fc_bias": t(inputs["L1_cond_fc_bias"]),
        "fT": t(f.transpose(2, 0, 1)),
        "w_ada": t(inputs["L2_cond_w_ada"]),
        "b_ada": t(inputs["L2_cond_b_ada"]),
        "w_qkv": t(np.concatenate([np.asarray(inputs["L2_cond_w_" + n]) for n in "qkv"], axis=1)),
        "b_qkv": t(np.concatenate([np.asarray(inputs["L2_cond_b_" + n]) for n in "qkv"])),
        "w_o": t(inputs["L2_cond_w_o"]),
        "b_o": t(inputs["L2_cond_b_o"]),
        "w_f1": t(inputs["L2_cond_w_f1"]),
        "w_f1Tb": t(np.concatenate([np.asarray(inputs["L2_cond_w_f1"]).T.reshape(4, 128, D), np.asarray(inputs["L2_cond_b_f1"]).reshape(4, 128, 1)],
                                   axis=2).transpose(1, 0, 2)),
        "w_f2": t(inputs["L2_cond_w_f2"]),
        "b_f2": t(inputs["L2_cond_b_f2"]),
        "w_up": t(np.concatenate([np.asarray(inputs[n]).reshape(-1, D).T for n in ("L3_cond_s_w1", "L3_cond_s_w3", "L3_cond_r_w1")], axis=1)),
        "w_sd": t(np.asarray(inputs["L3_cond_s_w2"]).transpose(0, 2, 1).reshape(FF, D)),
        "w_rd": t(np.asarray(inputs["L3_cond_r_w2"]).transpose(0, 2, 1).reshape(EXPERTS * 128, D)),
        "b_router": t(inputs["L3_cond_router_bias"]),
        "w_routerT": t(np.asarray(inputs["L3_cond_W_router"]).T),
    }


def kernel(**inputs):
    import concourse.bacc as bacc
    from concourse.bass_utils import run_bass_kernel_spmd

    nc = bacc.Bacc("TRN2", target_bir_lowering=False, num_devices=1)
    arrays = host_layout(inputs)
    ins = {n: nc.dram_tensor(n, a.shape, mybir.dt.from_np(a.dtype), kind="ExternalInput").ap() for n, a in arrays.items()}
    out = nc.dram_tensor("out", (BATCH, TOK, D), FP32, kind="ExternalOutput").ap()
    build(nc, ins, out)
    return run_bass_kernel_spmd(nc, [arrays], core_ids=[0]).results[0]["out"]
```

```python
import math
from contextlib import ExitStack

import concourse.bass as bass
from concourse import mybir


FP32 = mybir.dt.float32
FP16 = mybir.dt.float16
ALU = mybir.AluOpType
ACT = mybir.ActivationFunctionType
AX = mybir.AxisListType

BATCH = 32
TOK = 128
D = 128
RANK = 16
HEADS, HD = 16, 8
FF = 512
EXPERTS, TOP_K = 8, 2
SHARED_CHUNKS = 4
G = 4
GROUPS = BATCH // G
PAIRS = GROUPS // 2
NG = G * TOK
ADA = 6 * D + EXPERTS

MAX_NORM = 0.9999899864196777
CAP = math.atanh(MAX_NORM)
_beta = lambda a, b: math.exp(math.lgamma(a) + math.lgamma(b) - math.lgamma(a + b))
HEAD_SCALE = _beta(HD / 2, 0.5) / _beta(D / 2, 0.5)
ROW_OPS = 21
ROW_CLIPPED = 10
ROUTE_OPS = 16
MOB_OPS = 21
MOB_TANH = 6
STAT_OPS = 16
TINY = 1e-18


def build(nc, ins, out):
    ctx = ExitStack()
    with ctx:
        def sb(name, shape, dt=FP32):
            return ctx.enter_context(nc.sbuf_tensor(name + "_sb", shape, dt))

        def sem(name):
            return ctx.enter_context(nc.semaphore(name))

        X = sb("X", [TOK, BATCH, D])
        X3 = sb("X3", [TOK, BATCH, D])
        BR = sb("BR", [TOK, BATCH, D])
        ident = sb("ident", [128, 128])
        ident16 = sb("ident16", [128, 128], FP16)
        zero = sb("zero", [128, 1])
        tiny = sb("tiny", [128, 1])

        bank = [ctx.enter_context(nc.psum_tensor(f"bank{k}", [128, 512], FP32)) for k in range(4)]
        wide = ctx.enter_context(nc.psum_tensor("wide", [128, 2048], FP32))
        bank += [wide[:, 512 * k:512 * (k + 1)] for k in range(4)]

        dram_ada = nc.dram_tensor("ada_rows", (BATCH, ADA), FP32, kind="Internal").ap()

        condT = sb("condT", [D, BATCH])
        score_w = sb("score_w", [D, 1])
        score_b = sb("score_b", [128, 1])
        w1T = sb("w1T", [D, D])
        fc_bias = sb("fc_bias", [D, 1])
        w_ada = sb("w_ada", [D, 6 * D])
        b_ada = sb("b_ada", [BATCH, 6 * D])
        w_router = sb("w_router", [D, 2, EXPERTS])
        ada_sb = sb("ada_sb", [BATCH, ADA])
        bias1 = sb("bias1", [D, BATCH])
        keep = sb("keep", [TOK, BATCH])
        mv = sb("mv", [TOK, BATCH, 2])

        nsq = [sb(f"nsq{q}", [TOK, G]) for q in range(2)]
        above = [sb(f"above{q}", [TOK, G]) for q in range(2)]
        factor = sb("factor", [TOK, BATCH])
        junkA = [sb(f"junkA{q}", [TOK, G, D]) for q in range(2)]
        junkV = [sb(f"junkV{q}", [TOK, G, D]) for q in range(2)]
        early = sb("early", [128, 8 * NG])
        X1, X1T, MB, YT = [[early[:, (2 * k + q) * NG:(2 * k + q + 1) * NG].rearrange("p (g n) -> p g n", g=G) for q in range(2)] for k in range(4)]
        fT = [sb(f"fT{q}", [RANK, G, D]) for q in range(2)]
        st6 = [sb(f"st6{q}", [TOK, G, 6]) for q in range(2)]

        w_qkv = sb("w_qkv", [D, 3 * D])
        wqkv_hl = [sb(f"wqkv_{n}", [D, 3 * D], FP16) for n in ("hi", "lo")]
        w_o = sb("w_o", [D, D])
        b_qkv = sb("b_qkv", [128, 3 * D])
        b_o = sb("b_o", [128, D])
        row_r = sb("row_r", [TOK, BATCH])
        row_n2 = sb("row_n2", [TOK, BATCH])
        sm = [sb(f"sm{k}", [TOK, BATCH]) for k in range(10)]
        ADR = [sb(f"ADR{q}", [128, G, 2 * D]) for q in range(2)]
        ADG = [sb(f"ADG{q}", [128, G, D]) for q in range(2)]
        U = [sb(f"U{q}", [TOK, G, D]) for q in range(2)]
        junkU = w_ada[:, 0:NG].rearrange("p (g n) -> p g n", g=G)
        n2u = [sb(f"n2u{q}", [TOK, G]) for q in range(2)]
        su = [sb(f"su{q}", [TOK, G]) for q in range(2)]
        UHL = [[sb(f"UT{n}{q}", [D, NG], FP16) for n in ("hi", "lo")] for q in range(2)]
        big = sb("big", [128, 16 * NG])
        P = [big[:, q * 4 * NG:(q + 1) * 4 * NG].rearrange("p (i c n) -> p i c n", i=4, c=4) for q in range(2)]
        QKV = [big[:, (8 + 3 * q) * NG:(11 + 3 * q) * NG].rearrange("p (g n) -> p g n", g=G) for q in range(2)]
        OS = [big[:, (14 + q) * NG:(15 + q) * NG].rearrange("p (c n) -> p c n", c=4) for q in range(2)]
        SQ = [sb(f"SQ{q}", [TOK, 3 * D]) for q in range(2)]
        ST = [sb(f"ST{q}", [TOK, G * 51]) for q in range(2)]
        FC = [sb(f"FC{q}", [TOK, G, 48]) for q in range(2)]
        FP = [sb(f"FP{q}", [TOK, G * 3]) for q in range(2)]
        SC = [sb(f"SC{q}", [TOK, 2 * D]) for q in range(2)]
        QS = [sb(f"QS{q}", [TOK, HEADS, 4, HD], FP16) for q in range(2)]
        KS = [sb(f"KS{q}", [TOK, HEADS, 4, HD], FP16) for q in range(2)]
        V = [sb(f"V{q}", [TOK, G, HEADS, HD + 1]) for q in range(2)]
        QKT = [sb(f"QKT{q}", [128, 2, 4, TOK], FP16) for q in range(2)]
        RD = [sb(f"RD{q}", [TOK, HEADS]) for q in range(2)]
        ON = [sb(f"ON{q}", [TOK, D]) for q in range(2)]
        OT = [sb(f"OT{q}", [D, TOK]) for q in range(2)]
        AO = [sb(f"AO{q}", [TOK, D]) for q in range(2)]
        junkD, junkX = [[junkV[q][:, k, :] for q in range(2)] for k in (0, 2)]
        junkS = [sb(f"junkS{q}", [TOK, 2, D]) for q in range(2)]
        junkM = [junkV[q][:, 3, :] for q in range(2)]
        sbr = sb("sbr", [TOK, BATCH])
        n2a, n2g, dxg = sb("n2a", [TOK, BATCH]), sb("n2g", [TOK, BATCH]), sb("dxg", [TOK, BATCH])
        al, be = sb("al", [TOK, BATCH]), sb("be", [TOK, BATCH])
        w_f1 = sb("w_f1", [D, FF])
        wf1_hl = [sb(f"wf1_{n}", [D, FF], FP16) for n in ("hi", "lo")]
        w_f1Tb = sb("w_f1Tb", [128, 4, D + 1])
        gram_hl = [sb(f"gram_{n}", [D, D + 1], FP16) for n in ("hi", "lo")]
        bb_f1 = sb("bb_f1", [128, 1])
        w_f2 = sb("w_f2", [128, 4, D])
        b_f2 = sb("b_f2", [128, D])
        C = [sb(f"C{q}", [TOK, G, D]) for q in range(2)]
        HT = [early[:, q * 4 * NG:(q + 1) * 4 * NG].rearrange("p (k n) -> p k n", k=4) for q in range(2)]
        hq = [sb(f"hq{q}", [TOK, G]) for q in range(2)]
        sh = [sb(f"sh{q}", [TOK, G]) for q in range(2)]
        FO = [sb(f"FO{q}", [TOK, G, D]) for q in range(2)]
        UP = 4 * FF
        w_up = big[:, 0:UP]
        wup_hl = [sb(f"wup_{n}", [D, UP], FP16) for n in ("hi", "lo")]
        wr_hl = [sb(f"wr_{n}", [D, EXPERTS], FP16) for n in ("hi", "lo")]
        w_sd = sb("w_sd", [128, SHARED_CHUNKS, D])
        w_rd = early[:, 0:EXPERTS * D].rearrange("p (e n) -> p e n", e=EXPERTS)
        wrd_hl = [sb(f"wrd_{n}", [128, EXPERTS, D], FP16) for n in ("hi", "lo")]
        b_router = sb("b_router", [128, EXPERTS])
        ADT = [sb(f"ADT{q}", [128, G, EXPERTS]) for q in range(2)]
        earlier = sb("earlier", [128, EXPERTS, EXPERTS])
        S1 = [junkA[q][:, :, :].rearrange("p g n -> p (g n)") for q in range(2)]
        HS = HT
        HR = [ADR[k // 2][:, :, :].rearrange("p g n -> p (g n)")[:, (k % 2) * NG:(k % 2 + 1) * NG] for k in range(4)]
        HRHL = [[big[:, (2 * q + h) * EXPERTS * NG // 2:(2 * q + h + 1) * EXPERTS * NG // 2].bitcast(FP16).rearrange("p (e n) -> p e n", e=EXPERTS) for h in range(2)]
                for q in range(2)]
        sg = [sb(f"sg{q}", [TOK, G, EXPERTS]) for q in range(2)]
        gates = [sb(f"gates{q}", [TOK, G, EXPERTS]) for q in range(2)]
        cmpb = [junkS[k][:, :, :].rearrange("p a (g x y) -> p (a g) x y", x=EXPERTS, y=EXPERTS) for k in range(2)]
        rt = [sb(f"rt{k}", [TOK, G, EXPERTS]) for k in range(3)]
        rs = [sb(f"rs{k}", [TOK, G]) for k in range(3)]
        OUT = FO
        X4 = C

        mvq = [sb(f"mvq{q}", [TOK, G, 2]) for q in range(2)]
        held_pool = sb("held_pool", [128, 1])
        held = sb("held", [128, 64])

        consts = sem("consts")
        x_first = sem("x_first")
        x_rest = sem("x_rest")
        wA_in = sem("wA_in")
        wB_in = sem("wB_in")
        wC_in = sem("wC_in")
        wD_in = sem("wD_in")
        wup_in = sem("wup_in")
        wB_split = sem("wB_split")
        split_high = sem("split_high")
        split_low = sem("split_low")
        gram2_mm = sem("gram2_mm")
        gram2_done = sem("gram2_done")
        bank3_clear = sem("bank3_clear")
        f_in = [sem(f"f_in{q}") for q in range(2)]
        ada_mm = sem("ada_mm")
        ada_done = sem("ada_done")
        ada_stored = sem("ada_stored")
        keep_mm = sem("keep_mm")
        keep_lin = sem("keep_lin")
        keep_sig = sem("keep_sig")
        keep_done = sem("keep_done")
        norm_done = sem("norm_done")
        norm_bc = sem("norm_bc")
        rank_done = sem("rank_done")
        fac_done = sem("fac_done")
        x1_done = sem("x1_done")
        x1T_mm = sem("x1T_mm")
        x1T_done = sem("x1T_done")
        gram_mm = sem("gram_mm")
        mb_done = sem("mb_done")
        y_mm = sem("y_mm")
        yT_done = sem("yT_done")
        yT_mm = sem("yT_mm")
        x2_done = sem("x2_done")
        statA = sem("statA")
        aggrA = sem("aggrA")
        mvA = sem("mvA")
        chain = sem("chain")
        chain_act = sem("chain_act")
        rows_ready = sem("rows_ready")
        coef_ready = sem("coef_ready")
        adr_in = sem("adr_in")
        adg_in = sem("adg_in")
        u_half = sem("u_half")
        u_done = sem("u_done")
        n2u_done = sem("n2u_done")
        su_ln = sem("su_ln")
        su_rs = sem("su_rs")
        su_done = sem("su_done")
        uT_mm = sem("uT_mm")
        uT_hi = sem("uT_hi")
        uT_lo = sem("uT_lo")
        qkv_mm = sem("qkv_mm")
        qkv_done = sem("qkv_done")
        sq_done = sem("sq_done")
        hsum_done = sem("hsum_done")
        psum_done = sem("psum_done")
        st_ln = sem("st_ln")
        st_rs = sem("st_rs")
        fp_a = sem("fp_a")
        fac_b = sem("fac_b")
        scaled = sem("scaled")
        v_done = sem("v_done")
        hi_done = sem("hi_done")
        lo_done = sem("lo_done")
        t16_mm = sem("t16_mm")
        t16_out = sem("t16_out")
        score_low = sem("score_low")
        score_high = sem("score_high")
        exp_low = sem("exp_low")
        exp_high = sem("exp_high")
        av_mm = sem("av_mm")
        os_done = sem("os_done")
        ot_mm = sem("ot_mm")
        rd_done = sem("rd_done")
        on_done = sem("on_done")
        onT_mm = sem("onT_mm")
        onT_out = sem("onT_out")
        wo_mm = sem("wo_mm")
        ao_done = sem("ao_done")
        ga_done = sem("ga_done")
        n2a_done = sem("n2a_done")
        n2g_done = sem("n2g_done")
        dx_done = sem("dx_done")
        x3_scaled = sem("x3_scaled")
        x3_branch = sem("x3_branch")
        x3_done = sem("x3_done")
        c_adr_in = sem("c_adr_in")
        c_adg_in = sem("c_adg_in")
        c_u_half = sem("c_u_half")
        c_u_done = sem("c_u_done")
        c_n2u_done = sem("c_n2u_done")
        c_su_ln = sem("c_su_ln")
        c_su_rs = sem("c_su_rs")
        c_su_done = sem("c_su_done")
        c_done = sem("c_done")
        cT_mm = sem("cT_mm")
        cT_hi = sem("cT_hi")
        cT_lo = sem("cT_lo")
        f1_mm = sem("f1_mm")
        h_out = sem("h_out")
        gram_h_mm = sem("gram_h_mm")
        h_dot = sem("h_dot")
        h_n2 = sem("h_n2")
        h_n2_all = sem("h_n2_all")
        h_ln = sem("h_ln")
        h_rs = sem("h_rs")
        h_scale_done = sem("h_scale_done")
        f2_mm = sem("f2_mm")
        ff_done = sem("ff_done")
        c_ga_done = sem("c_ga_done")
        c_n2a_done = sem("c_n2a_done")
        c_n2g_done = sem("c_n2g_done")
        c_dx_done = sem("c_dx_done")
        dt_in = sem("dt_in")
        x4_first = sem("x4_first")
        x4_scaled = sem("x4_scaled")
        x4_branch = sem("x4_branch")
        x4_sum = sem("x4_sum")
        x4_done = sem("x4_done")
        x4_copy = sem("x4_copy")
        x4T_mm = sem("x4T_mm")
        x4_hi = sem("x4_hi")
        x4_lo = sem("x4_lo")
        rl_mm = sem("rl_mm")
        rl_done = sem("rl_done")
        sig_done = sem("sig_done")
        rchain = sem("rchain")
        gates_done = sem("gates_done")
        up_mm = sem("up_mm")
        silu_done = sem("silu_done")
        hs_mul = sem("hs_mul")
        gelu_done = sem("gelu_done")
        hr_low = sem("hr_low")
        sd_mm = sem("sd_mm")
        rd_mm = sem("rd_mm")
        acc_done = sem("acc_done")
        out_done = sem("out_done")
        bank1_free = sem("bank1_free")
        bank2_free = sem("bank2_free")
        bank3_free = sem("bank3_free")
        out_stored = [sem(f"out_stored{q}") for q in range(2)]

        def need(eng, semaphore, value):
            if not (isinstance(value, int) and value <= 0):
                eng.wait_ge(semaphore, value)

        pair = [0]

        def run_steps(eng, step):
            pair[0] = 0
            step(0, 0)
            with eng.Fori(0, PAIRS - 1) as i:
                pair[0] = i
                step(2 * i + 1, 1)
                step(2 * i + 2, 0)
            pair[0] = PAIRS - 1
            step(GROUPS - 1, 1)

        def tile(s, q, r, k=0):
            group, place = s + (r - 2 + k) // G, (r - 2 + k) % G
            number = group * G + place
            if isinstance(number, int) and not 0 <= number < BATCH:
                return None
            return number, group, (q + (r - 2 + k) // G) % 2, place

        def run_slots(eng, slot):
            run_steps(eng, lambda s, q: [slot(s, q, r) for r in range(G)])
            slot(GROUPS, 0, 0)
            slot(GROUPS, 0, 1)

        block = ctx.enter_context(nc.Block())

        x_v = ins["x"].rearrange("b t d -> t b d")
        out_v = out.rearrange("b t d -> t b d")
        f_v = ins["fT"]

        def row(name, parts):
            return ins[name].rearrange("(a n) -> a n", a=1).broadcast_to([parts, ins[name].shape[0]])

        WA_LOADS = 9
        mob_at = [ROW_OPS, 2 * ROW_OPS + MOB_OPS + STAT_OPS]
        norm2_at = ROW_OPS + MOB_OPS + STAT_OPS
        last_banks = ((2, 3, 1), (4, 5, 6))

        @block.sync
        def _(sp):
            sp.dma_start(X[:, 0:2 * G, :], x_v[:, 0:2 * G, :]).then_inc(x_first, 16)
            sp.dma_start(condT[:, :], ins["condT"]).then_inc(wA_in, 16)
            sp.dma_start(score_w[:, :], ins["score_w"]).then_inc(wA_in, 16)
            sp.dma_start(score_b[:, :], row("score_b", 128)).then_inc(wA_in, 16)
            sp.dma_start(w1T[:, :], ins["w1T"]).then_inc(wA_in, 16)
            sp.dma_start(fc_bias[:, :], ins["fc_bias"].rearrange("(p a) -> p a", a=1)).then_inc(wA_in, 16)
            for q in range(2):
                sp.dma_start(fT[q][:, :, :], f_v[:, q * G:(q + 1) * G, :]).then_inc(f_in[q], 16)
            sp.dma_start(w_ada[:, :], ins["w_ada"]).then_inc(wA_in, 16)
            sp.dma_start(b_ada[:, :], row("b_ada", BATCH)).then_inc(wA_in, 16)
            sp.dma_start(w_router[:, 0, :], ins["w_routerT"][0:D, :]).then_inc(wA_in, 16)
            sp.dma_start(w_router[:, 1, :], ins["w_routerT"][D:2 * D, :]).then_inc(wA_in, 16)
            for c in range(1, PAIRS):
                sp.dma_start(X[:, 2 * G * c:2 * G * (c + 1), :], x_v[:, 2 * G * c:2 * G * (c + 1), :]).then_inc(x_rest, 16)
            sp.wait_ge(ada_done, 3)
            sp.dma_start(dram_ada, ada_sb[:, :]).then_inc(ada_stored, 16)
            with sp.Fori(0, PAIRS - 1) as i:
                for q in range(2):
                    sp.wait_ge(gram_mm, 2 * i + q + 1)
                    sp.dma_start(fT[q][:, :, :], f_v[:, bass.ds(2 * G * i + (2 + q) * G, G), :]).then_inc(f_in[q], 16)
            sp.dma_start(w_qkv[:, :], ins["w_qkv"]).then_inc(wB_in, 16)
            sp.dma_start(w_o[:, :], ins["w_o"]).then_inc(wB_in, 16)
            sp.dma_start(b_qkv[:, :], row("b_qkv", 128)).then_inc(wB_in, 16)
            sp.dma_start(b_o[:, :], row("b_o", 128)).then_inc(wB_in, 16)
            sp.dma_start(w_f1[:, :], ins["w_f1"]).then_inc(wC_in, 16)
            sp.dma_start(w_f1Tb[:, :, :], ins["w_f1Tb"]).then_inc(wC_in, 16)
            sp.dma_start(w_f2[:, :, :], ins["w_f2"].rearrange("(k p) n -> p k n", p=128)).then_inc(wC_in, 16)
            sp.dma_start(b_f2[:, :], row("b_f2", 128)).then_inc(wC_in, 16)
            sp.dma_start(w_sd[:, :, :], ins["w_sd"].rearrange("(k p) n -> p k n", p=128)).then_inc(wD_in, 16)
            sp.dma_start(b_router[:, :], row("b_router", 128)).then_inc(wD_in, 16)
            sp.wait_ge(ada_stored, 16)
            ada_v = dram_ada.rearrange("b n -> () b n")

            def load_rows(s, q):
                sp.dma_start(ADR[q][:, :, :], ada_v[:, bass.ds(s * G, G), 0:2 * D].broadcast_to([128, G, 2 * D])).then_inc(adr_in, 16)

            def load_gates(s, q):
                sp.dma_start(ADG[q][:, :, :], ada_v[:, bass.ds(s * G, G), 2 * D:3 * D].broadcast_to([128, G, D])).then_inc(adg_in, 16)
            load_rows(0, 0)
            load_gates(0, 0)
            sp.wait_ge(yT_mm, GROUPS)
            sp.dma_start(w_rd[:, :, :], ins["w_rd"].rearrange("(k p) n -> p k n", p=128)).then_inc(wD_in, 16)

            def step_b(s, q):
                if isinstance(s, int) and s == GROUPS - 1:
                    return
                need(sp, u_done, s * G)
                sp.wait_ge(adr_in, 16 * (s + 1))
                load_rows(s + 1, 1 - q)
                if not (isinstance(s, int) and s == 0):
                    sp.wait_ge(ga_done, s * G + 2)
                sp.wait_ge(adg_in, 16 * (s + 1))
                load_gates(s + 1, 1 - q)
            run_steps(sp, step_b)
            sp.wait_ge(os_done, BATCH)
            sp.wait_ge(v_done, BATCH)
            sp.wait_ge(scaled, BATCH)
            sp.wait_ge(ot_mm, BATCH)
            sp.dma_start(w_up[:, :], ins["w_up"]).then_inc(wup_in, 16)

            def load_c(s, q):
                sp.dma_start(ADR[q][:, :, :], ada_v[:, bass.ds(s * G, G), 3 * D:5 * D].broadcast_to([128, G, 2 * D])).then_inc(c_adr_in, 16)

            def load_cg(s, q):
                sp.dma_start(ADG[q][:, :, :], ada_v[:, bass.ds(s * G, G), 5 * D:6 * D].broadcast_to([128, G, D])).then_inc(c_adg_in, 16)
            sp.wait_ge(u_done, BATCH)
            load_c(0, 0)
            sp.wait_ge(ga_done, BATCH + 2)
            load_cg(0, 0)

            def step_c(s, q):
                if isinstance(s, int) and s == GROUPS - 1:
                    return
                need(sp, c_u_done, s * G)
                sp.wait_ge(c_adr_in, 16 * (s + 1))
                load_c(s + 1, 1 - q)
                need(sp, c_ga_done, s)
                sp.wait_ge(c_adg_in, 16 * (s + 1))
                load_cg(s + 1, 1 - q)
            run_steps(sp, step_c)

            def load_t(s, q):
                sp.dma_start(ADT[q][:, :, :], ada_v[:, bass.ds(s * G, G), 6 * D:ADA].broadcast_to([128, G, EXPERTS])).then_inc(dt_in, 16)
            load_t(0, 0)

            def store(s, q):
                sp.wait_ge(out_done, (s + 1) * G)
                sp.dma_start(out_v[:, bass.ds(s * G, G), :], OUT[q][:, :, :]).then_inc(out_stored[q], 16)

            def step_d(s, q):
                last = isinstance(s, int) and s == GROUPS - 1
                if not last:
                    need(sp, rl_done, s)
                    sp.wait_ge(dt_in, 16 * (s + 1))
                    load_t(s + 1, 1 - q)
                if not (isinstance(s, int) and s == 0):
                    store(s - 1, 1 - q)
            run_steps(sp, step_d)
            for half in range(2):
                T = (GROUPS - 1) * G + half * G // 2
                sp.wait_ge(out_done, T + G // 2)
                sp.dma_start(out_v[:, T:T + G // 2, :], OUT[1][:, half * G // 2:(half + 1) * G // 2, :]).then_inc(out_stored[1], 16)
            for q in range(2):
                sp.wait_ge(out_stored[q], 16 * (PAIRS + 1 + q))

        @block.gpsimd
        def _(pool):
            pool.memset(ident[:, :], 0.0).then_inc(consts, 1)
            pool.memset(ident16[:, :], 0.0).then_inc(consts, 1)
            pool.memset(tiny[:, :], TINY)
            pool.memset(zero[:, :], 0.0).then_inc(consts, 1)
            pool.wait_ge(consts, 3)
            for m in (ident, ident16):
                pool.affine_select(out=m[:, :], in_=m[:, :], compare_op=ALU.not_equal, fill=1.0, base=0,
                                   pattern=[[-1, 128]], channel_multiplier=1).then_inc(consts, 1)
            def double_rows(i):
                for q in range(2):
                    s = 2 * i + q
                    pool.wait_ge(fac_done, s + 1)
                    need(pool, x1T_mm, s - 1)
                    pool.tensor_tensor(X1[q][:, :, :], X[:, bass.ds(s * G, G), :],
                                       factor[:, bass.ds(s * G, G)].unsqueeze(2).broadcast_to([TOK, G, D]), ALU.mult).then_inc(x1_done, 1)
            for q in range(2):
                pool.memset(AO[q][:, :], 0.0).then_inc(ga_done, 1)
                pool.memset(QS[q][:, :, :, :], 0.0)
                pool.memset(KS[q][:, :, :, :], 0.0)
                pool.memset(V[q][:, :, :, HD:HD + 1], HEAD_SCALE).then_inc(consts, 1)
            pool.memset(earlier[:, :, :], 1.0).then_inc(consts, 1)
            pool.wait_ge(consts, 8)
            pool.affine_select(out=earlier[:, :, :], in_=earlier[:, :, :], compare_op=ALU.is_gt, fill=0.0, base=0,
                               pattern=[[1, EXPERTS], [-1, EXPERTS]], channel_multiplier=0).then_inc(consts, 1)
            double_rows(0)
            with pool.Fori(1, PAIRS) as i:
                double_rows(i)
            pool.wait_ge(wB_in, 64)
            pool.tensor_copy(wqkv_hl[0][:, :], w_qkv[:, :]).then_inc(wB_split, 1)
            pool.wait_ge(wB_split, 1)
            pool.tensor_tensor(wqkv_hl[1][:, :], w_qkv[:, :], wqkv_hl[0][:, :], ALU.subtract).then_inc(wB_split, 1)

            def split(hl, w, count):
                pool.tensor_copy(hl[0], w).then_inc(split_high, 1)
                pool.wait_ge(split_high, count)
                pool.tensor_tensor(hl[1], w, hl[0], ALU.subtract).then_inc(split_low, 1)
            pool.wait_ge(wC_in, 64)
            split([h[:, :] for h in wf1_hl], w_f1[:, :], 1)
            split([h[:, :] for h in wr_hl], w_router[:, 0, :], 2)
            pool.wait_ge(wD_in, 48)
            split([h[:, :, :] for h in wrd_hl], w_rd[:, :, :], 3)


            def v_scale(T, s, q, j):
                need(pool, fac_b, s + 1)
                need(pool, av_mm, T - 2)
                pool.tensor_tensor(V[q][:, j, :, 0:HD], QKV[q][:, j, 2 * D:3 * D].rearrange("p (h d) -> p h d", d=HD),
                                   FC[q][:, j, 32:48].unsqueeze(2).broadcast_to([TOK, HEADS, HD]), ALU.mult).then_inc(v_done, 1)

            def gate(T, s, q, j):
                need(pool, ao_done, T + 1)
                if j == 0:
                    need(pool, adg_in, 4 * T + 16)
                pool.tensor_tensor(BR[:, bass.ds(T, 1), :], AO[j % 2][:, :].unsqueeze(1), ADG[q][:, j:j + 1, :], ALU.mult).then_inc(ga_done, 1)

            def slot(s, q, r):
                ahead, behind = tile(s, q, r, 1), tile(s, q, r, -2)
                if ahead:
                    v_scale(*ahead)
                if behind:
                    gate(*behind)
            run_slots(pool, slot)
            gate(BATCH - 2, GROUPS - 1, 1, 2)
            gate(BATCH - 1, GROUPS - 1, 1, 3)

            def split_up(k):
                part = slice(k * FF, (k + 1) * FF)
                split([h[:, part] for h in wup_hl], w_up[:, part], 4 + k)
            pool.wait_ge(wup_in, 16)
            split_up(0)

            def pool_hold(semaphore, value):
                need(pool, semaphore, value)
                pool.tensor_tensor(held_pool[:, :], zero[:, :], zero[:, :], ALU.add)

            def per_row(t, rows):
                return t[:, rows].unsqueeze(2).broadcast_to([TOK, G, D])

            def sum3(s):
                rows = bass.ds(s * G, G)
                pool.tensor_tensor(X3[:, rows, :], X[:, rows, :], per_row(al, rows), ALU.mult).then_inc(x3_scaled, 1)
                pool.tensor_tensor(BR[:, rows, :], BR[:, rows, :], per_row(be, rows), ALU.mult).then_inc(x3_branch, 1)
                need(pool, x3_scaled, s + 1)
                pool_hold(x3_branch, s + 1)
                pool.tensor_tensor(X3[:, rows, :], X3[:, rows, :], BR[:, rows, :], ALU.add).then_inc(x3_done, 1)

            def gate_c(s, q):
                pool.wait_ge(ff_done, (s + 1) * G)
                pool.wait_ge(c_adg_in, 16 * s + 16)
                pool.tensor_tensor(BR[:, bass.ds(s * G, G), :], FO[q][:, :, :], ADG[q][:, :, :], ALU.mult).then_inc(c_ga_done, 1)

            def step_c(s, q):
                if not (isinstance(s, int) and s == GROUPS - 1):
                    sum3(s + 1)
                if isinstance(s, int) and s == 0:
                    for k in range(1, 4):
                        split_up(k)
                if not (isinstance(s, int) and s == 0):
                    gate_c(s - 1, 1 - q)
            pool.wait_ge(coef_ready, 1)
            sum3(0)
            run_steps(pool, step_c)
            gate_c(GROUPS - 1, 1)

            def sum4(s, q):
                rows = bass.ds(s * G, G)
                need(pool, x4T_mm, s)
                need(pool, x4_copy, s)
                pool.tensor_tensor(X4[q][:, :, :], X3[:, rows, :], per_row(al, rows), ALU.mult).then_inc(x4_scaled, 1)
                pool.tensor_tensor(BR[:, rows, :], BR[:, rows, :], per_row(be, rows), ALU.mult).then_inc(x4_branch, 1)
                pool_hold(x4_scaled, s)
                pool.tensor_tensor(X4[q][:, :, :], X4[q][:, :, :], X[:, rows, :], ALU.add).then_inc(x4_sum, 1)
                need(pool, x4_branch, s)
                pool_hold(x4_sum, s)
                pool.tensor_tensor(X4[q][:, :, :], X4[q][:, :, :], BR[:, rows, :], ALU.add).then_inc(x4_done, 1)
            pool.wait_ge(coef_ready, 2)
            pool.wait_ge(x4_done, 1)

            def low_hidden(s, q):
                for e in range(EXPERTS):
                    need(pool, gelu_done, 8 * s + e + 1)
                    pool.tensor_tensor(HRHL[q][1][:, e, :], HR[e % 4], HRHL[q][0][:, e, :], ALU.subtract).then_inc(hr_low, 1)

            def step_d(s, q):
                if not (isinstance(s, int) and s == GROUPS - 1):
                    sum4(s + 1, 1 - q)
                low_hidden(s, q)
            run_steps(pool, step_d)

        @block.scalar
        def _(act):
            act.wait_ge(consts, 5)
            act.wait_ge(keep_lin, 1)
            act.activation(keep[:, :], keep[:, :], ACT.Sigmoid, bias=zero[:, 0:1]).then_inc(keep_sig, 1)
            act.preload_act_table_set("gelu_and_others")

            def norms(i):
                need(act, rank_done, 2 * i)
                need(act, norm_done, 8 * i)
                for q in range(2):
                    for j in range(G):
                        act.activation(junkA[q][:, j, :], X[:, bass.ds((2 * i + q) * G + j, 1), :], ACT.Square,
                                       accum_out=nsq[q][:, j:j + 1]).then_inc(norm_done, 1)

            def linear_gelu(i):
                for q in range(2):
                    act.wait_ge(x1T_mm, 2 * i + q + 1)
                    act.activation(X1T[q][:, :, :], bank[2 + q][:, :], ACT.Copy).then_inc(x1T_done, 1)
                for q in range(2):
                    act.wait_ge(y_mm, 2 * i + q + 1)
                    for j in range(G):
                        act.activation(YT[q][:, j, :], bank[6 + q][:, j * TOK:(j + 1) * TOK], ACT.Gelu,
                                       bias=bias1[:, bass.ds((2 * i + q) * G + j, 1)]).then_inc(yT_done, 1)
            act.wait_ge(ada_done, 1)
            act.wait_ge(x_first, 16)
            norms(0)
            act.wait_ge(x_rest, 16 * (PAIRS - 1))
            with act.Fori(1, PAIRS) as i:
                norms(i)
                linear_gelu(i - 1)
            linear_gelu(PAIRS - 1)
            act.preload_act_table_set("natural_log_exp_and_others")

            def small(out_, in_, func, at, **more):
                act.wait_ge(chain, at)
                act.activation(out_[:, :], in_[:, :], func, **more).then_inc(chain_act, 1)

            def norm_rows(at):
                small(sm[1], sm[0], ACT.Ln, at + 4)
                act.wait_ge(chain_act, at_act[0] + 1)
                act.activation(sm[2][:, :], sm[1][:, :], ACT.Exp, scale=0.5, bias=zero[:, 0:1]).then_inc(chain_act, 1)
                act.activation(sm[3][:, :], sm[1][:, :], ACT.Exp, scale=-0.5, bias=zero[:, 0:1]).then_inc(chain_act, 1)
                small(sm[5], sm[4], ACT.Ln, at + ROW_CLIPPED, bias=1.0)
                act.activation(sm[6][:, :], sm[4][:, :], ACT.Ln, scale=-1.0, bias=1.0).then_inc(chain_act, 1)
                small(sm[8], sm[7], ACT.Ln, at + ROW_OPS)
                act.wait_ge(chain_act, at_act[0] + 6)
                act.activation(row_r[:, :], sm[8][:, :], ACT.Exp, scale=-0.5, bias=zero[:, 0:1]).then_inc(rows_ready, 1)
                at_act[0] += 6
            at_act = [0]
            norm_rows(0)

            def act_mobius(k, tanh_set):
                small(sm[2], sm[0], ACT.Ln, mob_at[k] + 2)
                act.activation(sm[4][:, :], sm[1][:, :], ACT.Ln).then_inc(chain_act, 1)
                act.wait_ge(chain_act, at_act[0] + 2)
                act.activation(sm[3][:, :], sm[2][:, :], ACT.Exp, scale=-0.5).then_inc(chain_act, 1)
                act.activation(sm[5][:, :], sm[4][:, :], ACT.Exp, scale=0.5).then_inc(chain_act, 1)
                act.preload_act_table_set(tanh_set)
                small(sm[7], sm[6], ACT.Tanh, mob_at[k] + MOB_TANH)
                at_act[0] += 5

            def front_norm(s, q):
                need(act, u_done, (s + 1) * G)
                need(act, n2u_done, s * G)
                for j in range(G):
                    act.activation(junkU[:, j, :], U[q][:, j, :], ACT.Square, accum_out=n2u[q][:, j:j + 1]).then_inc(n2u_done, 1)
                need(act, n2u_done, (s + 1) * G)
                act.activation(n2u[q][:, :], n2u[q][:, :], ACT.Ln, bias=tiny[:, 0:1]).then_inc(su_ln, 1)
                need(act, su_ln, s + 1)
                act.activation(n2u[q][:, :], n2u[q][:, :], ACT.Exp, scale=-0.5).then_inc(su_rs, 1)

            def front_high(s, q):
                need(act, uT_mm, s + 1)
                act.activation(UHL[q][0][:, :], bank[0][:, :], ACT.Copy).then_inc(uT_hi, 1)

            def squares(T, q, j):
                need(act, qkv_done, T + 1)
                need(act, hsum_done, T - 1)
                act.activation(SQ[j % 2][:, :], QKV[q][:, j, :], ACT.Square).then_inc(sq_done, 1)

            def stats(s, q):
                need(act, psum_done, s + 1)
                act.activation(ST[q][:, :], ST[q][:, :], ACT.Ln, bias=tiny[:, 0:1]).then_inc(st_ln, 1)
                need(act, st_ln, s + 1)
                act.activation(ST[q][:, :], ST[q][:, :], ACT.Exp, scale=-0.5).then_inc(st_rs, 1)

            def high_parts(T, j):
                need(act, scaled, T + 1)
                need(act, t16_mm, T - 1)
                sc = SC[j % 2][:, :].rearrange("p (a h d) -> p a h d", a=2, d=HD)
                act.activation(QS[j % 2][:, :, 0:3:2, :], sc[:, 0, :, :].unsqueeze(2).broadcast_to([TOK, HEADS, 2, HD]), ACT.Copy).then_inc(hi_done, 1)
                act.activation(KS[j % 2][:, :, 0:2, :], sc[:, 1, :, :].unsqueeze(2).broadcast_to([TOK, HEADS, 2, HD]), ACT.Copy).then_inc(hi_done, 1)

            def qk_out(T, j):
                need(act, t16_mm, T + 1)
                need(act, score_high, T - 1)
                act.activation(QKT[j % 2][:, :, :, :].rearrange("p a c n -> p (a c n)"), bank[2][:, :].bitcast(FP16), ACT.Copy).then_inc(t16_out, 1)

            def exps(T, j, half):
                need(act, score_high if half else score_low, T + 1)
                need(act, av_mm, T - 1)
                act.activation(P[j % 2][:, 2 * half:2 * half + 2, :, :].rearrange("p i c n -> p (i c n)"), wide[:, 1024 * half:1024 * half + 1024],
                               ACT.Exp, scale=HD ** -0.5).then_inc(exp_high if half else exp_low, 1)

            def o_out(T, j):
                need(act, av_mm, T + 1)
                need(act, ot_mm, T)
                act.activation(OS[j % 2][:, :, :].rearrange("p c n -> p (c n)"), bank[3][:, :], ACT.Copy).then_inc(os_done, 1)

            def on_out(T, j):
                need(act, onT_mm, T + 1)
                need(act, wo_mm, T)
                act.activation(OT[j % 2][:, :], bank[1][:, 0:TOK], ACT.Copy).then_inc(onT_out, 1)

            def gated_norm(T, j):
                need(act, exp_low, T + 3 if not isinstance(T, int) else min(T + 3, BATCH))
                need(act, ga_done, T + 3)
                act.activation(junkS[j % 2][:, 1:2, :], BR[:, bass.ds(T, 1), :], ACT.Square, accum_out=n2g[:, bass.ds(T, 1)]).then_inc(n2g_done, 1)

            def slot(s, q, r):
                now, after, back, oldest = tile(s, q, r), tile(s, q, r, 2), tile(s, q, r, -1), tile(s, q, r, -2)
                have = not (isinstance(s, int) and s in (0, GROUPS))
                front = not (isinstance(s, int) and s >= GROUPS - 1)
                F = (s + 1) * G
                if isinstance(s, int) and s == 0 and r < 2:
                    after = None
                if now:
                    exps(now[0], now[3], 0)
                if front and r == 1:
                    front_norm(s + 1, 1 - q)
                if r == 0 and have:
                    stats(s, q)
                if front and r == 3:
                    squares(F, 1 - q, 0)
                if after and r > 0:
                    high_parts(after[0], after[3])
                if back:
                    o_out(back[0], back[3])
                if after and r == 0:
                    high_parts(after[0], after[3])
                if now:
                    exps(now[0], now[3], 1)
                if front and r == 3:
                    squares(F + 1, 1 - q, 1)
                if front and r == 1:
                    front_high(s + 1, 1 - q)
                if oldest:
                    gated_norm(oldest[0], oldest[3])
                if after:
                    qk_out(after[0], after[3])
                if back:
                    on_out(back[0], back[3])
                if front and r == 3:
                    squares(F + 2, 1 - q, 2)
                    squares(F + 3, 1 - q, 3)
            front_norm(0, 0)
            front_high(0, 0)
            for j in range(G):
                squares(j, 0, j)
            stats(0, 0)
            for j in range(2):
                high_parts(j, j)
            for j in range(2):
                qk_out(j, j)
            run_slots(act, slot)
            o_out(BATCH - 1, 3)
            on_out(BATCH - 1, 3)
            for T in (BATCH - 2, BATCH - 1):
                gated_norm(T, T % G)

            act_mobius(0, "gelu_and_others")
            act.preload_act_table_set("natural_log_exp_and_others")

            norm_rows(norm2_at)

            def c_front_norm(s, q):
                need(act, c_u_done, (s + 1) * G)
                need(act, c_n2u_done, s * G)
                for j in range(G):
                    act.activation(junkU[:, j, :], U[q][:, j, :], ACT.Square, accum_out=n2u[q][:, j:j + 1]).then_inc(c_n2u_done, 1)
                need(act, c_n2u_done, (s + 1) * G)
                act.activation(n2u[q][:, :], n2u[q][:, :], ACT.Ln, bias=tiny[:, 0:1]).then_inc(c_su_ln, 1)
                need(act, c_su_ln, s + 1)
                act.activation(n2u[q][:, :], n2u[q][:, :], ACT.Exp, scale=-0.5).then_inc(c_su_rs, 1)

            def c_front_high(s, q):
                need(act, cT_mm, s + 1)
                act.activation(UHL[q][0][:, :], bank[0][:, :], ACT.Copy).then_inc(cT_hi, 1)

            def h_evacuate(s, q, k):
                need(act, f1_mm, 4 * s + k + 1)
                act.activation(HT[q][:, k, :], bank[4 + k], ACT.Identity, bias=w_f1Tb[:, k, D:D + 1]).then_inc(h_out, 1)

            def h_norm(s, q):
                need(act, h_n2_all, s + 1)
                act.activation(hq[q][:, :], hq[q][:, :], ACT.Ln).then_inc(h_ln, 1)
                need(act, h_ln, s + 1)
                act.activation(hq[q][:, :], hq[q][:, :], ACT.Exp, scale=-0.5).then_inc(h_rs, 1)

            def c_norms(s, q):
                if isinstance(s, int) and s == GROUPS - 1:
                    act.wait_ge(c_n2g_done, s * G)
                else:
                    act.wait_ge(h_out, 4 * s + 5)
                need(act, ff_done, (s + 1) * G)
                for j in range(G):
                    T = s * G + j
                    act.activation(junkA[1][:, j, :], FO[q][:, j, :], ACT.Square, accum_out=n2a[:, bass.ds(T, 1)]).then_inc(c_n2a_done, 1)
                need(act, c_ga_done, s + 1)
                for j in range(G):
                    T = s * G + j
                    act.activation(junkA[0][:, j:j + 1, :], BR[:, bass.ds(T, 1), :], ACT.Square, accum_out=n2g[:, bass.ds(T, 1)]).then_inc(c_n2g_done, 1)

            def step_c(s, q):
                last = isinstance(s, int) and s == GROUPS - 1
                for k in range(4):
                    h_evacuate(s, q, k)
                if not last:
                    c_front_norm(s + 1, 1 - q)
                h_norm(s, q)
                if not last:
                    c_front_high(s + 1, 1 - q)
                if not (isinstance(s, int) and s == 0):
                    c_norms(s - 1, 1 - q)
            c_front_norm(0, 0)
            c_front_high(0, 0)
            run_steps(act, step_c)
            c_norms(GROUPS - 1, 1)
            act_mobius(1, "silu_and_others")

            def d_front(s, q):
                need(act, x4T_mm, s + 1)
                act.activation(UHL[q][0][:, :], bank[0][:, :], ACT.Copy).then_inc(x4_hi, 1)
                need(act, x4_done, s + 1)
                act.activation(X[:, bass.ds(s * G, G), :], X4[q][:, :, :], ACT.Copy).then_inc(x4_copy, 1)

            def d_router(s, q):
                need(act, rl_done, s + 1)
                act.activation(sg[q][:, :, :], sg[q][:, :, :], ACT.Sigmoid).then_inc(sig_done, 1)

            def step_d(s, q):
                last = isinstance(s, int) and s == GROUPS - 1
                for k in range(SHARED_CHUNKS):
                    need(act, up_mm, 16 * s + 2 * k + 1)
                    need(act, hs_mul, 4 * s + k - 1)
                    act.activation(S1[k % 2][:, :], bank[4 + (2 * k) % 4], ACT.Silu).then_inc(silu_done, 1)
                if not last:
                    d_front(s + 1, 1 - q)
                for e in range(EXPERTS):
                    need(act, up_mm, 16 * s + 8 + e + 1)
                    if e == 0:
                        need(act, rd_mm, s * G - 3)
                    need(act, hr_low, 8 * s + e - 3)
                    act.activation(HR[e % 4], bank[4 + e % 4], ACT.Gelu)
                    act.activation(HRHL[q][0][:, e, :], bank[4 + e % 4], ACT.Gelu).then_inc(gelu_done, 1)
                if not last:
                    d_router(s + 1, 1 - q)
            d_front(0, 0)
            d_router(0, 0)
            run_steps(act, step_d)

        @block.tensor
        def _(pe):
            mm = nc.tensor.matmul
            pe.wait_ge(wA_in, 16 * WA_LOADS)
            mm(bank[0][:, 0:BATCH], score_w[:, 0:1].to_broadcast([D, 128]), condT[:, :], start=True, stop=True).then_inc(keep_mm, 1)
            mm(bank[4][0:BATCH, :], condT[:, :], w_ada[:, 0:512], start=True, stop=True)
            mm(bank[5][0:BATCH, 0:256], condT[:, :], w_ada[:, 512:768], start=True, stop=True)
            mm(bank[5][0:BATCH, 256:256 + EXPERTS], condT[:, :], w_router[:, 1, :], start=True, stop=True).then_inc(ada_mm, 1)
            pe.wait_ge(consts, 5)
            pe.wait_ge(ada_done, 3)
            pe.wait_ge(keep_lin, 1)

            def spread_norms(i):
                need(pe, rank_done, 2 * i)
                for q in range(2):
                    pe.wait_ge(norm_done, 8 * i + 4 * q + 4)
                    for j in range(G):
                        last = nc.tensor.transpose(bank[q][:, j * TOK:(j + 1) * TOK], nsq[q][:, j:j + 1].to_broadcast([TOK, TOK]), ident[:, :])
                    last.then_inc(norm_bc, 1)

            def gram(i):
                for q in range(2):
                    pe.wait_ge(f_in[q], 16 * i + 16)
                    need(pe, mb_done, 2 * i)
                    for j in range(G):
                        last = mm(bank[4 + q][:, j * D:(j + 1) * D], fT[q][:, j, :], fT[q][:, j, :], start=True, stop=True)
                    last.then_inc(gram_mm, 1)

            def transpose_x1(i):
                pe.wait_ge(x2_done, 2 * i + 2)
                for q in range(2):
                    pe.wait_ge(x1_done, 2 * i + q + 1)
                    for j in range(G):
                        last = nc.tensor.transpose(bank[2 + q][:, j * TOK:(j + 1) * TOK], X1[q][:, j, :], ident[:, :])
                    last.then_inc(x1T_mm, 1)

            def linear(i):
                for q in range(2):
                    pe.wait_ge(mb_done, 2 * i + q + 1)
                    pe.wait_ge(x1T_done, 2 * i + q + 1)
                    for j in range(G):
                        last = mm(bank[6 + q][:, j * TOK:(j + 1) * TOK], MB[q][:, j, :], X1T[q][:, j, :], start=True, stop=True)
                    last.then_inc(y_mm, 1)

            def transpose_y(i):
                for q in range(2):
                    pe.wait_ge(yT_done, 8 * i + 4 * q + 4)
                    for j in range(G):
                        last = nc.tensor.transpose(bank[2 + q][:, j * TOK:(j + 1) * TOK], YT[q][:, j, :], ident[:, :])
                    last.then_inc(yT_mm, 1)
            spread_norms(0)
            gram(0)
            with pe.Fori(1, PAIRS) as i:
                spread_norms(i)
                transpose_x1(i - 1)
                linear(i - 1)
                gram(i)
                transpose_y(i - 1)
            transpose_x1(PAIRS - 1)
            linear(PAIRS - 1)
            transpose_y(PAIRS - 1)
            pe.wait_ge(wC_in, 64)
            pe.wait_ge(x2_done, GROUPS + 2)
            for k in range(4):
                mm(bank[1][:, 0:D + 1], w_f1Tb[:, k, 0:D], w_f1Tb[:, k, :], start=k == 0, stop=k == 3)
            for k in range(4):
                last = mm(bank[2][:, 0:1], w_f1Tb[:, k, D:D + 1].to_broadcast([128, 128]), w_f1Tb[:, k, D:D + 1], start=k == 0, stop=k == 3)
            last.then_inc(gram2_mm, 1)
            pe.wait_ge(wB_split, 2)

            def product(out_, left, right, start=True, stop=True):
                mm(out_, left[0], right[0], start=start, stop=False)
                mm(out_, left[0], right[1], start=False, stop=False)
                return mm(out_, left[1], right[0], start=False, stop=stop)

            def u_transpose(s, q):
                need(pe, u_done, (s + 1) * G)
                need(pe, qkv_done, s * G)
                for j in range(G):
                    last = nc.tensor.transpose(bank[0][:, j * TOK:(j + 1) * TOK], U[q][:, j, :], ident[:, :])
                last.then_inc(uT_mm, 1)

            def qkv(T, s, q, j, out_=bank[0]):
                need(pe, uT_lo, s + 1)
                if out_ is bank[0]:
                    need(pe, qkv_done, T)
                part = slice(j * TOK, (j + 1) * TOK)
                product(out_[:, 0:3 * D], [h[:, part] for h in UHL[q]], [w[:, :] for w in wqkv_hl]).then_inc(qkv_mm, 1)

            def qk_transpose(T, j):
                need(pe, lo_done, T + 1)
                need(pe, t16_out, T)
                b16 = bank[2][:, :].bitcast(FP16)
                for a, src in enumerate((QS, KS)):
                    flat = src[j % 2][:, :, :, :].rearrange("p h s d -> p (h s d)")
                    for c in range(4):
                        last = nc.tensor.transpose(b16[:, (4 * a + c) * TOK:(4 * a + c + 1) * TOK], flat[:, c * 128:(c + 1) * 128], ident16[:, :])
                last.then_inc(t16_mm, 1)

            def scores(T, j, half):
                need(pe, t16_out, T + 1)
                need(pe, exp_high if half else exp_low, T)
                t = QKT[j % 2]
                for c in range(4):
                    for i in (2 * half, 2 * half + 1):
                        r = slice(32 * i, 32 * i + 32)
                        last = mm(bank[4 + i][:, c * TOK:(c + 1) * TOK], t[r, 1, c, :], t[r, 0, c, :], start=True, stop=True)
                last.then_inc(score_high if half else score_low, 1)

            def attend(T, q, j):
                need(pe, exp_high, T + 1)
                need(pe, v_done, T + 1)
                need(pe, os_done, T)
                for c in range(4):
                    for i in range(4):
                        last = mm(bank[3][32 * i:32 * i + HD + 1, c * TOK:(c + 1) * TOK], V[q][:, j, 4 * c + i, :], P[j % 2][:, i, c, :], start=True, stop=True)
                last.then_inc(av_mm, 1)

            def o_transpose(T, j):
                need(pe, os_done, T + 1)
                need(pe, ao_done, T)
                for c in range(4):
                    last = nc.tensor.transpose(bank[1][:, c * 128:(c + 1) * 128], OS[j % 2][:, c, :], ident[:, :])
                last.then_inc(ot_mm, 1)

            def on_transpose(T, j):
                need(pe, on_done, T + 1)
                nc.tensor.transpose(bank[1][:, 0:TOK], ON[j % 2][:, :], ident[:, :]).then_inc(onT_mm, 1)

            def project(T, j):
                need(pe, onT_out, T + 1)
                mm(bank[1][:, TOK:2 * TOK], OT[j % 2][:, :], w_o[:, :], start=True, stop=True).then_inc(wo_mm, 1)

            def slot(s, q, r):
                now, nxt, after, back = tile(s, q, r), tile(s, q, r, 1), tile(s, q, r, 2), tile(s, q, r, -1)
                front = not (isinstance(s, int) and s >= GROUPS - 1)
                first = isinstance(s, int) and s == 0 and r < 2
                F = (s + 1) * G
                if nxt and not first:
                    scores(nxt[0], nxt[3], 0)
                if front:
                    if r == 1:
                        u_transpose(s + 1, 1 - q)
                    elif r > 1:
                        qkv(F + 2 * r - 4, s + 1, 1 - q, 2 * r - 4)
                if back:
                    o_transpose(back[0], back[3])
                if after and not first:
                    qk_transpose(after[0], after[3])
                if nxt and not first:
                    scores(nxt[0], nxt[3], 1)
                if front and r > 1:
                    qkv(F + 2 * r - 3, s + 1, 1 - q, 2 * r - 3)
                if back:
                    on_transpose(back[0], back[3])
                if now:
                    attend(now[0], now[2], now[3])
                if back:
                    project(back[0], back[3])
            u_transpose(0, 0)
            for j in range(G):
                qkv(j, 0, 0, j, bank[(0, 5, 6, 7)[j]])
            pe.wait_ge(gram2_done, 3)
            qk_transpose(0, 0)
            qk_transpose(1, 1)
            scores(0, 0, 0)
            scores(0, 0, 1)
            pe.wait_ge(bank3_clear, 1)
            run_slots(pe, slot)
            o_transpose(BATCH - 1, 3)
            on_transpose(BATCH - 1, 3)
            project(BATCH - 1, 3)

            pe.wait_ge(ao_done, BATCH)

            def c_transpose(s, q):
                need(pe, c_done, s + 1)
                need(pe, cT_lo, s)
                for j in range(G):
                    last = nc.tensor.transpose(bank[0][:, j * TOK:(j + 1) * TOK], C[q][:, j, :], ident[:, :])
                last.then_inc(cT_mm, 1)

            def step_c(s, q):
                last_step = isinstance(s, int) and s == GROUPS - 1
                need(pe, cT_lo, s + 1)
                for k in range(4):
                    need(pe, h_out, 4 * s + k - 3)
                    product(bank[4 + k], [w[:, k * 128:(k + 1) * 128] for w in wf1_hl], [h[:, :] for h in UHL[q]]).then_inc(f1_mm, 1)
                need(pe, h_n2, s)
                for j in range(G):
                    last = product(bank[1 + j // 2][:, (j % 2) * (D + 1):(j % 2 + 1) * (D + 1)], [h[:, j * TOK:(j + 1) * TOK] for h in UHL[q]], [g[:, :] for g in gram_hl])
                last.then_inc(gram_h_mm, 1)
                need(pe, h_out, 4 * s + 4)
                need(pe, ff_done, s * G)
                for j in range(G):
                    for k in range(4):
                        last = mm(bank[3][:, j * D:(j + 1) * D], HT[q][:, k, j * TOK:(j + 1) * TOK], w_f2[:, k, :], start=k == 0, stop=k == 3)
                last.then_inc(f2_mm, 1)
                if not last_step:
                    c_transpose(s + 1, 1 - q)
            pe.wait_ge(split_low, 1)
            c_transpose(0, 0)
            run_steps(pe, step_c)

            pe.wait_ge(wD_in, 48)
            pe.wait_ge(ff_done, BATCH)

            def d_front(s, q):
                need(pe, x4_done, s + 1)
                need(pe, rl_done, s)
                for j in range(G):
                    last = nc.tensor.transpose(bank[0][:, j * TOK:(j + 1) * TOK], X4[q][:, j, :], ident[:, :])
                last.then_inc(x4T_mm, 1)

            def d_router(s, q):
                need(pe, x4_lo, s + 1)
                for j in range(G):
                    last = product(bank[0][:, j * EXPERTS:(j + 1) * EXPERTS], [h[:, j * TOK:(j + 1) * TOK] for h in UHL[q]], [w[:, :] for w in wr_hl])
                last.then_inc(rl_mm, 1)

            def up(s, q, n):
                col = (n % 2) * FF + (n // 2) * 128 if n < 8 else 2 * FF + (n - 8) * 128
                if n == 0:
                    need(pe, x4_lo, s + 1)
                if n < 4:
                    need(pe, gelu_done, 8 * s - 4 + n + 1)
                elif n < 12:
                    k = (n - 4) // 2
                    if n % 2 == 0:
                        need(pe, silu_done, 4 * s + k + 1)
                    else:
                        need(pe, hs_mul, 4 * s + k + 1)
                else:
                    need(pe, gelu_done, 8 * s + n - 12 + 1)
                product(bank[4 + n % 4], [w[:, col:col + 128] for w in wup_hl], [h[:, :] for h in UHL[q]]).then_inc(up_mm, 1)

            def down(s, q, j, banks=(2, 3, 1), free=0):
                T = s * G + j
                part = slice(j * TOK, (j + 1) * TOK)
                shared, low, high = [bank[b] for b in banks]
                if j == 0:
                    need(pe, hs_mul, 4 * s + 4)
                    need(pe, hr_low, 8 * s + 8)
                need(pe, bank2_free, T + 1 - free)
                for k in range(SHARED_CHUNKS):
                    last = mm(shared[:, 0:D], HS[q][:, k, part], w_sd[:, k, :], start=k == 0, stop=k == SHARED_CHUNKS - 1)
                last.then_inc(sd_mm, 1)
                need(pe, bank3_free, T + 1 - free)
                for e in range(4):
                    product(low[:, e * D:(e + 1) * D], [h[:, e, part] for h in HRHL[q]], [w[:, e, :] for w in wrd_hl])
                need(pe, bank1_free, T + 1 - free)
                for e in range(4):
                    last = product(high[:, e * D:(e + 1) * D], [h[:, 4 + e, part] for h in HRHL[q]], [w[:, 4 + e, :] for w in wrd_hl])
                last.then_inc(rd_mm, 1)

            def step_d(s, q):
                first = isinstance(s, int) and s == 0
                last_step = isinstance(s, int) and s == GROUPS - 1
                for j in range(G):
                    for n in range(4 * j, 4 * j + 4):
                        up(s, q, n)
                    if j == 1 and not last_step:
                        d_front(s + 1, 1 - q)
                    if not first:
                        down(s - 1, 1 - q, j)
                    if j == 2 and not last_step:
                        d_router(s + 1, 1 - q)
            pe.wait_ge(split_low, 7)
            d_front(0, 0)
            d_router(0, 0)
            run_steps(pe, step_d)
            for j in range(G):
                down(GROUPS - 1, 1, j, last_banks[j % 2], 1 if j else 0)

        @block.vector
        def _(dve):
            places = iter(range(64))

            def hold(semaphore, value):
                dve.wait_ge(semaphore, value)
                place = next(places)
                nc.vector.tensor_scalar(held[:, place:place + 1], zero[:, 0:1], 1.0, None, ALU.mult)

            def mark(semaphore, count=1):
                place = next(places)
                nc.vector.tensor_scalar(held[:, place:place + 1], zero[:, 0:1], 1.0, None, ALU.mult).then_inc(semaphore, count)

            dve.wait_ge(consts, 5)
            dve.wait_ge(wA_in, 16 * WA_LOADS)
            dve.wait_ge(keep_mm, 1)
            nc.vector.tensor_scalar(keep[:, :], bank[0][:, 0:BATCH], score_b[:, 0:1], None, ALU.add).then_inc(keep_lin, 1)
            nc.vector.tensor_scalar(bias1[:, :], condT[:, :], fc_bias[:, 0:1], None, ALU.add).then_inc(ada_done, 1)
            dve.wait_ge(ada_mm, 1)
            nc.vector.tensor_tensor(ada_sb[:, 0:512], bank[4][0:BATCH, :], b_ada[:, 0:512], ALU.add)
            nc.vector.tensor_tensor(ada_sb[:, 512:768], bank[5][0:BATCH, 0:256], b_ada[:, 512:768], ALU.add)
            nc.vector.tensor_copy(ada_sb[:, 768:ADA], bank[5][0:BATCH, 256:256 + EXPERTS]).then_inc(ada_done, 1)
            dve.wait_ge(ada_done, 2)
            sc = ada_sb[:, 0:768].rearrange("b (k n) -> b k n", k=2)[:, :, D:2 * D]
            nc.vector.tensor_scalar(sc, sc, 1.0, None, ALU.add).then_inc(ada_done, 1)
            dve.wait_ge(keep_sig, 1)
            nc.vector.tensor_scalar(keep[:, :], keep[:, :], float(TOK), 1.0, ALU.mult, ALU.max).then_inc(keep_done, 1)
            dve.wait_ge(keep_done, 1)

            def rank(i):
                need(dve, fac_done, 2 * i)
                for q in range(2):
                    s = 2 * i + q
                    dve.wait_ge(norm_bc, s + 1)
                    for j in range(G):
                        last = nc.vector.tensor_scalar(junkV[q][:, j, :], bank[q][:, j * TOK:(j + 1) * TOK], nsq[q][:, j:j + 1], 0.0,
                                                       ALU.is_gt, ALU.add, accum_out=above[q][:, j:j + 1])
                    last.then_inc(rank_done, 1)
                for q in range(2):
                    s = 2 * i + q
                    dve.wait_ge(rank_done, s + 1)
                    nc.vector.scalar_tensor_tensor(above[q][:, :], above[q][:, :], 1.0, keep[:, bass.ds(s * G, G)], ALU.add, ALU.is_le).then_inc(keep_done, 1)
                    dve.wait_ge(keep_done, 2 * i + q + 2)
                    nc.vector.tensor_scalar(factor[:, bass.ds(s * G, G)], above[q][:, :], 1.0, None, ALU.add).then_inc(fac_done, 1)

            def weights(i):
                for q in range(2):
                    s = 2 * i + q
                    dve.wait_ge(gram_mm, s + 1)
                    need(dve, y_mm, 2 * i)
                    nc.vector.scalar_tensor_tensor(MB[q][:, :, :], bank[4 + q][:, :].rearrange("p (g n) -> p g n", g=G), 1.0 / (D * RANK),
                                                   w1T[:, :].unsqueeze(1).broadcast_to([D, G, D]), ALU.mult, ALU.add).then_inc(mb_done, 1)

            def add_and_stats(i):
                for q in range(2):
                    s = 2 * i + q
                    dve.wait_ge(yT_mm, s + 1)
                    for j in range(G):
                        T = s * G + j
                        last = nc.vector.scalar_tensor_tensor(X[:, bass.ds(T, 1), :], X[:, bass.ds(T, 1), :], factor[:, bass.ds(T, 1)],
                                                              bank[2 + q][:, j * D:(j + 1) * D].unsqueeze(1), ALU.mult, ALU.add)
                    last.then_inc(x2_done, 1)
                for q in range(2):
                    s = 2 * i + q
                    hold(x2_done, s + 3)
                    for j in range(G):
                        last = nc.vector.bn_stats(st6[q][:, j, :], X[:, bass.ds(s * G + j, 1), :])
                    last.then_inc(statA, 1)
                for q in range(2):
                    s = 2 * i + q
                    hold(statA, s + 1)
                    for j in range(G):
                        last = nc.vector.bn_aggr(mvq[q][:, j, :], st6[q][:, j, :])
                    last.then_inc(aggrA, 1)
                for q in range(2):
                    s = 2 * i + q
                    dve.wait_ge(aggrA, s + 1)
                    nc.vector.tensor_scalar(mv[:, bass.ds(s * G, G), :], mvq[q][:, :, :], 1.0, None, ALU.mult).then_inc(mvA, 1)
            mark(x2_done, 2)
            rank(0)
            weights(0)
            with dve.Fori(1, PAIRS) as i:
                rank(i)
                weights(i)
                add_and_stats(i - 1)
            add_and_stats(PAIRS - 1)
            links = [0]

            def link(instruction):
                links[0] += 1
                instruction.then_inc(chain, 1)
                dve.wait_ge(chain, links[0])

            def run(instruction):
                links[0] += 1
                instruction.then_inc(chain, 1)

            def norm_rows(acts):
                vec, m, v = nc.vector, mv[:, :, 0], mv[:, :, 1]
                at = links[0]
                link(vec.tensor_tensor(row_n2[:, :], m, m, ALU.mult))
                link(vec.tensor_tensor(row_n2[:, :], row_n2[:, :], v, ALU.add))
                link(vec.tensor_scalar(row_n2[:, :], row_n2[:, :], float(D), None, ALU.mult))
                link(vec.tensor_scalar(sm[0][:, :], row_n2[:, :], TINY, None, ALU.max))
                link(vec.tensor_scalar(sm[9][:, :], sm[0][:, :], 0.0625, None, ALU.min))
                link(vec.tensor_scalar(sm[7][:, :], sm[9][:, :], 1 / 11, None, ALU.mult))
                for k in (9, 7, 5):
                    link(vec.scalar_tensor_tensor(sm[7][:, :], sm[7][:, :], 1 / k, sm[9][:, :], ALU.add, ALU.mult))
                dve.wait_ge(chain_act, acts + 3)
                run(vec.tensor_scalar(sm[4][:, :], sm[2][:, :], MAX_NORM, None, ALU.min))
                assert links[0] == at + ROW_CLIPPED
                run(vec.tensor_scalar(sm[8][:, :], sm[2][:, :], 0.25, None, ALU.is_lt))
                link(vec.scalar_tensor_tensor(sm[7][:, :], sm[7][:, :], 1 / 3, sm[9][:, :], ALU.add, ALU.mult))
                link(vec.scalar_tensor_tensor(sm[7][:, :], sm[7][:, :], 1.0, sm[8][:, :], ALU.add, ALU.mult))
                link(vec.tensor_scalar(sm[8][:, :], sm[8][:, :], -0.5, 0.5, ALU.mult, ALU.add))
                dve.wait_ge(chain_act, acts + 5)
                link(vec.tensor_tensor(sm[5][:, :], sm[5][:, :], sm[6][:, :], ALU.subtract))
                link(vec.tensor_tensor(sm[5][:, :], sm[5][:, :], sm[3][:, :], ALU.mult))
                link(vec.tensor_tensor(sm[5][:, :], sm[5][:, :], sm[8][:, :], ALU.mult))
                link(vec.tensor_tensor(sm[5][:, :], sm[5][:, :], sm[7][:, :], ALU.add))
                link(vec.reciprocal(sm[5][:, :], sm[5][:, :]))
                link(vec.tensor_tensor(sm[5][:, :], sm[5][:, :], sm[5][:, :], ALU.mult))
                link(vec.scalar_tensor_tensor(sm[7][:, :], sm[5][:, :], 1e-6, v, ALU.mult, ALU.add))
                assert links[0] == at + ROW_OPS
            dve.wait_ge(mvA, GROUPS)
            norm_rows(0)
            dve.wait_ge(wB_in, 64)

            def front1_half(s, q):
                dve.wait_ge(adr_in, 16 * (s + 1))
                need(dve, u_done, s * G)
                need(dve, uT_mm, s - 1)
                need(dve, n2u_done, (s - 1) * G)
                for j in range(G):
                    T = s * G + j
                    nc.vector.scalar_tensor_tensor(U[q][:, j:j + 1, :], X[:, bass.ds(T, 1), :], mv[:, bass.ds(T, 1), 0], ADR[q][:, j:j + 1, D:2 * D], ALU.subtract, ALU.mult).then_inc(u_half, 1)

            def front1_rest(s, q):
                for j in range(G):
                    T = s * G + j
                    need(dve, u_half, T + 1)
                    nc.vector.scalar_tensor_tensor(U[q][:, j, :], U[q][:, j, :], row_r[:, bass.ds(T, 1)], ADR[q][:, j, 0:D], ALU.mult, ALU.add).then_inc(u_done, 1)

            def front1(s, q):
                front1_half(s, q)
                front1_rest(s, q)

            def front2(s, q):
                need(dve, su_rs, s + 1)
                nc.vector.tensor_scalar(su[q][:, :], n2u[q][:, :], CAP, 1.0, ALU.mult, ALU.min).then_inc(su_done, 1)
                need(dve, uT_hi, s + 1)
                nc.vector.tensor_tensor(UHL[q][1][:, :], bank[0][:, :], UHL[q][0][:, :], ALU.subtract).then_inc(uT_lo, 1)

            def qkv_out(T, s, q, j, from_=bank[0]):
                need(dve, su_done, s + 1)
                need(dve, qkv_mm, T + 1)
                nc.vector.scalar_tensor_tensor(QKV[q][:, j, :], from_[:, 0:3 * D], su[q][:, j:j + 1], b_qkv[:, :], ALU.mult, ALU.add).then_inc(qkv_done, 1)

            def head_sums(T, q, j):
                need(dve, sq_done, T + 1)
                nc.vector.tensor_reduce(ST[q][:, j * 48:(j + 1) * 48], SQ[j % 2][:, :].rearrange("p (a d) -> p a d", d=HD), AX.X, ALU.add).then_inc(hsum_done, 1)

            def projection_sums(s, q):
                need(dve, hsum_done, (s + 1) * G)
                nc.vector.tensor_reduce(ST[q][:, G * 48:G * 51], ST[q][:, 0:G * 48].rearrange("p (a h) -> p a h", h=HEADS), AX.X, ALU.add).then_inc(psum_done, 1)

            def factors(s, q):
                need(dve, st_rs, s + 1)
                nc.vector.tensor_scalar(FP[q][:, :], ST[q][:, G * 48:G * 51], CAP * HEAD_SCALE, HEAD_SCALE, ALU.mult, ALU.min).then_inc(fp_a, 1)
                need(dve, fp_a, s + 1)
                nc.vector.scalar_tensor_tensor(FC[q][:, :, :].rearrange("p g (a h) -> p (g a) h", h=HEADS), ST[q][:, 0:G * 48].rearrange("p (a h) -> p a h", h=HEADS), CAP,
                                               FP[q][:, :].unsqueeze(2).broadcast_to([TOK, G * 3, HEADS]), ALU.mult, ALU.min).then_inc(fac_b, 1)

            def scale_qk(T, s, q, j):
                need(dve, fac_b, s + 1)
                need(dve, hi_done, 2 * T - 2)
                need(dve, scaled, T)
                nc.vector.tensor_tensor(SC[j % 2][:, :].rearrange("p (h d) -> p h d", d=HD), QKV[q][:, j, 0:2 * D].rearrange("p (h d) -> p h d", d=HD),
                                        FC[q][:, j, 0:32].unsqueeze(2).broadcast_to([TOK, 32, HD]), ALU.mult).then_inc(scaled, 1)

            def low_parts(T, j):
                sc = SC[j % 2][:, :].rearrange("p (a h d) -> p a h d", a=2, d=HD)
                need(dve, hi_done, 2 * T + 2)
                nc.vector.tensor_tensor(QS[j % 2][:, :, 1, :], sc[:, 0, :, :], QS[j % 2][:, :, 0, :], ALU.subtract)
                nc.vector.tensor_tensor(KS[j % 2][:, :, 2, :], sc[:, 1, :, :], KS[j % 2][:, :, 0, :], ALU.subtract).then_inc(lo_done, 1)

            def normalise(T, j):
                need(dve, ot_mm, T + 1)
                heads = bank[1][:, :].rearrange("p (h e) -> p h e", e=32)
                nc.vector.reciprocal(RD[j % 2][:, :], heads[:, :, HD]).then_inc(rd_done, 1)
                need(dve, rd_done, T + 1)
                nc.vector.tensor_tensor(ON[j % 2][:, :].rearrange("p (h d) -> p h d", d=HD), heads[:, :, 0:HD],
                                        RD[j % 2][:, :].unsqueeze(2).broadcast_to([TOK, HEADS, HD]), ALU.mult).then_inc(on_done, 1)

            def ao_out(T, j):
                need(dve, wo_mm, T + 1)
                need(dve, ga_done, T + 1)
                nc.vector.tensor_tensor(AO[j % 2][:, :], bank[1][:, TOK:2 * TOK], b_o[:, :], ALU.add).then_inc(ao_done, 1)

            def row_sums(T, j):
                square = nc.vector.scalar_tensor_tensor
                need(dve, ao_done, T + 1)
                square(junkD[j % 2], AO[j % 2][:, :], 1.0, AO[j % 2][:, :], ALU.mult, ALU.mult, accum_out=n2a[:, bass.ds(T, 1)]).then_inc(n2a_done, 1)
                need(dve, ga_done, T + 3)
                branch = BR[:, bass.ds(T, 1), :]
                nc.vector.tensor_scalar(junkM[j % 2].unsqueeze(1), branch, 1.0, 0.0, ALU.mult, ALU.add, accum_out=sbr[:, bass.ds(T, 1)])
                square(junkX[j % 2].unsqueeze(1), branch, 1.0, X[:, bass.ds(T, 1), :], ALU.mult, ALU.mult,
                       accum_out=dxg[:, bass.ds(T, 1)]).then_inc(dx_done, 1)

            def slot(s, q, r):
                after, back, oldest = tile(s, q, r, 2), tile(s, q, r, -1), tile(s, q, r, -2)
                front = not (isinstance(s, int) and s >= GROUPS - 1)
                first = isinstance(s, int) and s == 0 and r < 2
                have = not (isinstance(s, int) and s in (0, GROUPS))
                F = (s + 1) * G
                if r == 0 and have:
                    factors(s, q)
                if after and not first:
                    scale_qk(*after)
                if oldest:
                    ao_out(oldest[0], oldest[3])
                if r == 3 and front:
                    head_sums(F, 1 - q, 0)
                if after and not first:
                    low_parts(after[0], after[3])
                if r > 1 and front:
                    qkv_out(F + 2 * r - 4, s + 1, 1 - q, 2 * r - 4)
                if back:
                    normalise(back[0], back[3])
                if front:
                    if r == 1:
                        front2(s + 1, 1 - q)
                    elif r > 1:
                        qkv_out(F + 2 * r - 3, s + 1, 1 - q, 2 * r - 3)
                if front and r == 3:
                    head_sums(F + 1, 1 - q, 1)
                if oldest:
                    row_sums(oldest[0], oldest[3])
                if r == 0 and front:
                    front1(s + 1, 1 - q)
                if front and r == 3:
                    for j in range(2, G):
                        head_sums(F + j, 1 - q, j)
                    projection_sums(s + 1, 1 - q)
            front1_half(0, 0)
            dve.wait_ge(rows_ready, 1)
            front1_rest(0, 0)
            dve.wait_ge(gram2_mm, 1)
            nc.vector.tensor_copy(bb_f1[:, :], bank[2][:, 0:1])
            nc.vector.tensor_copy(gram_hl[0][:, :], bank[1][:, 0:D + 1]).then_inc(gram2_done, 1)
            dve.wait_ge(gram2_done, 1)
            nc.vector.tensor_tensor(gram_hl[1][:, :], bank[1][:, 0:D + 1], gram_hl[0][:, :], ALU.subtract).then_inc(gram2_done, 2)
            nc.vector.memset(bank[3][:, :], 0.0).then_inc(bank3_clear, 1)
            front2(0, 0)
            for j in range(G):
                qkv_out(j, 0, 0, j, bank[(0, 5, 6, 7)[j]])
                if j > 0:
                    head_sums(j - 1, 0, j - 1)
            head_sums(G - 1, 0, G - 1)
            projection_sums(0, 0)
            factors(0, 0)
            for j in range(2):
                scale_qk(j, 0, 0, j)
            for j in range(2):
                low_parts(j, j)
            run_slots(dve, slot)
            ao_out(BATCH - 2, 2)
            normalise(BATCH - 1, 3)
            row_sums(BATCH - 2, 2)
            ao_out(BATCH - 1, 3)
            row_sums(BATCH - 1, 3)

            def mobius(k, acts):
                vec = nc.vector
                assert links[0] == mob_at[k]
                run(vec.tensor_scalar(sm[0][:, :], n2a[:, :], TINY, None, ALU.max))
                link(vec.tensor_scalar(sm[1][:, :], n2g[:, :], TINY, None, ALU.max))
                run(vec.tensor_scalar(sm[9][:, :], row_n2[:, :], -1.0, 1.0, ALU.mult, ALU.add))
                dve.wait_ge(chain_act, acts + 4)
                link(vec.tensor_scalar(sm[3][:, :], sm[3][:, :], CAP, 1.0, ALU.mult, ALU.min))
                link(vec.tensor_tensor(sm[6][:, :], sm[3][:, :], sm[5][:, :], ALU.mult))
                link(vec.tensor_scalar(sm[6][:, :], sm[6][:, :], 1e-7, None, ALU.max))
                assert links[0] == mob_at[k] + MOB_TANH
                link(vec.reciprocal(sm[8][:, :], sm[6][:, :]))
                dve.wait_ge(chain_act, acts + 5)
                link(vec.tensor_tensor(sm[7][:, :], sm[7][:, :], sm[8][:, :], ALU.mult))
                link(vec.tensor_tensor(sm[7][:, :], sm[7][:, :], sm[3][:, :], ALU.mult))
                run(vec.tensor_tensor(sm[4][:, :], sm[7][:, :], dxg[:, :], ALU.mult))
                link(vec.tensor_tensor(sm[5][:, :], sm[7][:, :], sm[7][:, :], ALU.mult))
                run(vec.tensor_scalar(sm[4][:, :], sm[4][:, :], 2.0, 1.0, ALU.mult, ALU.add))
                link(vec.tensor_tensor(sm[5][:, :], sm[5][:, :], n2g[:, :], ALU.mult))
                run(vec.tensor_tensor(al[:, :], sm[4][:, :], sm[5][:, :], ALU.add))
                link(vec.tensor_tensor(sm[5][:, :], sm[5][:, :], row_n2[:, :], ALU.mult))
                link(vec.tensor_tensor(sm[5][:, :], sm[5][:, :], sm[4][:, :], ALU.add))
                run(vec.tensor_tensor(be[:, :], sm[9][:, :], sm[7][:, :], ALU.mult))
                link(vec.tensor_scalar(sm[5][:, :], sm[5][:, :], 1e-7, None, ALU.max))
                link(vec.reciprocal(sm[5][:, :], sm[5][:, :]))
                run(vec.tensor_tensor(be[:, :], be[:, :], sm[5][:, :], ALU.mult))
                link(vec.tensor_tensor(al[:, :], al[:, :], sm[5][:, :], ALU.mult))
                mark(coef_ready)
                assert links[0] == mob_at[k] + MOB_OPS
            dve.wait_ge(n2g_done, BATCH)
            dve.wait_ge(n2a_done, BATCH)
            dve.wait_ge(dx_done, BATCH)
            mobius(0, 6)

            vec, mx, vx = nc.vector, mv[:, :, 0], mv[:, :, 1]
            mb, cov, vb, t = sm[0][:, :], sm[1][:, :], sm[2][:, :], sm[3][:, :]
            link(vec.tensor_scalar(mb, sbr[:, :], 1.0 / D, None, ALU.mult))
            run(vec.tensor_tensor(cov, mx, mb, ALU.mult))
            link(vec.tensor_tensor(vb, mb, mb, ALU.mult))
            run(vec.scalar_tensor_tensor(cov, dxg[:, :], 1.0 / D, cov, ALU.mult, ALU.subtract))
            run(vec.scalar_tensor_tensor(vb, n2g[:, :], 1.0 / D, vb, ALU.mult, ALU.subtract))
            run(vec.tensor_tensor(mx, mx, al[:, :], ALU.mult))
            link(vec.tensor_tensor(mb, mb, be[:, :], ALU.mult))
            run(vec.tensor_tensor(cov, cov, al[:, :], ALU.mult))
            run(vec.tensor_tensor(vb, vb, be[:, :], ALU.mult))
            run(vec.tensor_tensor(t, al[:, :], al[:, :], ALU.mult))
            link(vec.tensor_tensor(mx, mx, mb, ALU.add))
            run(vec.tensor_tensor(vx, vx, t, ALU.mult))
            link(vec.scalar_tensor_tensor(vb, cov, 2.0, vb, ALU.mult, ALU.add))
            link(vec.tensor_tensor(vb, vb, be[:, :], ALU.mult))
            link(vec.tensor_tensor(vx, vx, vb, ALU.add))
            link(vec.tensor_scalar(vx, vx, 0.0, None, ALU.max))
            assert links[0] == norm2_at, links
            norm_rows(11)

            def c_front_half(s, q):
                need(dve, x3_done, s + 1)
                dve.wait_ge(c_adr_in, 16 * (s + 1))
                need(dve, c_u_done, s * G)
                need(dve, c_n2u_done, (s - 1) * G)
                for j in range(G):
                    T = s * G + j
                    nc.vector.scalar_tensor_tensor(U[q][:, j:j + 1, :], X3[:, bass.ds(T, 1), :], mv[:, bass.ds(T, 1), 0], ADR[q][:, j:j + 1, D:2 * D], ALU.subtract, ALU.mult).then_inc(c_u_half, 1)

            def c_front_rest(s, q):
                for j in range(G):
                    T = s * G + j
                    need(dve, c_u_half, T + 1)
                    nc.vector.scalar_tensor_tensor(U[q][:, j, :], U[q][:, j, :], row_r[:, bass.ds(T, 1)], ADR[q][:, j, 0:D], ALU.mult, ALU.add).then_inc(c_u_done, 1)

            def c_front(s, q):
                c_front_half(s, q)
                c_front_rest(s, q)

            def c_scale(s, q):
                need(dve, c_su_rs, s + 1)
                nc.vector.tensor_scalar(su[q][:, :], n2u[q][:, :], CAP, 1.0, ALU.mult, ALU.min).then_inc(c_su_done, 1)
                need(dve, c_su_done, s + 1)
                need(dve, h_dot, (s - 1) * G)
                need(dve, cT_mm, s - 1)
                nc.vector.tensor_tensor(C[q][:, :, :], U[q][:, :, :], su[q][:, :].unsqueeze(2).broadcast_to([TOK, G, D]), ALU.mult).then_inc(c_done, 1)

            def c_low(s, q):
                need(dve, cT_hi, s + 1)
                nc.vector.tensor_tensor(UHL[q][1][:, :], bank[0][:, :], UHL[q][0][:, :], ALU.subtract).then_inc(cT_lo, 1)

            def h_norm(s, q):
                need(dve, gram_h_mm, s + 1)
                need(dve, h_dot, s * G)
                for j in range(G):
                    nc.vector.tensor_tensor_reduce(out=junkV[0][:, j, :], in0=bank[1 + j // 2][:, (j % 2) * (D + 1):(j % 2) * (D + 1) + D], in1=C[q][:, j, :],
                                                   scale=1.0, scalar=0.0, op0=ALU.mult, op1=ALU.add, accum_out=hq[q][:, j:j + 1]).then_inc(h_dot, 1)
                need(dve, h_dot, (s + 1) * G)
                for k in range(2):
                    last = nc.vector.scalar_tensor_tensor(hq[q][:, 2 * k:2 * k + 2], bank[1 + k][:, 0:2 * (D + 1)].rearrange("p (j n) -> p j n", n=D + 1)[:, :, D], 2.0,
                                                          hq[q][:, 2 * k:2 * k + 2], ALU.mult, ALU.add)
                last.then_inc(h_n2, 1)
                need(dve, h_n2, s + 1)
                nc.vector.tensor_scalar(hq[q][:, :], hq[q][:, :], bb_f1[:, 0:1], TINY, ALU.add, ALU.max).then_inc(h_n2_all, 1)

            def h_scale(s, q):
                need(dve, h_rs, s + 1)
                nc.vector.tensor_scalar(sh[q][:, :], hq[q][:, :], CAP, 1.0, ALU.mult, ALU.min).then_inc(h_scale_done, 1)

            def ff_out(s, q):
                need(dve, h_scale_done, s + 1)
                need(dve, f2_mm, s + 1)
                for j in range(G):
                    nc.vector.scalar_tensor_tensor(FO[q][:, j, :], bank[3][:, j * D:(j + 1) * D], sh[q][:, j:j + 1], b_f2[:, :], ALU.mult, ALU.add).then_inc(ff_done, 1)

            def c_dot(s, q):
                need(dve, c_ga_done, s + 1)
                need(dve, ff_done, (s + 1) * G)
                for j in range(G):
                    T = s * G + j
                    nc.vector.scalar_tensor_tensor(junkV[1][:, j:j + 1, :], BR[:, bass.ds(T, 1), :], 1.0, X3[:, bass.ds(T, 1), :], ALU.mult, ALU.mult,
                                                   accum_out=dxg[:, bass.ds(T, 1)]).then_inc(c_dx_done, 1)

            def step_c(s, q):
                last = isinstance(s, int) and s == GROUPS - 1
                first = isinstance(s, int) and s == 0
                if not last:
                    c_front(s + 1, 1 - q)
                if not first:
                    ff_out(s - 1, 1 - q)
                if not last:
                    c_scale(s + 1, 1 - q)
                h_norm(s, q)
                h_scale(s, q)
                if not last:
                    c_low(s + 1, 1 - q)
                if not first:
                    c_dot(s - 1, 1 - q)
            c_front_half(0, 0)
            dve.wait_ge(rows_ready, 2)
            c_front_rest(0, 0)
            c_scale(0, 0)
            c_low(0, 0)
            run_steps(dve, step_c)
            ff_out(GROUPS - 1, 1)
            c_dot(GROUPS - 1, 1)
            dve.wait_ge(c_dx_done, BATCH)
            dve.wait_ge(c_n2a_done, BATCH)
            dve.wait_ge(c_n2g_done, BATCH)
            mobius(1, 17)
            dve.wait_ge(cT_mm, GROUPS)
            fused = nc.vector.scalar_tensor_tensor
            for T in range(G):
                last = fused(X4[0][:, T, :], X3[:, T, :], al[:, T:T + 1], X[:, T, :], ALU.mult, ALU.add)
            last.then_inc(x4_first, 1)
            dve.wait_ge(x4_first, 1)
            for T in range(G):
                last = fused(X4[0][:, T, :], BR[:, T, :], be[:, T:T + 1], X4[0][:, T, :], ALU.mult, ALU.add)
            last.then_inc(x4_done, 1)

            def d_low(s, q):
                need(dve, x4_hi, s + 1)
                nc.vector.tensor_tensor(UHL[q][1][:, :], bank[0][:, :], UHL[q][0][:, :], ALU.subtract).then_inc(x4_lo, 1)

            def logits(s, q):
                need(dve, rl_mm, s + 1)
                need(dve, dt_in, 16 * (s + 1))
                nc.vector.tensor_tensor(sg[q][:, :, :], bank[0][:, 0:G * EXPERTS].rearrange("p (g e) -> p g e", e=EXPERTS), ADT[q][:, :, :], ALU.add).then_inc(rl_done, 1)

            def route(s, q):
                vec = nc.vector
                need(dve, sig_done, s + 1)
                ops = [0]

                def runs(instruction):
                    ops[0] += 1
                    instruction.then_inc(rchain, 1)

                def rlink(instruction):
                    runs(instruction)
                    dve.wait_ge(rchain, ROUTE_OPS * s + ops[0])
                sel = rt[0][:, :, :]
                rlink(vec.tensor_tensor(sel, sg[q][:, :, :], b_router[:, :].unsqueeze(1).broadcast_to([TOK, G, EXPERTS]), ALU.add))
                full = [TOK, G, EXPERTS, EXPERTS]
                mine, other = sel.unsqueeze(3).broadcast_to(full), sel.unsqueeze(2).broadcast_to(full)
                for g in range(G):
                    last = vec.tensor_tensor(cmpb[0][:, g, :, :], other[:, g], mine[:, g], ALU.is_gt)
                runs(last)
                for g in range(G):
                    last = vec.tensor_tensor(cmpb[1][:, g, :, :], other[:, g], mine[:, g], ALU.is_equal)
                rlink(last)
                rlink(vec.tensor_tensor(cmpb[1][:, :, :, :], cmpb[1][:, :, :, :], earlier[:, :, :].unsqueeze(1).broadcast_to(full), ALU.mult))
                rlink(vec.tensor_tensor(cmpb[0][:, :, :, :].rearrange("p g a b -> p (g a b)"), cmpb[0][:, :, :, :].rearrange("p g a b -> p (g a b)"),
                                        cmpb[1][:, :, :, :].rearrange("p g a b -> p (g a b)"), ALU.add))
                rlink(vec.tensor_reduce(rt[1][:, :, :].rearrange("p g e -> p (g e)"), cmpb[0][:, :, :, :].rearrange("p g a b -> p (g a) b"), AX.X, ALU.add))
                rlink(vec.tensor_scalar(rt[1][:, :, :], rt[1][:, :, :], float(TOP_K), None, ALU.is_lt))
                rlink(vec.tensor_tensor(rt[2][:, :, :], rt[1][:, :, :], sg[q][:, :, :], ALU.mult))
                rlink(vec.tensor_reduce(rs[0][:, :], rt[2][:, :, :], AX.X, ALU.add))
                runs(vec.tensor_scalar(rs[1][:, :], rs[0][:, :], 1e-9, None, ALU.is_gt))
                rlink(vec.tensor_scalar(rs[0][:, :], rs[0][:, :], 1e-9, None, ALU.add))
                runs(vec.tensor_scalar(rs[2][:, :], rs[1][:, :], -1.0 / (TOP_K * (2 + TOP_K)), 1.0 / (TOP_K * (2 + TOP_K)), ALU.mult, ALU.add))
                rlink(vec.reciprocal(rs[0][:, :], rs[0][:, :]))
                runs(vec.scalar_tensor_tensor(rs[0][:, :], rs[0][:, :], 1.0 / (2 + TOP_K), rs[1][:, :], ALU.mult, ALU.mult))
                rlink(vec.tensor_tensor(rt[1][:, :, :], rt[1][:, :, :], rs[2][:, :].unsqueeze(2).broadcast_to([TOK, G, EXPERTS]), ALU.mult))
                rlink(vec.tensor_tensor(rt[2][:, :, :], rt[2][:, :, :], rs[0][:, :].unsqueeze(2).broadcast_to([TOK, G, EXPERTS]), ALU.mult))
                assert ops[0] == ROUTE_OPS, ops
                vec.tensor_tensor(gates[q][:, :, :], rt[1][:, :, :], rt[2][:, :, :], ALU.add).then_inc(gates_done, 1)

            def gate_shared(s, q, k):
                need(dve, silu_done, 4 * s + k + 1)
                need(dve, up_mm, 16 * s + 2 * k + 2)
                if k == 0:
                    need(dve, sd_mm, s * G - 3)
                nc.vector.tensor_tensor(HS[q][:, k, :], bank[4 + (2 * k + 1) % 4], S1[k % 2][:, :], ALU.mult).then_inc(hs_mul, 1)

            def combine(s, q, j, banks=(2, 3, 1)):
                T = s * G + j
                stt = nc.vector.scalar_tensor_tensor
                low, high = OUT[q][:, j, :], AO[j % 2][:, :]
                low1 = OUT[q][:, j:j + 1, :]
                gate = lambda e: gates[q][:, j, e:e + 1]
                part = lambda e: bank[banks[2 if e >= 4 else 1]][:, (e % 4) * D:(e % 4 + 1) * D]
                at = 6 * T
                need(dve, sd_mm, T + 1)
                stt(low1, bank[banks[0]][:, 0:D].unsqueeze(1), 1.0 / (2 * (2 + TOP_K)), X[:, bass.ds(T, 1), :], ALU.mult, ALU.add).then_inc(bank2_free, 1)
                need(dve, rd_mm, T + 1)
                need(dve, gates_done, s + 1)
                nc.vector.tensor_scalar(high, part(4), gate(4), None, ALU.mult).then_inc(acc_done, 1)
                dve.wait_ge(bank2_free, T + 2)
                stt(low, part(0), gate(0), low, ALU.mult, ALU.add).then_inc(acc_done, 1)
                dve.wait_ge(acc_done, at + 1)
                stt(high, part(5), gate(5), high, ALU.mult, ALU.add).then_inc(acc_done, 1)
                dve.wait_ge(acc_done, at + 2)
                stt(low, part(1), gate(1), low, ALU.mult, ALU.add).then_inc(acc_done, 1)
                dve.wait_ge(acc_done, at + 3)
                stt(high, part(6), gate(6), high, ALU.mult, ALU.add).then_inc(acc_done, 1)
                dve.wait_ge(acc_done, at + 4)
                stt(low, part(2), gate(2), low, ALU.mult, ALU.add).then_inc(acc_done, 1)
                dve.wait_ge(acc_done, at + 5)
                stt(high, part(7), gate(7), high, ALU.mult, ALU.add).then_inc(bank1_free, 1)
                dve.wait_ge(acc_done, at + 6)
                stt(low, part(3), gate(3), low, ALU.mult, ALU.add).then_inc(bank3_free, 1)
                dve.wait_ge(bank1_free, T + 2)
                dve.wait_ge(bank3_free, T + 2)
                nc.vector.tensor_tensor(low, low, high, ALU.add).then_inc(out_done, 1)

            def step_d(s, q):
                first = isinstance(s, int) and s == 0
                last = isinstance(s, int) and s == GROUPS - 1
                for j in range(G):
                    if j < 2:
                        gate_shared(s, q, 2 * j)
                        gate_shared(s, q, 2 * j + 1)
                    if j == 3 and not last:
                        logits(s + 1, 1 - q)
                    if not first:
                        if j == 0:
                            dve.wait_ge(out_stored[1 - q], 16 * pair[0] + 16)
                        combine(s - 1, 1 - q, j)
                    if j == 1 and not last:
                        d_low(s + 1, 1 - q)
                    if j == 2:
                        route(s, q)
            for semaphore in (bank1_free, bank2_free, bank3_free):
                mark(semaphore)
            for q in range(2):
                mark(out_stored[q], 16)
            dve.wait_ge(wD_in, 48)
            d_low(0, 0)
            logits(0, 0)
            run_steps(dve, step_d)
            dve.wait_ge(out_stored[1], 16 * PAIRS)
            for j in range(G):
                combine(GROUPS - 1, 1, j, last_banks[j % 2])


def host_layout(inputs):
    import numpy as np
    t = lambda a: np.ascontiguousarray(a)
    f = np.asarray(inputs["fside_Bx1x1024x16_0"])[:, 0]
    return {
        "x": t(inputs["x"]),
        "condT": t(np.asarray(inputs["cond_1024"]).T),
        "score_w": t(inputs["L0_cond_score_w"]),
        "score_b": t(inputs["L0_cond_score_b"]),
        "w1T": t(np.asarray(inputs["L1_cond_W"]).T),
        "fc_bias": t(inputs["L1_cond_fc_bias"]),
        "fT": t(f.transpose(2, 0, 1)),
        "w_ada": t(inputs["L2_cond_w_ada"]),
        "b_ada": t(inputs["L2_cond_b_ada"]),
        "w_qkv": t(np.concatenate([np.asarray(inputs["L2_cond_w_" + n]) for n in "qkv"], axis=1)),
        "b_qkv": t(np.concatenate([np.asarray(inputs["L2_cond_b_" + n]) for n in "qkv"])),
        "w_o": t(inputs["L2_cond_w_o"]),
        "b_o": t(inputs["L2_cond_b_o"]),
        "w_f1": t(inputs["L2_cond_w_f1"]),
        "w_f1Tb": t(np.concatenate([np.asarray(inputs["L2_cond_w_f1"]).T.reshape(4, 128, D), np.asarray(inputs["L2_cond_b_f1"]).reshape(4, 128, 1)],
                                   axis=2).transpose(1, 0, 2)),
        "w_f2": t(inputs["L2_cond_w_f2"]),
        "b_f2": t(inputs["L2_cond_b_f2"]),
        "w_up": t(np.concatenate([np.asarray(inputs[n]).reshape(-1, D).T for n in ("L3_cond_s_w1", "L3_cond_s_w3", "L3_cond_r_w1")], axis=1)),
        "w_sd": t(np.asarray(inputs["L3_cond_s_w2"]).transpose(0, 2, 1).reshape(FF, D)),
        "w_rd": t(np.asarray(inputs["L3_cond_r_w2"]).transpose(0, 2, 1).reshape(EXPERTS * 128, D)),
        "b_router": t(inputs["L3_cond_router_bias"]),
        "w_routerT": t(np.asarray(inputs["L3_cond_W_router"]).T),
    }


def kernel(**inputs):
    import concourse.bacc as bacc
    from concourse.bass_utils import run_bass_kernel_spmd

    nc = bacc.Bacc("TRN2", target_bir_lowering=False, num_devices=1)
    arrays = host_layout(inputs)
    ins = {n: nc.dram_tensor(n, a.shape, mybir.dt.from_np(a.dtype), kind="ExternalInput").ap() for n, a in arrays.items()}
    out = nc.dram_tensor("out", (BATCH, TOK, D), FP32, kind="ExternalOutput").ap()
    build(nc, ins, out)
    return run_bass_kernel_spmd(nc, [arrays], core_ids=[0]).results[0]["out"]
```
